# Optimizing a Trainium2 kernel written in Bass

```python
import numpy as np
import jax
import jax.numpy as jnp

def _softmax(x, axis=-1):
    return jax.nn.softmax(x, axis=axis)

def _gelu(x):
    return jax.nn.gelu(x, approximate=True)

def _silu(x):
    return jax.nn.silu(x)

def _sigmoid(x):
    return jax.nn.sigmoid(x)

def _layernorm(x, axis=-1, eps=1e-05):
    m = jnp.mean(x, axis=axis, keepdims=True)
    v = jnp.var(x, axis=axis, keepdims=True)
    return (x - m) / jnp.sqrt(v + eps)

def _scatter_add(tgt, idx, src, axis=0):
    return tgt.at[idx].add(src)

def _segment_sum(src, seg, n):
    return jax.ops.segment_sum(src, seg, n)
kernel_name = 'mk_decoder_postln_d2_seqx_r8_9ce74a'

def setup_inputs(seed: int=0):
    np.random.seed(seed)
    _w = jnp.asarray

    def _rec_inputs():
        import jax
        import jax.numpy as jnp
        _rk = jax.random.key(seed)
        x = -0.0003929 + 0.9999 * jax.random.normal(jax.random.fold_in(_rk, 1), (128, 64, 128), jnp.float32)
        _lenS = 64 - jax.random.randint(jax.random.fold_in(_rk, 7), (128,), 0, max(1, 64 // 4) + 1, jnp.int32)
        _lenS2 = 64 - jax.random.randint(jax.random.fold_in(_rk, 8), (128,), 0, max(1, 64 // 4) + 1, jnp.int32)
        _ctx_1024P = jax.random.normal(jax.random.fold_in(_rk, 11), (128, 16, 128), jnp.float32)
        _ctx_1024c = jax.random.dirichlet(jax.random.fold_in(_rk, 511), 0.3 * jnp.ones((16,), jnp.float32), (128, 64))
        _ctx_1024t = jnp.einsum('bsk,bkd->bsd', _ctx_1024c, _ctx_1024P)
        _ctx_1024t = _ctx_1024t * jax.lax.rsqrt(jnp.mean(jnp.square(_ctx_1024t)) + 1e-12) * 0.953939
        ctx_1024 = 2.81802e-05 + 1.00001 * (_ctx_1024t + 0.3 * jax.random.normal(jax.random.fold_in(_rk, 611), (128, 64, 128), jnp.float32))
        itok_SxS2_0_2016 = jax.random.randint(jax.random.fold_in(_rk, 12), (64, 64), 0, 2017, jnp.int32)
        fside_BxSxS2_0 = -4.48278e-06 + 1.00019 * jax.random.normal(jax.random.fold_in(_rk, 13), (128, 64, 64), jnp.float32)
        _validS = jnp.arange(64)[None, :] < _lenS[:, None]
        _validS2 = jnp.arange(64)[None, :] < _lenS2[:, None]
        _causal = jnp.tril(jnp.ones((64, 64), dtype=bool))
        mask_BxSxS2_ff0 = jnp.where(jnp.ones((128, 64, 64), dtype=bool), 0.0, -1000000000.0).astype(jnp.float32)
        return (x, ctx_1024, itok_SxS2_0_2016, fside_BxSxS2_0, mask_BxSxS2_ff0)
    x, ctx_1024, itok_SxS2_0_2016, fside_BxSxS2_0, mask_BxSxS2_ff0 = _rec_inputs()

    def _L0_attn_setup():
        import jax, jax.numpy as jnp
        import numpy as np
        import math
        D_MODEL = 128
        NUM_HEADS = 16
        HEAD_DIM = D_MODEL // NUM_HEADS
        B, S = (2, 256)

        def _causal_attn(q, k, v):
            scale = 1.0 / math.sqrt(q.shape[-1])
            scores = jnp.einsum('bthd,bshd->bhts', q, k) * scale
            t = q.shape[1]
            mask = jnp.tril(jnp.ones((t, t), dtype=bool))
            scores = jnp.where(mask, scores, -jnp.inf)
            attn = jax.nn.softmax(scores, axis=-1)
            return jnp.einsum('bhts,bshd->bthd', attn, v)
        key = jax.random.key(seed)
        ks = jax.random.split(key, 7)
        sc = 0.02
        return {'x': jax.random.normal(ks[0], (B, S, D_MODEL), dtype=jnp.float32), 'Wqkv_w': jax.random.normal(ks[1], (3 * D_MODEL, D_MODEL), dtype=jnp.float32) * sc, 'Wqkv_b': jnp.zeros((3 * D_MODEL,), dtype=jnp.float32), 'conv_w': jax.random.normal(ks[2], (D_MODEL, D_MODEL, 3), dtype=jnp.float32) * sc, 'conv_b': jnp.zeros((D_MODEL,), dtype=jnp.float32), 'out_w': jax.random.normal(ks[3], (D_MODEL, D_MODEL), dtype=jnp.float32) * sc, 'out_b': jnp.zeros((D_MODEL,), dtype=jnp.float32)}
    _L0_attn_all = _L0_attn_setup()
    _L0_attn_in = {k: v for k, v in _L0_attn_all.items() if k in ('Wqkv_w', 'Wqkv_b', 'conv_w', 'conv_b', 'out_w', 'out_b')}
    del _L0_attn_all

    def _L0_xattn_setup():
        import jax, jax.numpy as jnp
        import numpy as np
        B, S, DIM, NH = (32, 64, 128, 8)
        DH = DIM // NH
        EPS = 1e-06
        LN_EPS = 1e-05

        def _make_hops(n):
            hops = np.zeros((n, n), dtype=np.int64)
            cur = 1
            for i in range(n):
                for j in range(i + 1, n):
                    hops[i, j] = cur
                    hops[j, i] = cur
                    cur += 1
            return (hops, cur)

        def _mlstm_forward(q, k, v, igate_w, igate_b, fgate_w, fgate_b, rpe, ln_w, ln_b, hops):
            Bq, Sq, _ = q.shape
            pos_emb = rpe[hops]
            gate_in = jnp.concatenate([q, k, v], axis=-1)
            ig = gate_in @ igate_w.T + igate_b
            fg = gate_in @ fgate_w.T + fgate_b
            ig = jnp.transpose(ig, (0, 2, 1))
            fg = jnp.transpose(fg, (0, 2, 1))
            qh = q.reshape(Bq, Sq, NH, DH).transpose(0, 2, 1, 3)
            kh = k.reshape(Bq, Sq, NH, DH).transpose(0, 2, 1, 3)
            vh = v.reshape(Bq, Sq, NH, DH).transpose(0, 2, 1, 3)
            log_f = jax.nn.log_sigmoid(fg)
            csum = jnp.cumsum(log_f, axis=-1)
            csum = jnp.concatenate([jnp.zeros((Bq, NH, 1), csum.dtype), csum], axis=-1)
            lfm = csum[:, :, :, None] - csum[:, :, None, :]
            ltr = jnp.tril(jnp.ones((Sq, Sq), dtype=bool))
            log_fg_matrix = jnp.where(ltr, lfm[:, :, 1:, 1:], -jnp.inf)
            log_D = log_fg_matrix + ig[:, :, None, :]
            max_log_D = jnp.max(log_D, axis=-1, keepdims=True)
            D = jnp.exp(log_D - max_log_D)
            k_scaled = kh / np.sqrt(DH).astype(np.float32)
            pe = pos_emb.reshape(Sq, Sq, NH, DH)
            k_hop = jnp.einsum('bhvc,vmhc->bhvm', qh, pe)
            qk = jnp.einsum('bhsd,bhtd->bhst', qh, k_scaled)
            C = (qk + k_hop) * D
            normalizer = jnp.maximum(jnp.abs(jnp.sum(C, axis=-1, keepdims=True)), jnp.exp(-max_log_D))
            Cn = C / (normalizer + EPS)
            h = Cn @ vh
            mu = jnp.mean(h, axis=-1, keepdims=True)
            var = jnp.mean(jnp.square(h - mu), axis=-1, keepdims=True)
            hn = (h - mu) / jnp.sqrt(var + LN_EPS)
            w = (1.0 + ln_w).reshape(NH, DH)
            b = ln_b.reshape(NH, DH)
            hn = hn * w[None, :, None, :] + b[None, :, None, :]
            return hn.transpose(0, 2, 1, 3).reshape(Bq, Sq, DIM)
        key = jax.random.key(seed)
        ks = jax.random.split(key, 8)
        hops_np, curnum = _make_hops(S)
        return {'q': jax.random.normal(ks[0], (B, S, DIM), dtype=jnp.float32), 'k': jax.random.normal(ks[1], (B, S, DIM), dtype=jnp.float32), 'v': jax.random.normal(ks[2], (B, S, DIM), dtype=jnp.float32), 'igate_w': jax.random.normal(ks[3], (NH, 3 * DIM), dtype=jnp.float32) * 0.02, 'igate_b': jax.random.normal(ks[4], (NH,), dtype=jnp.float32) * 0.1, 'fgate_w': jax.random.normal(ks[5], (NH, 3 * DIM), dtype=jnp.float32) * 0.02, 'fgate_b': jnp.linspace(3.0, 6.0, NH, dtype=jnp.float32), 'rpe': jax.random.normal(ks[6], (curnum, DIM), dtype=jnp.float32) * 0.02, 'ln_w': jax.random.normal(ks[7], (DIM,), dtype=jnp.float32) * 0.1, 'ln_b': jnp.zeros((DIM,), dtype=jnp.float32), 'hops': jnp.asarray(hops_np)}
    _L0_xattn_all = _L0_xattn_setup()
    _L0_xattn_in = {k: v for k, v in _L0_xattn_all.items() if k in ('igate_w', 'igate_b', 'fgate_w', 'fgate_b', 'rpe', 'ln_w', 'ln_b')}
    del _L0_xattn_all

    def _L0_ffn_setup():
        import jax, jax.numpy as jnp
        import numpy as np
        import math
        B, T, D, H, E, TOPK, CAPF = (4, 256, 128, 16, 8, 2, 2.0)
        HD = D // H

        def layernorm(x, g, b, eps=1e-05):
            m = jnp.mean(x, -1, keepdims=True)
            v = jnp.mean(jnp.square(x - m), -1, keepdims=True)
            return (x - m) * jax.lax.rsqrt(v + eps) * g + b

        def block_forward(x, ln1_g, ln1_b, Wqkv, Wproj, ln2_g, ln2_b, Wgate, W1, b1, W2, b2):
            Bb, Tt, d = x.shape
            hd = HD
            half = hd // 2
            h = layernorm(x, ln1_g, ln1_b)
            qkv = (h @ Wqkv).reshape(Bb, Tt, H, 3 * hd)
            q, k, v = (qkv[..., :hd], qkv[..., hd:2 * hd], qkv[..., 2 * hd:])
            inv_freq = 1.0 / 10000.0 ** (jnp.arange(0, hd, 2, dtype=jnp.float32) / hd)
            ang = jnp.arange(Tt, dtype=jnp.float32)[:, None] * inv_freq
            sin = jnp.sin(ang)[None, :, None, :].astype(x.dtype)
            cos = jnp.cos(ang)[None, :, None, :].astype(x.dtype)

            def rope(t):
                t1, t2 = (t[..., :half], t[..., half:])
                return jnp.concatenate([t1 * cos - t2 * sin, t1 * sin + t2 * cos], -1)
            q, k = (rope(q), rope(k))
            scores = jnp.einsum('bqhd,bkhd->bhqk', q, k) / math.sqrt(hd)
            causal = jnp.tril(jnp.ones((Tt, Tt), dtype=bool))
            scores = jnp.where(causal, scores, jnp.asarray(-1000000000.0, scores.dtype))
            probs = jax.nn.softmax(scores, axis=-1)
            attn = jnp.einsum('bhqk,bkhd->bqhd', probs, v).reshape(Bb, Tt, d) @ Wproj
            x = x + attn
            h2 = layernorm(x, ln2_g, ln2_b)
            flat = h2.reshape(-1, d)
            N = flat.shape[0]
            capacity = int(math.ceil(CAPF * N / E))
            gates = jax.nn.softmax((flat @ Wgate).astype(jnp.float32), -1).astype(flat.dtype)
            _, top_inds = jax.lax.top_k(gates, TOPK)
            mask = jnp.zeros((N, E), dtype=bool).at[jnp.arange(N)[:, None], top_inds].set(True)
            pos = jnp.cumsum(mask.astype(jnp.int32), axis=0) * mask - 1
            keep = (pos < capacity) & mask
            t_flat = jnp.repeat(jnp.arange(N), TOPK)
            e_flat = top_inds.reshape(-1)
            p = pos[t_flat, e_flat]
            kp = keep[t_flat, e_flat]
            p_eff = jnp.where(kp, p, capacity)
            exp_in = jnp.zeros((E, capacity, d), flat.dtype).at[e_flat, p_eff].set(flat[t_flat], mode='drop')
            hmid = jax.nn.gelu(jnp.einsum('ecd,edf->ecf', exp_in, W1) + b1[:, None, :], approximate=False)
            exp_out = jnp.einsum('ecf,efd->ecd', hmid, W2) + b2[:, None, :]
            gate = gates[t_flat, e_flat] * kp.astype(flat.dtype)
            p_g = jnp.minimum(p_eff, capacity - 1)
            moe = jnp.zeros((N, d), flat.dtype).at[t_flat].add(exp_out[e_flat, p_g] * gate[:, None])
            return x + moe.reshape(Bb, Tt, d)
        key = jax.random.key(seed)
        ks = jax.random.split(key, 8)
        s = 0.02
        return {'x': jax.random.normal(ks[0], (B, T, D), jnp.float32), 'ln1_g': jnp.ones((D,), jnp.float32), 'ln1_b': jnp.zeros((D,), jnp.float32), 'Wqkv': jax.random.normal(ks[1], (D, 3 * D), jnp.float32) * s, 'Wproj': jax.random.normal(ks[2], (D, D), jnp.float32) * s, 'ln2_g': jnp.ones((D,), jnp.float32), 'ln2_b': jnp.zeros((D,), jnp.float32), 'Wgate': jax.random.normal(ks[3], (D, E), jnp.float32) * s, 'W1': jax.random.normal(ks[4], (E, D, 4 * D), jnp.float32) * s, 'b1': jnp.zeros((E, 4 * D), jnp.float32), 'W2': jax.random.normal(ks[5], (E, 4 * D, D), jnp.float32) * s, 'b2': jnp.zeros((E, D), jnp.float32)}
    _L0_ffn_all = _L0_ffn_setup()
    _L0_ffn_in = {k: v for k, v in _L0_ffn_all.items() if k in ('ln1_g', 'ln1_b', 'Wqkv', 'Wproj', 'ln2_g', 'ln2_b', 'Wgate', 'W1', 'b1', 'W2', 'b2')}
    del _L0_ffn_all

    def _L1_attn_setup():
        import jax, jax.numpy as jnp
        import numpy as np
        B, S, D = (2, 256, 128)
        N_HEADS, N_KV_HEADS = (16, 4)
        HEAD_DIM = D // N_HEADS
        KV_GROUPS = N_HEADS // N_KV_HEADS
        ROPE_BASE = 10000.0

        def _apply_rope(t, cos, sin):
            t1, t2 = jnp.split(t, 2, axis=-1)
            return jnp.concatenate([t1 * cos - t2 * sin, t1 * sin + t2 * cos], axis=-1)
        key = jax.random.key(seed)
        ks = jax.random.split(key, 5)
        s = 0.02
        return {'x': jax.random.normal(ks[0], (B, S, D), dtype=jnp.float32), 'wq': jax.random.normal(ks[1], (D, D), dtype=jnp.float32) * s, 'wk': jax.random.normal(ks[2], (D, N_KV_HEADS * HEAD_DIM), dtype=jnp.float32) * s, 'wv': jax.random.normal(ks[3], (D, N_KV_HEADS * HEAD_DIM), dtype=jnp.float32) * s, 'wo': jax.random.normal(ks[4], (D, D), dtype=jnp.float32) * s}
    _L1_attn_all = _L1_attn_setup()
    _L1_attn_in = {k: v for k, v in _L1_attn_all.items() if k in ('wq', 'wk', 'wv', 'wo')}
    del _L1_attn_all

    def _L1_xattn_setup():
        import jax, jax.numpy as jnp
        import numpy as np
        HIDDEN = 128
        HEADS = 16
        DK = HIDDEN // HEADS
        B, N = (2, 256)
        key = jax.random.key(seed)
        ks = jax.random.split(key, 12)
        s = 0.02
        return {'q': jax.random.normal(ks[0], (B, N, HIDDEN), jnp.float32), 'k': jax.random.normal(ks[1], (B, N, HIDDEN), jnp.float32), 'v': jax.random.normal(ks[2], (B, N, HIDDEN), jnp.float32), 'attn_bias': jax.random.normal(ks[3], (B, N, N), jnp.float32), 'attention_mask': jnp.zeros((B, N, N), jnp.float32), 'Wq': jax.random.normal(ks[4], (HIDDEN, HIDDEN), jnp.float32) * s, 'bq': jnp.zeros((HIDDEN,), jnp.float32), 'Wk': jax.random.normal(ks[5], (HIDDEN, HIDDEN), jnp.float32) * s, 'bk': jnp.zeros((HIDDEN,), jnp.float32), 'Wv': jax.random.normal(ks[6], (HIDDEN, HIDDEN), jnp.float32) * s, 'bv': jnp.zeros((HIDDEN,), jnp.float32), 'Wo': jax.random.normal(ks[7], (HIDDEN, HIDDEN), jnp.float32) * s, 'bo': jnp.zeros((HIDDEN,), jnp.float32)}
    _L1_xattn_all = _L1_xattn_setup()
    _L1_xattn_in = {k: v for k, v in _L1_xattn_all.items() if k in ('Wq', 'bq', 'Wk', 'bk', 'Wv', 'bv', 'Wo', 'bo')}
    del _L1_xattn_all

    def _L1_ffn_setup():
        import jax, jax.numpy as jnp
        import numpy as np
        IN_DIM = 128
        HIDDEN = 128
        OUT_DIM = 128
        NUM_EXPERTS = 16
        TOP_K = 2
        ROUTER_TEMP = 1.0
        LN_EPS = 1e-05

        def _layernorm(h, g, b):
            mu = jnp.mean(h, axis=-1, keepdims=True)
            var = jnp.mean(jnp.square(h - mu), axis=-1, keepdims=True)
            return (h - mu) * jax.lax.rsqrt(var + LN_EPS) * g + b
        key = jax.random.key(seed)
        ks = jax.random.split(key, 8)
        s_in = 1.0 / np.sqrt(IN_DIM)
        s_h = 1.0 / np.sqrt(HIDDEN)
        x = jax.random.normal(ks[0], (4, 256, IN_DIM), dtype=jnp.float32)
        Wr = jax.random.uniform(ks[1], (IN_DIM, NUM_EXPERTS), jnp.float32, -s_in, s_in)
        br = jax.random.uniform(ks[2], (NUM_EXPERTS,), jnp.float32, -s_in, s_in)
        W1 = jax.random.uniform(ks[3], (NUM_EXPERTS, IN_DIM, HIDDEN), jnp.float32, -s_in, s_in)
        b1 = jax.random.uniform(ks[4], (NUM_EXPERTS, HIDDEN), jnp.float32, -s_in, s_in)
        g1 = jnp.ones((NUM_EXPERTS, HIDDEN), jnp.float32)
        be1 = jnp.zeros((NUM_EXPERTS, HIDDEN), jnp.float32)
        W2 = jax.random.uniform(ks[5], (NUM_EXPERTS, HIDDEN, OUT_DIM), jnp.float32, -s_h, s_h)
        b2 = jax.random.uniform(ks[6], (NUM_EXPERTS, OUT_DIM), jnp.float32, -s_h, s_h)
        return {'x': x, 'Wr': Wr, 'br': br, 'W1': W1, 'b1': b1, 'g1': g1, 'be1': be1, 'W2': W2, 'b2': b2}
    _L1_ffn_all = _L1_ffn_setup()
    _L1_ffn_in = {k: v for k, v in _L1_ffn_all.items() if k in ('Wr', 'br', 'W1', 'b1', 'g1', 'be1', 'W2', 'b2')}
    del _L1_ffn_all
    return {'x': x, 'ctx_1024': ctx_1024, 'itok_SxS2_0_2016': itok_SxS2_0_2016, 'fside_BxSxS2_0': fside_BxSxS2_0, 'mask_BxSxS2_ff0': mask_BxSxS2_ff0, 'L0_attn_Wqkv_w': _L0_attn_in['Wqkv_w'], 'L0_attn_Wqkv_b': _L0_attn_in['Wqkv_b'], 'L0_attn_conv_w': _L0_attn_in['conv_w'], 'L0_attn_conv_b': _L0_attn_in['conv_b'], 'L0_attn_out_w': _L0_attn_in['out_w'], 'L0_attn_out_b': _L0_attn_in['out_b'], 'L0_xattn_igate_w': _L0_xattn_in['igate_w'], 'L0_xattn_igate_b': _L0_xattn_in['igate_b'], 'L0_xattn_fgate_w': _L0_xattn_in['fgate_w'], 'L0_xattn_fgate_b': _L0_xattn_in['fgate_b'], 'L0_xattn_rpe': _L0_xattn_in['rpe'], 'L0_xattn_ln_w': _L0_xattn_in['ln_w'], 'L0_xattn_ln_b': _L0_xattn_in['ln_b'], 'L0_ffn_ln1_g': _L0_ffn_in['ln1_g'], 'L0_ffn_ln1_b': _L0_ffn_in['ln1_b'], 'L0_ffn_Wqkv': _L0_ffn_in['Wqkv'], 'L0_ffn_Wproj': _L0_ffn_in['Wproj'], 'L0_ffn_ln2_g': _L0_ffn_in['ln2_g'], 'L0_ffn_ln2_b': _L0_ffn_in['ln2_b'], 'L0_ffn_Wgate': _L0_ffn_in['Wgate'], 'L0_ffn_W1': _L0_ffn_in['W1'], 'L0_ffn_b1': _L0_ffn_in['b1'], 'L0_ffn_W2': _L0_ffn_in['W2'], 'L0_ffn_b2': _L0_ffn_in['b2'], 'L1_attn_wq': _L1_attn_in['wq'], 'L1_attn_wk': _L1_attn_in['wk'], 'L1_attn_wv': _L1_attn_in['wv'], 'L1_attn_wo': _L1_attn_in['wo'], 'L1_xattn_Wq': _L1_xattn_in['Wq'], 'L1_xattn_bq': _L1_xattn_in['bq'], 'L1_xattn_Wk': _L1_xattn_in['Wk'], 'L1_xattn_bk': _L1_xattn_in['bk'], 'L1_xattn_Wv': _L1_xattn_in['Wv'], 'L1_xattn_bv': _L1_xattn_in['bv'], 'L1_xattn_Wo': _L1_xattn_in['Wo'], 'L1_xattn_bo': _L1_xattn_in['bo'], 'L1_ffn_Wr': _L1_ffn_in['Wr'], 'L1_ffn_br': _L1_ffn_in['br'], 'L1_ffn_W1': _L1_ffn_in['W1'], 'L1_ffn_b1': _L1_ffn_in['b1'], 'L1_ffn_g1': _L1_ffn_in['g1'], 'L1_ffn_be1': _L1_ffn_in['be1'], 'L1_ffn_W2': _L1_ffn_in['W2'], 'L1_ffn_b2': _L1_ffn_in['b2']}

def reference(x, ctx_1024, itok_SxS2_0_2016, fside_BxSxS2_0, mask_BxSxS2_ff0, L0_attn_Wqkv_w, L0_attn_Wqkv_b, L0_attn_conv_w, L0_attn_conv_b, L0_attn_out_w, L0_attn_out_b, L0_xattn_igate_w, L0_xattn_igate_b, L0_xattn_fgate_w, L0_xattn_fgate_b, L0_xattn_rpe, L0_xattn_ln_w, L0_xattn_ln_b, L0_ffn_ln1_g, L0_ffn_ln1_b, L0_ffn_Wqkv, L0_ffn_Wproj, L0_ffn_ln2_g, L0_ffn_ln2_b, L0_ffn_Wgate, L0_ffn_W1, L0_ffn_b1, L0_ffn_W2, L0_ffn_b2, L1_attn_wq, L1_attn_wk, L1_attn_wv, L1_attn_wo, L1_xattn_Wq, L1_xattn_bq, L1_xattn_Wk, L1_xattn_bk, L1_xattn_Wv, L1_xattn_bv, L1_xattn_Wo, L1_xattn_bo, L1_ffn_Wr, L1_ffn_br, L1_ffn_W1, L1_ffn_b1, L1_ffn_g1, L1_ffn_be1, L1_ffn_W2, L1_ffn_b2):
    import jax
    import jax.numpy as jnp

    def _L0_attn_ref(x, Wqkv_w, Wqkv_b, conv_w, conv_b, out_w, out_b):
        import jax, jax.numpy as jnp
        import numpy as np
        import math
        D_MODEL = 128
        NUM_HEADS = 16
        HEAD_DIM = D_MODEL // NUM_HEADS
        B, S = (2, 256)

        def _causal_attn(q, k, v):
            scale = 1.0 / math.sqrt(q.shape[-1])
            scores = jnp.einsum('bthd,bshd->bhts', q, k) * scale
            t = q.shape[1]
            mask = jnp.tril(jnp.ones((t, t), dtype=bool))
            scores = jnp.where(mask, scores, -jnp.inf)
            attn = jax.nn.softmax(scores, axis=-1)
            return jnp.einsum('bhts,bshd->bthd', attn, v)
        b, s, d = x.shape
        qkv = x @ Wqkv_w.T + Wqkv_b
        qkv = qkv.reshape(b, s, 3, NUM_HEADS, HEAD_DIM)
        q, k, v = (qkv[:, :, 0], qkv[:, :, 1], qkv[:, :, 2])
        ctx = _causal_attn(q, k, v)
        ctx_c = ctx.reshape(b, s, d).transpose(0, 2, 1)
        conv_out = jax.lax.conv_general_dilated(ctx_c, conv_w, window_strides=(1,), padding=[(1, 1)], dimension_numbers=('NCH', 'OIH', 'NCH')) + conv_b[None, :, None]
        q2 = conv_out.transpose(0, 2, 1).reshape(b, s, NUM_HEADS, HEAD_DIM)
        ctx2 = _causal_attn(q2, k, v)
        out = ctx2.reshape(b, s, d) @ out_w.T + out_b
        return out

    def _L0_xattn_ref(q, k, v, igate_w, igate_b, fgate_w, fgate_b, rpe, ln_w, ln_b, hops):
        import jax, jax.numpy as jnp
        import numpy as np
        B, S, DIM, NH = (32, 64, 128, 8)
        DH = DIM // NH
        EPS = 1e-06
        LN_EPS = 1e-05

        def _make_hops(n):
            hops = np.zeros((n, n), dtype=np.int64)
            cur = 1
            for i in range(n):
                for j in range(i + 1, n):
                    hops[i, j] = cur
                    hops[j, i] = cur
                    cur += 1
            return (hops, cur)

        def _mlstm_forward(q, k, v, igate_w, igate_b, fgate_w, fgate_b, rpe, ln_w, ln_b, hops):
            Bq, Sq, _ = q.shape
            pos_emb = rpe[hops]
            gate_in = jnp.concatenate([q, k, v], axis=-1)
            ig = gate_in @ igate_w.T + igate_b
            fg = gate_in @ fgate_w.T + fgate_b
            ig = jnp.transpose(ig, (0, 2, 1))
            fg = jnp.transpose(fg, (0, 2, 1))
            qh = q.reshape(Bq, Sq, NH, DH).transpose(0, 2, 1, 3)
            kh = k.reshape(Bq, Sq, NH, DH).transpose(0, 2, 1, 3)
            vh = v.reshape(Bq, Sq, NH, DH).transpose(0, 2, 1, 3)
            log_f = jax.nn.log_sigmoid(fg)
            csum = jnp.cumsum(log_f, axis=-1)
            csum = jnp.concatenate([jnp.zeros((Bq, NH, 1), csum.dtype), csum], axis=-1)
            lfm = csum[:, :, :, None] - csum[:, :, None, :]
            ltr = jnp.tril(jnp.ones((Sq, Sq), dtype=bool))
            log_fg_matrix = jnp.where(ltr, lfm[:, :, 1:, 1:], -jnp.inf)
            log_D = log_fg_matrix + ig[:, :, None, :]
            max_log_D = jnp.max(log_D, axis=-1, keepdims=True)
            D = jnp.exp(log_D - max_log_D)
            k_scaled = kh / np.sqrt(DH).astype(np.float32)
            pe = pos_emb.reshape(Sq, Sq, NH, DH)
            k_hop = jnp.einsum('bhvc,vmhc->bhvm', qh, pe)
            qk = jnp.einsum('bhsd,bhtd->bhst', qh, k_scaled)
            C = (qk + k_hop) * D
            normalizer = jnp.maximum(jnp.abs(jnp.sum(C, axis=-1, keepdims=True)), jnp.exp(-max_log_D))
            Cn = C / (normalizer + EPS)
            h = Cn @ vh
            mu = jnp.mean(h, axis=-1, keepdims=True)
            var = jnp.mean(jnp.square(h - mu), axis=-1, keepdims=True)
            hn = (h - mu) / jnp.sqrt(var + LN_EPS)
            w = (1.0 + ln_w).reshape(NH, DH)
            b = ln_b.reshape(NH, DH)
            hn = hn * w[None, :, None, :] + b[None, :, None, :]
            return hn.transpose(0, 2, 1, 3).reshape(Bq, Sq, DIM)
        return _mlstm_forward(q, k, v, igate_w, igate_b, fgate_w, fgate_b, rpe, ln_w, ln_b, hops)

    def _L0_ffn_ref(x, ln1_g, ln1_b, Wqkv, Wproj, ln2_g, ln2_b, Wgate, W1, b1, W2, b2):
        import jax, jax.numpy as jnp
        import numpy as np
        import math
        B, T, D, H, E, TOPK, CAPF = (4, 256, 128, 16, 8, 2, 2.0)
        HD = D // H

        def layernorm(x, g, b, eps=1e-05):
            m = jnp.mean(x, -1, keepdims=True)
            v = jnp.mean(jnp.square(x - m), -1, keepdims=True)
            return (x - m) * jax.lax.rsqrt(v + eps) * g + b

        def block_forward(x, ln1_g, ln1_b, Wqkv, Wproj, ln2_g, ln2_b, Wgate, W1, b1, W2, b2):
            Bb, Tt, d = x.shape
            hd = HD
            half = hd // 2
            h = layernorm(x, ln1_g, ln1_b)
            qkv = (h @ Wqkv).reshape(Bb, Tt, H, 3 * hd)
            q, k, v = (qkv[..., :hd], qkv[..., hd:2 * hd], qkv[..., 2 * hd:])
            inv_freq = 1.0 / 10000.0 ** (jnp.arange(0, hd, 2, dtype=jnp.float32) / hd)
            ang = jnp.arange(Tt, dtype=jnp.float32)[:, None] * inv_freq
            sin = jnp.sin(ang)[None, :, None, :].astype(x.dtype)
            cos = jnp.cos(ang)[None, :, None, :].astype(x.dtype)

            def rope(t):
                t1, t2 = (t[..., :half], t[..., half:])
                return jnp.concatenate([t1 * cos - t2 * sin, t1 * sin + t2 * cos], -1)
            q, k = (rope(q), rope(k))
            scores = jnp.einsum('bqhd,bkhd->bhqk', q, k) / math.sqrt(hd)
            causal = jnp.tril(jnp.ones((Tt, Tt), dtype=bool))
            scores = jnp.where(causal, scores, jnp.asarray(-1000000000.0, scores.dtype))
            probs = jax.nn.softmax(scores, axis=-1)
            attn = jnp.einsum('bhqk,bkhd->bqhd', probs, v).reshape(Bb, Tt, d) @ Wproj
            x = x + attn
            h2 = layernorm(x, ln2_g, ln2_b)
            flat = h2.reshape(-1, d)
            N = flat.shape[0]
            capacity = int(math.ceil(CAPF * N / E))
            gates = jax.nn.softmax((flat @ Wgate).astype(jnp.float32), -1).astype(flat.dtype)
            _, top_inds = jax.lax.top_k(gates, TOPK)
            mask = jnp.zeros((N, E), dtype=bool).at[jnp.arange(N)[:, None], top_inds].set(True)
            pos = jnp.cumsum(mask.astype(jnp.int32), axis=0) * mask - 1
            keep = (pos < capacity) & mask
            t_flat = jnp.repeat(jnp.arange(N), TOPK)
            e_flat = top_inds.reshape(-1)
            p = pos[t_flat, e_flat]
            kp = keep[t_flat, e_flat]
            p_eff = jnp.where(kp, p, capacity)
            exp_in = jnp.zeros((E, capacity, d), flat.dtype).at[e_flat, p_eff].set(flat[t_flat], mode='drop')
            hmid = jax.nn.gelu(jnp.einsum('ecd,edf->ecf', exp_in, W1) + b1[:, None, :], approximate=False)
            exp_out = jnp.einsum('ecf,efd->ecd', hmid, W2) + b2[:, None, :]
            gate = gates[t_flat, e_flat] * kp.astype(flat.dtype)
            p_g = jnp.minimum(p_eff, capacity - 1)
            moe = jnp.zeros((N, d), flat.dtype).at[t_flat].add(exp_out[e_flat, p_g] * gate[:, None])
            return x + moe.reshape(Bb, Tt, d)
        return block_forward(x, ln1_g, ln1_b, Wqkv, Wproj, ln2_g, ln2_b, Wgate, W1, b1, W2, b2)

    def _L1_attn_ref(x, wq, wk, wv, wo):
        import jax, jax.numpy as jnp
        import numpy as np
        B, S, D = (2, 256, 128)
        N_HEADS, N_KV_HEADS = (16, 4)
        HEAD_DIM = D // N_HEADS
        KV_GROUPS = N_HEADS // N_KV_HEADS
        ROPE_BASE = 10000.0

        def _apply_rope(t, cos, sin):
            t1, t2 = jnp.split(t, 2, axis=-1)
            return jnp.concatenate([t1 * cos - t2 * sin, t1 * sin + t2 * cos], axis=-1)
        Bx, Sx, Dx = x.shape
        q = (x @ wq).reshape(Bx, Sx, N_HEADS, HEAD_DIM)
        k = (x @ wk).reshape(Bx, Sx, N_KV_HEADS, HEAD_DIM)
        v = (x @ wv).reshape(Bx, Sx, N_KV_HEADS, HEAD_DIM)
        half = HEAD_DIM // 2
        inv_freq = 1.0 / ROPE_BASE ** (jnp.arange(0, half, dtype=jnp.float32) / half)
        pos = jnp.arange(Sx, dtype=jnp.float32)
        ang = pos[:, None] * inv_freq[None, :]
        cos = jnp.cos(ang)[:, None, :]
        sin = jnp.sin(ang)[:, None, :]
        q = _apply_rope(q, cos, sin)
        k = _apply_rope(k, cos, sin)
        k = jnp.broadcast_to(k[:, :, None, :, :], (Bx, Sx, KV_GROUPS, N_KV_HEADS, HEAD_DIM)).reshape(Bx, Sx, N_HEADS, HEAD_DIM)
        v = jnp.broadcast_to(v[:, :, None, :, :], (Bx, Sx, KV_GROUPS, N_KV_HEADS, HEAD_DIM)).reshape(Bx, Sx, N_HEADS, HEAD_DIM)
        scale = 1.0 / jnp.sqrt(jnp.float32(HEAD_DIM))
        scores = jnp.einsum('bshd,bthd->bhst', q, k) * scale
        causal = jnp.tril(jnp.ones((Sx, Sx), dtype=bool))
        scores = jnp.where(causal[None, None, :, :], scores, jnp.float32(-jnp.inf))
        attn = jax.nn.softmax(scores, axis=-1)
        out = jnp.einsum('bhst,bthd->bshd', attn, v).reshape(Bx, Sx, Dx)
        return out @ wo

    def _L1_xattn_ref(q, k, v, attn_bias, attention_mask, Wq, bq, Wk, bk, Wv, bv, Wo, bo):
        import jax, jax.numpy as jnp
        import numpy as np
        HIDDEN = 128
        HEADS = 16
        DK = HIDDEN // HEADS
        B, N = (2, 256)
        b, n, _ = q.shape
        scale = DK ** (-0.5)
        qh = (q @ Wq + bq).reshape(b, n, HEADS, DK).transpose(0, 2, 1, 3)
        kh = (k @ Wk + bk).reshape(b, -1, HEADS, DK).transpose(0, 2, 1, 3)
        vh = (v @ Wv + bv).reshape(b, -1, HEADS, DK).transpose(0, 2, 1, 3)
        scores = jnp.einsum('bhnd,bhmd->bhnm', qh * scale, kh)
        scores = scores + attn_bias[:, None, :, :] + attention_mask[:, None, :, :]
        probs = jax.nn.softmax(scores, axis=-1)
        ctx = jnp.einsum('bhnm,bhmd->bhnd', probs, vh)
        ctx = ctx.transpose(0, 2, 1, 3).reshape(b, n, HEADS * DK)
        return ctx @ Wo + bo

    def _L1_ffn_ref(x, Wr, br, W1, b1, g1, be1, W2, b2):
        import jax, jax.numpy as jnp
        import numpy as np
        IN_DIM = 128
        HIDDEN = 128
        OUT_DIM = 128
        NUM_EXPERTS = 16
        TOP_K = 2
        ROUTER_TEMP = 1.0
        LN_EPS = 1e-05

        def _layernorm(h, g, b):
            mu = jnp.mean(h, axis=-1, keepdims=True)
            var = jnp.mean(jnp.square(h - mu), axis=-1, keepdims=True)
            return (h - mu) * jax.lax.rsqrt(var + LN_EPS) * g + b
        orig_shape = x.shape[:-1]
        x_flat = x.reshape(-1, x.shape[-1])
        logits = (x_flat @ Wr + br) / max(ROUTER_TEMP, 1e-06)
        probs = jax.nn.softmax(logits, axis=-1)
        topk_w, topk_idx = jax.lax.top_k(probs, TOP_K)
        topk_w = topk_w / jnp.clip(jnp.sum(topk_w, axis=-1, keepdims=True), 1e-09)
        h = jnp.einsum('nc,ech->neh', x_flat, W1) + b1
        h = _layernorm(h, g1, be1)
        h = jax.nn.gelu(h, approximate=False)
        expert_out = jnp.einsum('neh,eho->neo', h, W2) + b2
        sel = jnp.take_along_axis(expert_out, topk_idx[:, :, None], axis=1)
        y_flat = jnp.sum(sel * topk_w[:, :, None], axis=1)
        return y_flat.reshape(*orig_shape, y_flat.shape[-1])
    x = _layernorm(x + _L0_attn_ref(x, L0_attn_Wqkv_w, L0_attn_Wqkv_b, L0_attn_conv_w, L0_attn_conv_b, L0_attn_out_w, L0_attn_out_b), axis=-1)
    x = _layernorm(x + _L0_xattn_ref(x, ctx_1024, ctx_1024, L0_xattn_igate_w, L0_xattn_igate_b, L0_xattn_fgate_w, L0_xattn_fgate_b, L0_xattn_rpe, L0_xattn_ln_w, L0_xattn_ln_b, itok_SxS2_0_2016), axis=-1)
    x = _layernorm(x + _L0_ffn_ref(x, L0_ffn_ln1_g, L0_ffn_ln1_b, L0_ffn_Wqkv, L0_ffn_Wproj, L0_ffn_ln2_g, L0_ffn_ln2_b, L0_ffn_Wgate, L0_ffn_W1, L0_ffn_b1, L0_ffn_W2, L0_ffn_b2), axis=-1)
    x = _layernorm(x + _L1_attn_ref(x, L1_attn_wq, L1_attn_wk, L1_attn_wv, L1_attn_wo), axis=-1)
    x = _layernorm(x + _L1_xattn_ref(x, ctx_1024, ctx_1024, fside_BxSxS2_0, mask_BxSxS2_ff0, L1_xattn_Wq, L1_xattn_bq, L1_xattn_Wk, L1_xattn_bk, L1_xattn_Wv, L1_xattn_bv, L1_xattn_Wo, L1_xattn_bo), axis=-1)
    x = _layernorm(x + _L1_ffn_ref(x, L1_ffn_Wr, L1_ffn_br, L1_ffn_W1, L1_ffn_b1, L1_ffn_g1, L1_ffn_be1, L1_ffn_W2, L1_ffn_b2), axis=-1)
    return x

_drawn_inputs = setup_inputs


def setup_inputs(seed=0):
    import zlib

    import numpy as np

    out = dict(_drawn_inputs(seed))
    spreads = {'L0_attn_Wqkv_b': (0.0, 0.1),
     'L0_attn_conv_b': (0.0, 2.0),
     'L0_attn_out_b': (0.0, 0.1),
     'L0_xattn_ln_b': (0.0, 0.1),
     'L0_ffn_ln1_g': (1.0, 0.6),
     'L0_ffn_ln1_b': (0.0, 0.406),
     'L0_ffn_ln2_g': (1.0, 0.6),
     'L0_ffn_ln2_b': (0.0, 0.56),
     'L0_ffn_b1': (0.0, 0.53),
     'L0_ffn_b2': (0.0, 0.1),
     'L1_xattn_bq': (0.0, 0.8),
     'L1_xattn_bk': (0.0, 2.0),
     'L1_xattn_bv': (0.0, 0.1),
     'L1_xattn_bo': (0.0, 0.1),
     'L1_ffn_g1': (1.0, 0.2),
     'L1_ffn_be1': (0.0, 0.301)}
    factors = {'L0_attn_conv_w': 43.718,
     'L0_xattn_igate_b': 64.0,
     'L0_ffn_W1': 2.818,
     'L0_ffn_W2': 2.689,
     'L1_attn_wq': 8.0,
     'L1_attn_wk': 8.0,
     'L1_xattn_Wq': 8.0,
     'L1_xattn_Wk': 8.0}
    for name, (base, spread) in spreads.items():
        noise = np.random.default_rng([zlib.crc32(name.encode()), seed]).standard_normal(out[name].shape)
        drawn = base * np.exp(spread * noise) if base else spread * noise
        out[name] = jnp.asarray(drawn.astype(out[name].dtype))
    for name, factor in factors.items():
        out[name] = (out[name] * factor).astype(out[name].dtype)
    return out
```

```python
from contextlib import ExitStack

import numpy as np
import concourse.bass as bass
from concourse import mybir

F32 = mybir.dt.float32
BF16 = mybir.dt.bfloat16
I32 = mybir.dt.int32
U32 = mybir.dt.uint32
ACT = mybir.ActivationFunctionType
ALU = mybir.AluOpType
AX = mybir.AxisListType.X

P = 128
S = 64
D = 128
NB = P // S
H = 16
HD = D // H
MH = 8
MD = D // MH
NR = 2
U = 2
CREDIT = 2
E0, F0 = 8, 4
E1 = 16
BELOW = 64.0
FAR = 2.0 ** 20
EPS_LN = 1e-5
NEG = -1e30
SCALE = HD ** -0.5


def capacity(n_tokens):
    return -(-2 * n_tokens // E0)


def slot_tiles(n_tokens):
    return 2 * n_tokens // P + E1


def constants(n_tokens):
    p = np.arange(P)
    same = (p[:, None] // S) == (p[None, :] // S)
    t = np.arange(S)
    half = HD // 2
    inv_freq = (1.0 / np.float32(10000.0) ** (np.arange(half, dtype=np.float32) / half)).astype(np.float32)
    ang = (p % S).astype(np.float32)[None, :] * inv_freq[p % half][:, None]
    f = {
        "ident": np.eye(P),
        "tri2": same & (p[:, None] <= p[None, :]),
        "ones2": same,
        "diag64": (p[:, None] % S) == t[None, :],
        "head16": p[:, None] // HD == np.arange(H)[None, :],
        "head8": p[:, None] // MD == np.arange(MH)[None, :],
        "head4": (p[:, None] % 64) // MD == np.arange(64 // MD)[None, :],
        "cos": np.cos(ang.astype(np.float64)),
        "sin": np.sin(ang.astype(np.float64)),
    }
    f["head8q"] = f["head8"] * MD ** -0.5
    b = {"tri16": p[:, None] <= p[None, :], "ones16": np.ones((P, P)), "ident16": np.eye(P), "causal16": np.where(t[None, :] <= (p % S)[:, None], 0.0, NEG)}
    f["expert"] = np.tile(np.arange(E1) - BELOW, (P, 1))
    f["region0"] = np.tile(np.arange(E0) * capacity(n_tokens), (P, 1))
    n = slot_tiles(n_tokens)
    f["tile_start"] = np.tile(np.arange(n) * P, (P, 1))
    return ({k: v.astype(np.float32) for k, v in f.items()}, b)


def offsets(pieces):
    at, out = 0, {}
    for name, a in pieces.items():
        out[name] = (at, a.shape[1])
        at += a.shape[1]
    return out, at


def build(nc, T, out):
    B = T["x"].shape[0]
    NT = B * S // P
    cf, cb = constants(B * S)
    cf_at, cf_n = offsets(cf)
    cb_at, cb_n = offsets(cb)

    with ExitStack() as ctx:
        def sb(name, shape, dt=F32):
            return ctx.enter_context(nc.sbuf_tensor(name, shape, dt))

        def ps(name, shape, dt=F32):
            return ctx.enter_context(nc.psum_tensor(name, shape, dt))

        def sem(name):
            return ctx.enter_context(nc.semaphore(name))

        def dram(name, shape, dt=F32):
            return nc.dram_tensor(name, shape, dt, kind="Internal").ap()

        consts = sb("consts", [P, cf_n])
        consts16 = sb("consts16", [P, cb_n], BF16)

        def const(name):
            at, n = cf_at[name]
            return consts[:, at:at + n]

        def const16(name):
            at, n = cb_at[name]
            return consts16[:, at:at + n]

        ident, ident16, causal16 = const("ident"), const16("ident16"), const16("causal16")

        scores_ps = ps("scores_ps", [P, U, NR, 512])
        turned_ps = ps("turned_ps", [P, 2, 512])
        heads_ps = ps("heads_ps", [P, 512])
        desk_ps = ps("desk_ps", [P, 512])
        trans_ps = desk_ps[:, 0:P]
        setup_ps = scores_ps[:].rearrange("p u g (k n) -> p (u g k) n", n=P)

        def both(name, n, dt=F32):
            b = sb(name, [P, U, n], dt)
            return [b[:, u, :] for u in range(U)]

        x_in, x_out, x_res = both("x_in", D), both("x_out", D), both("x_res", D)
        x_T, q_T, o_T, ctx_o, y = both("x_T", P), both("q_T", P), both("o_T", P), both("ctx_o", D), both("y", D)
        turned, probs = both("turned", H * S), both("probs", H * S)
        k_bd, v_bd = both("k_bd", H * P), both("v_bd", 8 * NB * 2 * (HD + 1))
        row_max, recip = both("row_max", H), both("recip", H)
        pad_T = both("pad_T", NB * (S + 2))
        stat, mv, veps, rstd = both("stat", 6), both("mv", 2), both("veps", 1), both("rstd", 1)
        minus_half, ln_eps = sb("minus_half", [P, 16]), sb("ln_eps", [P, 1])

        w_raw = sb("w_raw", [P, 7, P])
        a_w = sb("a_w", [P, 7, P])
        a_col = sb("a_col", [P, 3])
        a_row = sb("a_row", [P, 2, D])

        HOPS = S // 2
        hop_at = sb("hop_at", [P, HOPS], I32)
        assert HOPS == 2 * E1
        hop_rows = sb("hop_rows", [P, HOPS, D])
        hop_T = sb("hop_T", [P, HOPS, P])
        o_w1, o_w2 = hop_rows[:, 0:E1, :], hop_rows[:, E1:2 * E1, :]
        o_b1, o_b2 = hop_T[:, 0:E1, :], hop_T[:, E1:2 * E1, :]
        GS = min(512, capacity(B * S))
        NJ = slot_tiles(B * S)
        pool_n = NJ * E1 + 6 * U * P
        shared = sb("shared", [P, max(U * F0 * GS, pool_n, U * (2 * P + 12 * S))])

        def views(at, n):
            return [shared[:, at + n * u:at + n * u + n] for u in range(U)]
        hx_in, hx_T, hop_bd, hop_out = (views(U * at, n) for at, n in (
            (0, D), (D, P), (D + P, 4 * S), (D + P + 4 * S, MH * S)))
        g_raw, g_w = sb("gate_raw", [2 * MH, 3, D]), sb("gate_w", [P, 3, 2 * MH])
        g_row = sb("gate_bias", [P, 2 * MH])
        m_row = sb("mlstm_ln", [P, 2, D])
        c_in, c_two, hop_in = both("c_in", D), both("c_two", NB * D), both("hop_in", MH * S)
        c_T = both("c_T", P)
        gates, neg_abs, exp_abs, soft = both("gates", 16), both("neg_abs", 8), both("exp_abs", 8), both("soft", 8)
        log_f, csum, g_key = both("log_f", 8), both("csum", 8), both("g_key", 8)
        g_diag, decay = both("g_diag", MH * S), both("decay", MH * S)
        cmax, floor, denom, denom2, denom3 = (both(k, 8) for k in ("cmax", "floor", "denom", "denom2", "denom3"))
        m_vbd = both("m_vbd", 4 * NB * 2 * (MD + 1))
        h_sum, h_mid, h_sq, h_var = both("h_sum", 8), both("h_mid", D), both("h_sq", D), both("h_var", 8)
        h_veps, h_rstd, z = both("h_veps", 8), both("h_rstd", 8), both("z", D)
        f_raw = sb("ffn_qkv_raw", [P, 3 * D])
        f_w = sb("ffn_attn_w", [P, 6, D])
        f_col = sb("ffn_ln", [P, 4])
        f_gate = sb("ffn_gate", [P, 8])
        x2, xn, r4 = both("x2", D), both("xn", D), both("r4", D)
        h_T = both("h_T", P)
        rope_c, rope_s, rope_k = both("rope_c", 2 * P), both("rope_s", 2 * P), both("rope_k", P)
        logits0 = sb("logits0", [P, NT, 8])

        NSLOT0 = E0 * capacity(B * S)
        NSLOT1 = NJ * P
        assert NT * E1 <= H * S
        r_gate, r_tmp, r_pos = (sb(k, [P, NT, E1]) for k in ("r_gate", "r_tmp", "r_pos"))
        r_scan, r_scan2, r_one, r_two = (a[:, 0:NT * E1].rearrange("p (t e) -> p t e", e=E1) for a in turned + probs)
        r_mask = sb("r_mask", [P, NT * E1], BF16)
        r_a, r_b = sb("r_a", [P, NT]), sb("r_b", [P, NT])
        r_cnt, r_cnt2, r_end, r_base = (sb(k, [P, E1]) for k in ("r_cnt", "r_cnt2", "r_end", "r_base"))
        r_int = sb("r_int", [P, E1], I32)
        r_le, r_ej = shared[:, 0:NJ * E1].rearrange("p (j e) -> p j e", e=E1), sb("r_ej", [P, NJ])
        expert_of = sb("expert_of", [P, NJ], I32)
        slot_f, weight = sb("slot_f", [P, 2, NT]), sb("weight", [P, 2, NT])
        slot_put, slot_get = sb("slot_put", [P, 2, NT], U32), sb("slot_get", [P, 2, NT], U32)
        r_slot, r_low = sb("r_slot", [P, 2, NT], I32), sb("r_low", [P, 2, NT], I32)
        token = sb("token", [P, NT], I32)
        put_at, put_tok = both("put_at", 2, U32), both("put_tok", 1, I32)
        zeros_i = sb("zeros_i", [P, NSLOT1 // P if NSLOT1 > NSLOT0 else NSLOT0 // P], I32)
        CAP = capacity(B * S)
        GE, J = CAP // GS, GS // P
        assert CAP % GS == 0 and GS % P == 0 and (GE == 1 or GE % 2 == 0)
        e_w1 = [sb(f"e_w1{w}", [P, F0 * P]) for w in range(2)]
        e_w2 = [sb(f"e_w2{w}", [P, F0, D]) for w in range(2)]
        e_b1 = [sb(f"e_b1{w}", [P, F0]) for w in range(2)]
        e_b2 = [sb(f"e_b2{w}", [P, D]) for w in range(2)]
        at0_all, at1_all = sb("at0_all", [P, NSLOT0 // GS, J], I32), sb("at1_all", [P, NJ], I32)
        e_at, e_in, e_T, e_out = both("e_at", J, I32), both("e_in", GS), both("e_T", GS), both("e_out", GS)
        e_mid = [a.rearrange("p (f n) -> p f n", f=F0) for a in views(0, F0 * GS)]
        l_raw = sb("l_raw", [P, 2 * 32])
        l_w = sb("l_w", [P, 6, D])
        c_w = sb("c_w", [P, 4, D])
        c_col, c_row = sb("c_col", [P, 3]), sb("c_row", [P, 2, D])
        rt_w, rt_row = sb("rt_w", [P, E1]), sb("rt_row", [P, E1])
        got, got_at, got_w = both("got", 2 * D), both("got_at", 2, U32), both("got_w", 2)
        fm_in, fm = both("fm_in", 2 * S), both("fm", S)
        x4, x5, x5b, x6 = both("x4", D), both("x5", D), both("x5b", D), both("x6", D)
        logits1 = sb("logits1", [P, NT, E1])
        o_g, o_b = sb("o_g", [P, E1]), sb("o_b", [P, E1])
        o_at = both("o_at", 1, I32)
        o_in, o_in_T, o_h, o_hn, o_g_T, o_out = (views(NJ * E1 + U * P * k, P) for k in range(6))

        loaded, w_turned, w_ready = sem("loaded"), sem("weights_turned"), sem("weights_ready")
        w_copied = sem("weights_copied")
        zeroed = sem("constants_set")
        dve_done = ["k_copied", "max_done", "shifted", "recip_done", "normed",  "y_done",
                    "stat_done", "mv_done", "ln_done"]
        act_done = ["q_copied", "exp_done", "turn0_copied", "turn1_copied"]
        pe_done = ["qk_done", "scores_done", "turn0_done", "turn1_done", "pv_done", "conv_done",
                   "out_done"]
        pool_done = ["x_res_done", "veps_done", "rstd_done"]
        s = {k: sem(k) for k in dve_done + act_done + pe_done + pool_done}
        desk_full, desk_empty = sem("desk_full"), sem("desk_empty")
        in_loaded = [sem(f"x_in_loaded{u}") for u in range(U)]
        x_stored = [sem(f"x_out_stored{u}") for u in range(U)]

        hop_idx, hop_gathered = sem("hop_index_loaded"), sem("hop_rows_gathered")
        hop_turned, hop_copied = sem("hop_turned"), sem("hop_copied")
        hx_loaded = [sem(f"hx_loaded{u}") for u in range(U)]
        hop_stored = [sem(f"hop_stored{u}") for u in range(U)]
        c_loaded = [sem(f"c_loaded{u}") for u in range(U)]
        xn_stored = [sem(f"xn_stored{u}") for u in range(U)]
        route_shifted, route_exp = sem("route_shifted"), sem("route_exp")
        route_masked, route_counted, route_chain = sem("route_masked"), sem("route_counted"), sem("route_chain")
        counts_read = sem("route_counts_read")
        zero_sem, table_sem, routed = sem("zeros_set"), sem("tables_cleared"), sem("routed")
        put_done = [sem(f"put_done{u}") for u in range(U)]
        e_loaded = [sem(f"e_weights_loaded{w}") for w in range(2)]
        e_in_loaded = [sem(f"e_in_loaded{u}") for u in range(U)]
        at_loaded = sem("slot_tables_loaded")
        e_stored = [sem(f"e_out_stored{u}") for u in range(U)]
        gelu_done, up_done = sem("gelu_done"), sem("up_done")
        got_loaded, x6_stored = ([sem(f"{k}{u}") for u in range(U)] for k in ("got_loaded", "x6_stored"))
        late = sem("late_weights_loaded")
        o_in_loaded, o_stored = ([sem(f"{k}{u}") for u in range(U)] for k in ("o_in_loaded", "o_stored"))
        z_loaded, z_stored = ([sem(f"{k}{u}") for u in range(U)] for k in ("z_loaded", "z_stored"))
        dve2 = ["e_out_done", "expert_done", "got_ready", "c1_done", "c2_done", "biased",
                "o_h_done", "o_hn_done", "o_out_done",
                "hb_done", "hop_out1", "gates_done", "neg_abs_done", "log_f_done", "g_key_done", "cmax_done",
                "denom_done", "denom2_done", "denom3_done", "h_sum_done", "h_mid_done", "h_var_done", "rope_done", "x3_done"]
        act2 = ["e_T_done", "o_T_done", "o_g_done", "hop_out0", "m_v_done", "exp_abs_done", "soft_done", "decay_done", "floor_done"]
        pe2 = ["e_turned", "down_done", "o_turned", "o_up", "o_hturned", "o_down", "hop_done"]
        pool2 = ["put_ready", "at_done", "fm_done", "x5b_done", "g_diag_done", "h_sq_done", "h_veps_done", "h_rstd_done", "z1_done", "z2_done",
                 "z3_done", "z_done", "rope_k_done", "r4_done"]
        s["put_free"] = sem("put_free")
        s |= {k: sem(k) for k in dve2 + act2 + pe2 + pool2}
        dve_done, act_done, pe_done, pool_done = dve_done + dve2, act_done + act2, pe_done + pe2, pool_done + pool2

        BASE = {1: dict(att=0, q=0, k=0, qk=0, out=0, ln=0, desk=0),
                3: dict(att=2 * NT, q=2 * NT, k=NT, qk=NT, out=NT, ln=NT, desk=4 * NT + S),
                5: dict(att=4 * NT, q=3 * NT, k=3 * NT, qk=2 * NT, out=2 * NT, ln=4 * NT, desk=13 * NT + S)}
        hop_dram = dram("hop_dram", [B * S, MH * S])
        xn_dram, r4_dram = dram("xn_dram", [B * S, D]), dram("r4_dram", [B * S, D])
        x6_dram = dram("x6_dram", [B * S, D])
        token_of0, token_of1 = dram("token_of0", [NSLOT0, 1], I32), dram("token_of1", [NSLOT1, 1], I32)
        moe0, moe1 = dram("moe0", [NSLOT0, D]), dram("moe1", [NSLOT1, D])
        c_flat = T["ctx_1024"].rearrange("b s d -> (b s) d")

        x1 = dram("x1", [B * S, D])
        x0 = T["x"].rearrange("b s d -> (b s) d")
        w_loads = [
            (consts[:], T["consts"]), (shared[:, 0:cb_n], T["consts16"]),
            (w_raw[:, 0:3, :], T["L0_attn_Wqkv_w"].rearrange("(k o) c -> o k c", k=3)),
            (w_raw[:, 3:6, :].rearrange("p a b -> p (a b)"), T["L0_attn_conv_w"].rearrange("o i k -> o (i k)")),
            (w_raw[:, 6, :], T["L0_attn_out_w"]),
            (a_col[:, 0:2], T["L0_attn_Wqkv_b"][0:2 * D].rearrange("(k o) -> o k", k=2)),
            (a_col[:, 2:3], T["L0_attn_conv_b"].rearrange("(o k) -> o k", k=1)),
            (a_row[:, 0, :], T["L0_attn_Wqkv_b"][2 * D:3 * D].partition_broadcast(P)),
            (a_row[:, 1, :], T["L0_attn_out_b"].partition_broadcast(P)),
        ]

        def column(name):
            return T[name].rearrange("(o k) -> o k", k=1)

        w_loads += [
            (hop_at[:], T["itok_SxS2_0_2016"].rearrange("(j v) m -> (v m) j", v=2)),
            (g_raw[0:MH].rearrange("p k c -> p (k c)"), T["L0_xattn_igate_w"]),
            (g_raw[MH:2 * MH].rearrange("p k c -> p (k c)"), T["L0_xattn_fgate_w"]),
            (g_row[:, 0:MH], T["L0_xattn_igate_b"].partition_broadcast(P)),
            (g_row[:, MH:2 * MH], T["L0_xattn_fgate_b"].partition_broadcast(P)),
            (m_row[:, 0, :], T["L0_xattn_ln_w"].partition_broadcast(P)),
            (m_row[:, 1, :], T["L0_xattn_ln_b"].partition_broadcast(P)),
            (f_raw[:], T["L0_ffn_Wqkv"]), (f_w[:, 5, :], T["L0_ffn_Wproj"]), (f_gate[:], T["L0_ffn_Wgate"]),
            (f_col[:, 0:1], column("L0_ffn_ln1_g")), (f_col[:, 1:2], column("L0_ffn_ln1_b")),
            (f_col[:, 2:3], column("L0_ffn_ln2_g")), (f_col[:, 3:4], column("L0_ffn_ln2_b")),
        ]

        late_loads = [
            (l_w[:, 0, :], T["L1_attn_wq"]), (l_raw[:, 0:32], T["L1_attn_wk"]), (l_raw[:, 32:64], T["L1_attn_wv"]),
            (l_w[:, 5, :], T["L1_attn_wo"]),
            (c_w[:, 0, :], T["L1_xattn_Wq"]), (c_w[:, 1, :], T["L1_xattn_Wk"]), (c_w[:, 2, :], T["L1_xattn_Wv"]),
            (c_w[:, 3, :], T["L1_xattn_Wo"]), (c_col[:, 0:1], column("L1_xattn_bq")),
            (c_col[:, 1:2], column("L1_xattn_bk")),
            (c_row[:, 0, :], T["L1_xattn_bv"].partition_broadcast(P)),
            (c_row[:, 1, :], T["L1_xattn_bo"].partition_broadcast(P)),
            (rt_w[:], T["L1_ffn_Wr"]), (rt_row[:], T["L1_ffn_br"].partition_broadcast(P)),
            (o_w1, T["L1_ffn_W1"].rearrange("e c h -> c e h")),
            (o_w2, T["L1_ffn_W2"].rearrange("e c h -> c e h")),
            (o_b1.rearrange("p e h -> p (e h)"), T["L1_ffn_b1"].rearrange("e h -> (e h)").partition_broadcast(P)),
            (o_b2.rearrange("p e h -> p (e h)"), T["L1_ffn_b2"].rearrange("e h -> (e h)").partition_broadcast(P)),
            (o_g[:], T["L1_ffn_g1"].rearrange("e h -> h e")), (o_b[:], T["L1_ffn_be1"].rearrange("e h -> h e")),
        ]

        def tile_rows(a, n):
            return a[bass.ds(n * P, P), :]

        W_READY = 5
        block = ctx.enter_context(nc.Block())

        @block.sync
        def _(sp):
            for u in range(U):
                sp.sem_inc(x_stored[u], 16)
            for dst, src in w_loads:
                sp.dma_start(dst, src, allow_slow_non_contiguous=True).then_inc(loaded, 16)

            def load1(t, u):
                sp.wait_ge(s["x_res_done"], t + u + 1)
                sp.dma_start(x_in[u], tile_rows(x0, t + u)).then_inc(in_loaded[u], 16)

            def store1(t, u):
                sp.wait_ge(s["ln_done"], t + u + 1 + 2)
                sp.dma_start(tile_rows(x1, t + u), x_out[u]).then_inc(x_stored[u], 16)

            for u in range(U):
                load1(0, u)
            sp.wait_ge(zero_sem, 1)
            sp.dma_start(token_of0.rearrange("(p n) x -> p (n x)", p=P), zeros_i[:, 0:NSLOT0 // P])\
              .then_inc(table_sem, 16)
            sp.dma_start(token_of1.rearrange("(p n) x -> p (n x)", p=P), zeros_i[:, 0:NSLOT1 // P])\
              .then_inc(table_sem, 16)
            with sp.Fori(0, NT // U - 1) as r:
                t = U * r
                for u in range(U):
                    load1(t + U, u)
                for u in range(U):
                    store1(t, u)
            for u in range(U):
                store1(NT - U, u)
            for u in range(U):
                sp.wait_ge(x_stored[u], 16 * (NT // U) + 16)

            x1_rows = x1.rearrange("(b v) d -> b v d", v=S)
            hop_rows_dram = hop_dram.rearrange("(b v) k -> b v k", v=S)

            def load2(v, u):
                sp.wait_ge(desk_full, 4 * NT + v + u - 1)
                sp.dma_start(hx_in[u][0:B], x1_rows[:, bass.ds(v + u, 1), :].rearrange("b v d -> b (v d)"))\
                  .then_inc(hx_loaded[u], 16)

            def store2(v, u):
                sp.wait_ge(s["hop_out0"], v + u + 3)
                sp.wait_ge(s["hop_out1"], v + u + 3)
                sp.dma_start(hop_rows_dram[:, bass.ds(v + u, 1), :].rearrange("b v k -> b (v k)"),
                             hop_out[u][0:B]).then_inc(hop_stored[u], 16)

            for u in range(U):
                sp.sem_inc(hop_stored[u], 16)
                load2(0, u)
            with sp.Fori(0, S // U - 1) as r:
                for u in range(U):
                    load2(U * r + U, u)
                for u in range(U):
                    store2(U * r, u)
            for u in range(U):
                store2(S - U, u)
            for u in range(U):
                sp.wait_ge(hop_stored[u], 16 * (S // U) + 16)

            for dst, src in late_loads:
                sp.dma_start(dst, src, allow_slow_non_contiguous=True).then_inc(late, 16)

            def load3(t, u):
                sp.wait_ge(s["z_done"], t + u + 1)
                sp.dma_start(x_in[u], tile_rows(x1, t + u)).then_inc(in_loaded[u], 16)
                sp.dma_start(c_in[u], tile_rows(c_flat, t + u)).then_inc(c_loaded[u], 16)
                two = c_flat[bass.ds((t + u) * P, P), :].rearrange("(b t) d -> t b d", b=NB)
                for par in range(2):
                    sp.dma_start(c_two[u][S * par:S * par + S].rearrange("p (b d) -> p b d", b=NB), two)\
                      .then_inc(c_loaded[u], 16)
                sp.dma_start(hop_in[u], tile_rows(hop_dram, t + u)).then_inc(c_loaded[u], 16)

            def store3(t, u):
                sp.wait_ge(s["ln_done"], NT + 3 * t + 2 * U + u + 3)
                sp.dma_start(tile_rows(xn_dram, t + u), xn[u]).then_inc(xn_stored[u], 16)
                sp.wait_ge(s["r4_done"], t + u + 3)
                sp.dma_start(tile_rows(r4_dram, t + u), r4[u]).then_inc(xn_stored[u], 16)

            per = 32
            for u in range(U):
                sp.sem_inc(xn_stored[u], per)
                load3(0, u)
            with sp.Fori(0, NT // U - 1) as r:
                for u in range(U):
                    load3(U * r + U, u)
                for u in range(U):
                    store3(U * r, u)
            for u in range(U):
                store3(NT - U, u)
            for u in range(U):
                sp.wait_ge(xn_stored[u], per * (NT // U) + per)

            def watch_puts(n0):
                with sp.Fori(0, NT // U) as r:
                    for u in range(U):
                        sp.wait_ge(put_done[u], 16 * n0 + 32 * r + 32)
                        sp.sem_inc(s["put_free"], 1)

            for u in range(U):
                sp.sem_inc(e_stored[u], 16)
            sp.sem_inc(s["put_free"], CREDIT)
            watch_puts(0)
            sp.dma_start(at0_all[:], token_of0.rearrange("(q p j) x -> p q (j x)", p=P, j=J),
                         allow_slow_non_contiguous=True).then_inc(at_loaded, 16)
            out0 = moe0.rearrange("(q p j) d -> q p (j d)", p=P, j=J)

            with sp.Fori(0, E0 // 2) as r:
                for i in range(2 * GE):
                    if i >= 2:
                        sp.wait_ge(s["e_out_done"], 2 * GE * r + i - 2 + 3)
                        sp.dma_start(out0[bass.ds(2 * GE * r + i - 2, 1)].rearrange("q p n -> p (q n)"),
                                     e_out[i % 2]).then_inc(e_stored[i % 2], 16)
                for i in range(2 * GE - 2, 2 * GE):
                    sp.wait_ge(s["e_out_done"], 2 * GE * r + i + 3)
                    sp.dma_start(out0[bass.ds(2 * GE * r + i, 1)].rearrange("q p n -> p (q n)"),
                                 e_out[i % 2]).then_inc(e_stored[i % 2], 16)

            for u in range(U):
                sp.wait_ge(e_stored[u], 16 * GE * E0 // 2 + 16)

            for u in range(U):
                sp.sem_inc(x6_stored[u], 16)
            fs_flat = T["fside_BxSxS2_0"].rearrange("b s t -> (b s) t")
            mask_flat = T["mask_BxSxS2_ff0"].rearrange("b s t -> (b s) t")

            def load5(t, u):
                sp.wait_ge(s["x5b_done"], t + u + 1)
                sp.wait_ge(s["c2_done"], t + u + 1)
                sp.wait_ge(s["fm_done"], t + u + 1)
                sp.dma_start(x_in[u], tile_rows(r4_dram, t + u)).then_inc(in_loaded[u], 16)
                sp.dma_start(c_in[u], tile_rows(c_flat, t + u)).then_inc(c_loaded[u], 16)
                sp.dma_start(fm_in[u][:, 0:S], tile_rows(fs_flat, t + u)).then_inc(c_loaded[u], 16)
                sp.dma_start(fm_in[u][:, S:2 * S], tile_rows(mask_flat, t + u)).then_inc(c_loaded[u], 16)

            def store5(t, u):
                sp.wait_ge(s["ln_done"], BASE[5]["ln"] + 3 * t + 2 * U + u + 3)
                sp.dma_start(tile_rows(x6_dram, t + u), x6[u])\
                  .then_inc(x6_stored[u], 16)

            for u in range(U):
                load5(0, u)
            with sp.Fori(0, NT // U - 1) as r:
                for u in range(U):
                    load5(U * r + U, u)
                for u in range(U):
                    store5(U * r, u)
            for u in range(U):
                store5(NT - U, u)
            for u in range(U):
                sp.wait_ge(x6_stored[u], 16 * (NT // U) + 16)

            for u in range(U):
                sp.sem_inc(o_stored[u], 16)
                sp.sem_inc(z_stored[u], 16)
            watch_puts(NT)
            sp.dma_start(at1_all[:], token_of1.rearrange("(p q) x -> p (q x)", p=P)).then_inc(at_loaded, 16)

            def store6(r, u):
                sp.wait_ge(s["o_out_done"], U * r + u + 3)
                sp.dma_start(tile_rows(moe1, U * r + u), o_out[u]).then_inc(o_stored[u], 16)

            with sp.Fori(0, NJ // U - 1) as r:
                for u in range(U):
                    store6(r, u)
            for u in range(U):
                store6(NJ // U - 1, u)
            for u in range(U):
                sp.wait_ge(o_stored[u], 16 * (NJ // U) + 16)

            def load7(t, u):
                sp.wait_ge(s["c1_done"], NT + t + u + 1)
                sp.dma_start(x_in[u], tile_rows(x6_dram, t + u)).then_inc(z_loaded[u], 16)

            def store7(t, u):
                sp.wait_ge(s["ln_done"], 7 * NT + NJ + t + u + 3)
                sp.dma_start(tile_rows(out.rearrange("b s d -> (b s) d"), t + u), x_out[u]).then_inc(z_stored[u], 16)

            for u in range(U):
                load7(0, u)
            with sp.Fori(0, NT // U - 1) as r:
                for u in range(U):
                    load7(U * r + U, u)
                for u in range(U):
                    store7(U * r, u)
            for u in range(U):
                store7(NT - U, u)
            for u in range(U):
                sp.wait_ge(z_stored[u], 16 * (NT // U) + 16)

        @block.tensor
        def _(pe):
            for k in pe_done:
                pe.sem_inc(s[k], CREDIT)
            pe.wait_ge(loaded, 16 * len(w_loads))
            taps = w_raw[:, 3:6, :].rearrange("p a b -> p (a b)").rearrange("p (i k) -> p k i", k=3)
            for k in range(7):
                last = pe.transpose(setup_ps[:, k, :], taps[:, k - 3, :] if 3 <= k < 6 else w_raw[:, k, :], ident)
            for k in range(3):
                last = pe.transpose(setup_ps[:, 8 + k, 0:2 * MH], g_raw[:, k, :], ident[0:2 * MH, 0:2 * MH])
            last.then_inc(w_turned, 1)
            pe.wait_ge(w_ready, W_READY)
            pe.wait_ge(zeroed, U + 1)

            def scores(m, u, q, k_done, causal):
                pe.wait_ge(s["q_copied"], q + 2)
                pe.wait_ge(s["k_copied"], k_done + 2)
                pe.wait_ge(s["shifted"], m)
                keys = k_bd[u].rearrange("p (h t) -> p h t", t=P)
                for g in range(NR):
                    if causal:
                        pe.matmul(scores_ps[:, u, g, :], ident16,
                                  causal16.unsqueeze(1).broadcast_to([P, 8, S]),
                                  start=True, stop=False, skip_group_check=True)
                for b in range(NB):
                    for g in range(NR):
                        last = pe.matmul(scores_ps[S * b:S * b + S, u, g, :],
                                         q_T[u][:, S * b:S * b + S],
                                         keys[:, 8 * g:8 * g + 8, S * b:S * b + S],
                                         start=not causal, stop=True, skip_group_check=True)
                last.then_inc(s["scores_done"], 1)

            def mix(m, u, v_use):
                pe.wait_ge(s["exp_done"], m + 2)
                for half in range(2):
                    pe.wait_ge(s[f"turn{half}_copied"], m + 1)
                    for k in range(4):
                        hp = 4 * half + k
                        last = pe.transpose(turned_ps[:, half, P * k:P * k + P],
                                            probs[u][:, P * hp:P * hp + P], ident)
                    last.then_inc(s[f"turn{half}_done"], 1)
                pe.wait_ge(desk_empty, v_use + 2)
                pe.wait_ge(s["normed"], m + 1)
                for hp in range(8):
                    if hp % 4 == 0:
                        pe.wait_ge(s[f"turn{hp // 4}_copied"], m + 2)
                    last = pe.matmul(heads_ps[:, 36 * hp:36 * hp + 36], turned[u][:, P * hp:P * hp + P],
                                     v_bd[u][:, 36 * hp:36 * hp + 36], start=True, stop=True,
                                     skip_group_check=True)
                last.then_inc(s["pv_done"], 1)

            def turn(use, src):
                pe.wait_ge(desk_empty, use + 1)
                pe.transpose(trans_ps, src, ident).then_inc(desk_full, 1)

            def values(use, u, src_T, w):
                pe.wait_ge(desk_empty, use + 1)
                wv = w.rearrange("p (g h c) -> p h g c", g=8, h=2)
                for b in range(NB):
                    for par in range(2):
                        last = pe.matmul(desk_ps[S * par:S * par + S, S * b:S * b + S],
                                         src_T[u][:, S * b:S * b + S], wv[:, par], start=True, stop=True,
                                         skip_group_check=True)
                last.then_inc(desk_full, 1)

            with pe.Fori(0, NT // U) as r:
                t = U * r
                d = 4 * t
                for u in range(U):
                    pe.wait_ge(in_loaded[u], 8 * t + 16)
                    turn(d + u, x_in[u])
                for u in range(U):
                    pe.wait_ge(desk_empty, d + u + 2)
                    pe.wait_ge(s["y_done"], t + u + 1)
                    for k in range(2):
                        last = pe.matmul(scores_ps[:, u, k, 0:P], a_w[:, k, :], x_T[u],
                                         start=True, stop=True, skip_group_check=True)
                    last.then_inc(s["qk_done"], 1)
                for u in range(U):
                    values(d + 2 + u, u, x_T, a_w[:, 2, :])
                for u in range(U):
                    scores(2 * t + u + 1, u, 2 * t + u + 1, t + u + 1, True)
                for u in range(U):
                    mix(2 * t + u + 1, u, d + 2 + u)
                for u in range(U):
                    pe.wait_ge(s["normed"], 2 * t + u + 3)
                    turn(d + 4 + u, ctx_o[u])
                for u in range(U):
                    pe.wait_ge(desk_empty, d + 4 + u + 2)
                    pad = pad_T[u].rearrange("p (b s) -> p b s", b=NB)
                    for k in range(3):
                        last = pe.matmul(scores_ps[:, u, 0, 0:P], a_w[:, 3 + k, :], pad[:, :, k:k + S],
                                         start=(k == 0), stop=(k == 2), skip_group_check=True)
                    last.then_inc(s["conv_done"], 1)
                for u in range(U):
                    scores(2 * t + 2 + u + 1, u, 2 * t + 2 + u + 1, t + u + 1, True)
                for u in range(U):
                    mix(2 * t + 2 + u + 1, u, d + 2 + u)
                for u in range(U):
                    pe.wait_ge(s["normed"], 2 * t + 2 + u + 3)
                    turn(d + 6 + u, ctx_o[u])
                for u in range(U):
                    pe.wait_ge(desk_empty, d + 6 + u + 2)
                    pe.matmul(scores_ps[:, u, 0, 0:P], o_T[u], a_w[:, 6, :], start=True, stop=True,
                              skip_group_check=True).then_inc(s["out_done"], 1)

            pe.wait_ge(hop_gathered, 16 * HOPS)
            pe.wait_ge(s["y_done"], NT + 2)
            for c in range(HOPS // 4):
                if c >= 4:
                    pe.wait_ge(hop_copied, c - 3)
                for k in range(4):
                    last = pe.transpose(setup_ps[:, 4 * (c % 4) + k, :], hop_rows[:, 4 * c + k, :], ident)
                last.then_inc(hop_turned, 1)
            with pe.Fori(0, S // U) as r:
                v = U * r
                for u in range(U):
                    pe.wait_ge(hx_loaded[u], 8 * v + 16)
                    pe.wait_ge(desk_empty, 4 * NT + v + u + 1)
                    pe.transpose(desk_ps[:, 0:B], hx_in[u][0:B], ident[0:B, 0:B]).then_inc(desk_full, 1)
                for u in range(U):
                    pe.wait_ge(desk_empty, 4 * NT + v + u + 2)
                    pe.wait_ge(s["hb_done"], v + u + 3)
                    pe.wait_ge(s["hop_out0"], v + u + 1)
                    vu = pe.to_reg(v + u + 1)
                    pe.wait_ge(hop_copied, HOPS // 4)
                    pe.wait_ge(s["hop_out1"], vu)
                    for g in range(NR):
                        last = pe.matmul(scores_ps[0:B, u, g, 0:4 * S], hx_T[u][64 * g:64 * g + 64, 0:B],
                                         hop_bd[u][64 * g:64 * g + 64, :], start=True, stop=True,
                                         skip_group_check=True)
                    last.then_inc(s["hop_done"], 1)

            base = BASE[3]

            def rope_products(n, u, hT, w):
                for k in range(4):
                    last = pe.matmul(scores_ps[:, u, k // 2, P * (k % 2):P * (k % 2) + P], w[:, k, :], hT[u],
                                     start=True, stop=True, skip_group_check=True)
                last.then_inc(s["qk_done"], 1)

            with pe.Fori(0, NT // U) as r:
                t = U * r
                d = base["desk"] + 9 * t
                m = base["att"] + 2 * t
                for u in range(U):
                    pe.wait_ge(in_loaded[u], 8 * t + 8 * NT + 16)
                    turn(d + u, x_in[u])
                for u in range(U):
                    pe.wait_ge(c_loaded[u], 32 * t + 64)
                    turn(d + 2 + u, c_in[u])
                for u in range(U):
                    pe.wait_ge(desk_empty, d + 4 + u + 1)
                    for k, src in enumerate((x_T, c_T, c_T)):
                        last = pe.matmul(desk_ps[:, 0:2 * MH], src[u], g_w[:, k, :], start=(k == 0), stop=(k == 2))
                    last.then_inc(desk_full, 1)
                for u in range(U):
                    pe.wait_ge(s["log_f_done"], t + u + 3)
                    pe.wait_ge(desk_empty, d + 6 + u + 1)
                    pe.matmul(desk_ps[:, 0:MH], const("tri2"), log_f[u], start=True, stop=True).then_inc(desk_full, 1)
                for u in range(U):
                    pe.wait_ge(s["k_copied"], base["k"] + 2 * t + u + 3)
                    pe.wait_ge(s["shifted"], m + u + 1)
                    keys = k_bd[u][:, 0:MH * P].rearrange("p (h t) -> p h t", t=P)
                    for b in range(NB):
                        last = pe.matmul(scores_ps[S * b:S * b + S, u, 0, :], x_T[u][:, S * b:S * b + S],
                                         keys[:, :, S * b:S * b + S], start=True, stop=True, skip_group_check=True)
                    last.then_inc(s["scores_done"], 1)
                for u in range(U):
                    pe.wait_ge(s["g_diag_done"], t + u + 3)
                    pe.wait_ge(s["turn1_copied"], m + u + 2)
                    pe.matmul(turned_ps[:, 1, :], const("ones2"), g_diag[u], start=True, stop=False)
                    pe.matmul(turned_ps[:, 1, :], ident16, causal16.unsqueeze(1).broadcast_to([P, MH, S]),
                              start=False, stop=True).then_inc(s["turn1_done"], 1)
                for u in range(U):
                    pe.wait_ge(s["exp_done"], m + u + 3)
                    pe.wait_ge(s["turn0_copied"], m + u + 2)
                    for k in range(4):
                        last = pe.transpose(turned_ps[:, 0, P * k:P * k + P], probs[u][:, P * k:P * k + P], ident)
                    last.then_inc(s["turn0_done"], 1)
                    pe.wait_ge(s["m_v_done"], t + u + 3)
                    pe.wait_ge(s["normed"], m + u + 2)
                    pe.wait_ge(s["turn0_copied"], m + u + 3)
                    w = NB * 2 * (MD + 1)
                    for k in range(4):
                        last = pe.matmul(heads_ps[:, w * k:w * k + w], turned[u][:, P * k:P * k + P],
                                         m_vbd[u][:, w * k:w * k + w], start=True, stop=True, skip_group_check=True)
                    last.then_inc(s["pv_done"], 1)
                for u in range(U):
                    pe.wait_ge(s["ln_done"], base["ln"] + 3 * t + U + u + 3)
                    turn(d + 8 + u, xn[u])
                for u in range(U):
                    pe.wait_ge(desk_empty, d + 8 + u + 2)
                    rope_products(base["qk"] + t + u + 1, u, h_T, f_w)
                for u in range(U):
                    values(d + 10 + u, u, h_T, f_w[:, 4, :])
                for u in range(U):
                    scores(m + 2 + u + 1, u, base["q"] + t + u + 1, base["k"] + 2 * t + 2 + u + 1, True)
                for u in range(U):
                    mix(m + 2 + u + 1, u, d + 10 + u)
                for u in range(U):
                    pe.wait_ge(s["normed"], m + 2 + u + 3)
                    turn(d + 12 + u, ctx_o[u])
                for u in range(U):
                    pe.wait_ge(desk_empty, d + 12 + u + 2)
                    pe.matmul(scores_ps[:, u, 0, 0:P], o_T[u], f_w[:, 5, :], start=True, stop=True,
                              skip_group_check=True).then_inc(s["out_done"], 1)
                for u in range(U):
                    pe.wait_ge(s["ln_done"], base["ln"] + 3 * t + 2 * U + u + 3)
                    turn(d + 14 + u, xn[u])
                for u in range(U):
                    pe.wait_ge(desk_empty, d + 16 + u + 1)
                    pe.matmul(desk_ps[:, 0:8], h_T[u], f_gate[:], start=True, stop=True).then_inc(desk_full, 1)


            def count(n, E):
                pe.wait_ge(route_masked, n)
                cols = NT * E
                for c in range(-(-cols // 512)):
                    w = min(512, cols - 512 * c)
                    for k, lhs in enumerate(("tri16", "ones16")):
                        last = pe.matmul(scores_ps[:, k, c, 0:w], const16(lhs), r_mask[:, 512 * c:512 * c + w],
                                         start=True, stop=True)
                last.then_inc(route_counted, 1)

            count(1, E0)
            pe.wait_ge(counts_read, 1)

            with pe.Fori(0, E0 // 2) as r:
                for i in range(2 * GE):
                    w, u, q = i // GE, i % 2, 2 * GE * r + i
                    pe.wait_ge(e_in_loaded[u], 16 * J * (GE * r + i // 2 + 1))
                    pe.wait_ge(s["e_T_done"], q + 1)
                    for j in range(J):
                        last = pe.transpose(turned_ps[:, u, P * j:P * j + P], e_in[u][:, P * j:P * j + P], ident)
                    last.then_inc(s["e_turned"], 1)
                    pe.wait_ge(s["e_T_done"], q + 3)
                    pe.wait_ge(e_loaded[w], 64 * r + 64)
                    for f in range(F0):
                        pe.wait_ge(gelu_done, F0 * q + f + 1)
                        pe.matmul(scores_ps[:, f // 2, f % 2, 0:GS], e_w1[w][:, P * f:P * f + P], e_T[u],
                                  start=True, stop=True).then_inc(up_done, 1)
                    pe.wait_ge(s["e_out_done"], q + 1)
                    bank = (heads_ps, desk_ps)[u]
                    for f in range(F0):
                        pe.wait_ge(gelu_done, F0 * q + f + 1 + F0)
                        for j in range(J):
                            last = pe.matmul(bank[:, P * j:P * j + P], e_mid[u][:, f, P * j:P * j + P],
                                             e_w2[w][:, f, :], start=(f == 0 and j == 0),
                                             stop=(f == F0 - 1 and j == J - 1), skip_group_check=True)
                    last.then_inc(s["down_done"], 1)

            base = BASE[5]
            pe.wait_ge(late, 16 * len(late_loads))
            pe.wait_ge(w_ready, W_READY + 2)
            with pe.Fori(0, NT // U) as r:
                t = U * r
                d = base["desk"] + 9 * t
                m = base["att"] + 2 * t
                ln = base["ln"] + 3 * t
                o2 = base["qk"] + 2 * t
                for u in range(U):
                    pe.wait_ge(s["ln_done"], ln + u + 3)
                    turn(d + u, x4[u])
                for u in range(U):
                    pe.wait_ge(desk_empty, d + u + 2)
                    rope_products(o2 + u + 1, u, x_T, l_w)
                for u in range(U):
                    values(d + 2 + u, u, x_T, l_w[:, 4, :])
                for u in range(U):
                    scores(m + u + 1, u, base["q"] + 2 * t + u + 1, base["k"] + 2 * t + u + 1, True)
                for u in range(U):
                    mix(m + u + 1, u, d + 2 + u)
                for u in range(U):
                    pe.wait_ge(s["normed"], m + u + 3)
                    turn(d + 4 + u, ctx_o[u])
                for u in range(U):
                    pe.wait_ge(desk_empty, d + 4 + u + 2)
                    pe.matmul(scores_ps[:, u, 0, 0:P], o_T[u], l_w[:, 5, :], start=True, stop=True,
                              skip_group_check=True).then_inc(s["out_done"], 1)
                for u in range(U):
                    pe.wait_ge(c_loaded[u], 32 * NT + 24 * t + 48)
                    turn(d + 6 + u, c_in[u])
                for u in range(U):
                    values(d + 8 + u, u, c_T, c_w[:, 2, :])
                for u in range(U):
                    pe.wait_ge(s["ln_done"], ln + U + u + 3)
                    turn(d + 10 + u, x5[u])
                for u in range(U):
                    pe.wait_ge(desk_empty, d + 10 + u + 2)
                    for k, src in enumerate((x_T, c_T)):
                        last = pe.matmul(scores_ps[:, u, k, 0:P], c_w[:, k, :], src[u], start=True, stop=True,
                                         skip_group_check=True)
                    last.then_inc(s["qk_done"], 1)
                for u in range(U):
                    scores(m + 2 + u + 1, u, base["q"] + 2 * t + 2 + u + 1, base["k"] + 2 * t + 2 + u + 1, False)
                for u in range(U):
                    mix(m + 2 + u + 1, u, d + 8 + u)
                for u in range(U):
                    pe.wait_ge(s["normed"], m + 2 + u + 3)
                    turn(d + 12 + u, ctx_o[u])
                for u in range(U):
                    pe.wait_ge(desk_empty, d + 12 + u + 2)
                    pe.matmul(scores_ps[:, u, 0, 0:P], o_T[u], c_w[:, 3, :], start=True, stop=True,
                              skip_group_check=True).then_inc(s["out_done"], 1)
                for u in range(U):
                    pe.wait_ge(s["ln_done"], ln + 2 * U + u + 3)
                    turn(d + 14 + u, x6[u])
                for u in range(U):
                    pe.wait_ge(desk_empty, d + 16 + u + 1)
                    pe.matmul(desk_ps[:, 0:E1], x_T[u], rt_w[:], start=True, stop=True).then_inc(desk_full, 1)

            count(2, E1)
            pe.wait_ge(counts_read, 2)
            with pe.Fori(0, NJ // U) as r:
                for u in range(U):
                    n = U * r + u + 1
                    pe.wait_ge(o_in_loaded[u], 16 * r + 16)
                    pe.wait_ge(s["o_T_done"], n)
                    pe.transpose(turned_ps[:, u, 0:P], o_in[u], ident).then_inc(s["o_turned"], 1)
                for u in range(U):
                    n = U * r + u + 1
                    e = pe.value_load(expert_of[0:1, bass.ds(U * r + u, 1)], min_val=0, max_val=E1 - 1)
                    pe.wait_ge(s["o_T_done"], n + 2)
                    pe.wait_ge(s["o_h_done"], n)
                    pe.matmul(scores_ps[:, u, 0, 0:P], o_in_T[u], o_w1[:, bass.ds(e, 1), :].rearrange("p e h -> p (e h)"),
                              start=True, stop=True).then_inc(s["o_up"], 1)
                for u in range(U):
                    n = U * r + u + 1
                    pe.wait_ge(s["ln_done"], 7 * NT + n + 2)
                    pe.wait_ge(s["o_g_done"], n)
                    pe.transpose(scores_ps[:, u, 1, 0:P], o_hn[u], ident).then_inc(s["o_hturned"], 1)
                for u in range(U):
                    n = U * r + u + 1
                    e = pe.value_load(expert_of[0:1, bass.ds(U * r + u, 1)], min_val=0, max_val=E1 - 1)
                    pe.wait_ge(s["o_g_done"], n + 2)
                    pe.wait_ge(s["o_out_done"], n)
                    pe.matmul((heads_ps, desk_ps)[u][:, 0:P], o_g_T[u],
                              o_w2[:, bass.ds(e, 1), :].rearrange("p e h -> p (e h)"),
                              start=True, stop=True).then_inc(s["o_down"], 1)

        @block.scalar
        def _(act):
            for k in act_done:
                act.sem_inc(s[k], CREDIT)
            act.sem_inc(desk_empty, 1)
            act.wait_ge(loaded, 16 * len(w_loads))
            act.wait_ge(zeroed, U + 1)

            def copy_turned(use, dst, src=None, **kw):
                act.wait_ge(desk_full, use + 1)
                act.activation(dst, trans_ps if src is None else src, ACT.Identity, **kw).then_inc(desk_empty, 1)

            def exp(m, u, scale):
                act.wait_ge(s["shifted"], m + 2)
                act.activation(probs[u], probs[u], ACT.Exp, scale=scale).then_inc(s["exp_done"], 1)

            def copy_probs(m, u):
                act.wait_ge(s["pv_done"], m)
                for half in range(2):
                    act.wait_ge(s[f"turn{half}_done"], m + 2)
                    act.activation(turned[u][:, 512 * half:512 * half + 512], turned_ps[:, half, :],
                                   ACT.Identity).then_inc(s[f"turn{half}_copied"], 1)

            with act.Fori(0, NT // U) as r:
                t = U * r
                for u in range(U):
                    copy_turned(4 * t + u, x_T[u])
                for u in range(U):
                    act.wait_ge(s["qk_done"], t + u + 3)
                    act.activation(q_T[u], scores_ps[:, u, 0, 0:P], ACT.Identity,
                                   bias=a_col[:, 0:1]).then_inc(s["q_copied"], 1)
                for u in range(U):
                    exp(2 * t + u + 1, u, SCALE)
                for u in range(U):
                    copy_probs(2 * t + u + 1, u)
                for u in range(U):
                    pad = pad_T[u].rearrange("p (b s) -> p b s", b=NB)
                    copy_turned(4 * t + 4 + u, pad[:, :, 1:1 + S], trans_ps.rearrange("p (b s) -> p b s", b=NB))
                for u in range(U):
                    act.wait_ge(s["conv_done"], t + u + 3)
                    act.activation(q_T[u], scores_ps[:, u, 0, 0:P], ACT.Identity,
                                   bias=a_col[:, 2:3]).then_inc(s["q_copied"], 1)
                for u in range(U):
                    exp(2 * t + 2 + u + 1, u, SCALE)
                for u in range(U):
                    copy_probs(2 * t + 2 + u + 1, u)
                for u in range(U):
                    copy_turned(4 * t + 6 + u, o_T[u])

            with act.Fori(0, S // U) as r:
                v = U * r
                for u in range(U):
                    copy_turned(4 * NT + v + u, hx_T[u][:, 0:B], desk_ps[:, 0:B])
                for u in range(U):
                    act.wait_ge(s["hop_done"], v + u + 3)
                    act.wait_ge(hop_stored[u], 8 * v + 16)
                    act.activation(hop_out[u][0:B, 0:4 * S], scores_ps[0:B, u, 0, 0:4 * S], ACT.Identity)\
                       .then_inc(s["hop_out0"], 1)

            base = BASE[3]
            with act.Fori(0, NT // U) as r:
                t = U * r
                d = base["desk"] + 9 * t
                m = base["att"] + 2 * t
                for u in range(U):
                    copy_turned(d + u, x_T[u])
                for u in range(U):
                    copy_turned(d + 2 + u, c_T[u])
                for u in range(U):
                    act.wait_ge(s["pv_done"], m + u + 1)
                    act.wait_ge(c_loaded[u], 32 * t + 64)
                    mvv = m_vbd[u].rearrange("p (g b h c) -> p g b h c", g=4, b=NB, h=2)
                    cv = c_two[u].rearrange("p (b g h c) -> p g b h c", b=NB, g=4, h=2)
                    for par in range(2):
                        rows = slice(S * par, S * par + S)
                        last = act.activation(mvv[rows, :, :, par, 0:MD], cv[rows, :, :, par, :], ACT.Identity)
                    last.then_inc(s["m_v_done"], 1)
                for u in range(U):
                    act.wait_ge(s["neg_abs_done"], t + u + 3)
                    act.activation(exp_abs[u], neg_abs[u], ACT.Exp).then_inc(s["exp_abs_done"], 1)
                for u in range(U):
                    act.wait_ge(s["exp_abs_done"], t + u + 3)
                    act.activation(soft[u], exp_abs[u], ACT.Ln, bias=1.0).then_inc(s["soft_done"], 1)
                for u in range(U):
                    act.wait_ge(s["turn1_copied"], m + u + 3)
                    act.activation(decay[u], decay[u], ACT.Exp).then_inc(s["decay_done"], 1)
                    act.wait_ge(s["cmax_done"], t + u + 3)
                    act.activation(floor[u], cmax[u], ACT.Exp, scale=-1.0).then_inc(s["floor_done"], 1)
                for u in range(U):
                    act.wait_ge(s["turn0_done"], m + u + 3)
                    act.activation(turned[u][:, 0:512], turned_ps[:, 0, :], ACT.Identity)\
                       .then_inc(s["turn0_copied"], 1)
                for u in range(U):
                    copy_turned(d + 8 + u, h_T[u], scale=f_col[:, 0:1], bias=f_col[:, 1:2])
                for u in range(U):
                    exp(m + 2 + u + 1, u, SCALE)
                for u in range(U):
                    copy_probs(m + 2 + u + 1, u)
                for u in range(U):
                    copy_turned(d + 12 + u, o_T[u])
                for u in range(U):
                    copy_turned(d + 14 + u, h_T[u], scale=f_col[:, 2:3], bias=f_col[:, 3:4])
                for u in range(U):
                    copy_turned(d + 16 + u, logits0[:, bass.ds(t + u, 1), :].rearrange("p t e -> p (t e)"),
                                desk_ps[:, 0:8])


            def route_exponentials(n, E):
                act.wait_ge(route_shifted, n)
                act.activation(r_gate[:, :, 0:E], r_gate[:, :, 0:E], ACT.Exp).then_inc(route_exp, 1)

            route_exponentials(1, E0)
            act.sem_inc(gelu_done, F0)
            with act.Fori(0, E0 // 2) as r:
                for i in range(2 * GE):
                    w, u, q = i // GE, i % 2, 2 * GE * r + i
                    act.wait_ge(s["e_turned"], q + 3)
                    act.activation(e_T[u], turned_ps[:, u, 0:GS], ACT.Identity, scale=f_col[:, 2:3],
                                   bias=f_col[:, 3:4]).then_inc(s["e_T_done"], 1)
                    act.wait_ge(s["down_done"], q + 1)
                    act.wait_ge(e_loaded[w], 64 * r + 64)
                    for f in range(F0):
                        act.wait_ge(up_done, F0 * q + f + 1)
                        act.activation(e_mid[u][:, f, :], scores_ps[:, f // 2, f % 2, 0:GS], ACT.Gelu,
                                       bias=e_b1[w][:, f:f + 1]).then_inc(gelu_done, 1)

            base = BASE[5]
            act.wait_ge(late, 16 * len(late_loads))
            act.wait_ge(w_ready, W_READY + 2)
            with act.Fori(0, NT // U) as r:
                t = U * r
                d = base["desk"] + 9 * t
                m = base["att"] + 2 * t
                for u in range(U):
                    copy_turned(d + u, x_T[u])
                for u in range(U):
                    exp(m + u + 1, u, SCALE)
                for u in range(U):
                    copy_probs(m + u + 1, u)
                for u in range(U):
                    copy_turned(d + 4 + u, o_T[u])
                for u in range(U):
                    copy_turned(d + 6 + u, c_T[u])
                for u in range(U):
                    copy_turned(d + 10 + u, x_T[u])
                for u in range(U):
                    act.wait_ge(s["qk_done"], base["qk"] + 2 * t + 2 + u + 3)
                    act.activation(q_T[u], scores_ps[:, u, 0, 0:P], ACT.Identity, bias=c_col[:, 2:3],
                                   scale=SCALE).then_inc(s["q_copied"], 1)
                for u in range(U):
                    exp(m + 2 + u + 1, u, 1.0)
                for u in range(U):
                    copy_probs(m + 2 + u + 1, u)
                for u in range(U):
                    copy_turned(d + 12 + u, o_T[u])
                for u in range(U):
                    copy_turned(d + 14 + u, x_T[u])

            route_exponentials(2, E1)
            with act.Fori(0, NJ // U) as r:
                for u in range(U):
                    act.wait_ge(s["o_turned"], U * r + u + 3)
                    act.activation(o_in_T[u], turned_ps[:, u, 0:P], ACT.Identity).then_inc(s["o_T_done"], 1)
                for u in range(U):
                    e = act.value_load(expert_of[0:1, bass.ds(U * r + u, 1)], min_val=0, max_val=E1 - 1)
                    act.wait_ge(s["o_hturned"], U * r + u + 3)
                    act.activation(o_g_T[u], scores_ps[:, u, 1, 0:P], ACT.Gelu, scale=o_g[:, bass.ds(e, 1)],
                                   bias=o_b[:, bass.ds(e, 1)]).then_inc(s["o_g_done"], 1)

        @block.vector
        def _(dve):
            for k in dve_done:
                dve.sem_inc(s[k], CREDIT)
            dve.wait_ge(w_turned, 1)
            dve.wait_ge(loaded, 16 * len(w_loads))
            dve.tensor_copy(consts16[:], shared[:, 0:cb_n]).then_inc(w_ready, 1)
            dve.tensor_copy(a_w[:], setup_ps[:, 0:7, :]).then_inc(w_ready, 1)
            dve.tensor_copy(g_w[:], setup_ps[:, 8:11, 0:2 * MH]).then_inc(w_ready, 1)
            dve.tensor_scalar(m_row[:, 0, :], m_row[:, 0, :], 1.0, None, ALU.add).then_inc(w_ready, 1)

            def rotate(dst, src):
                dv = dst.rearrange("p (h k c) -> p h k c", h=H, k=2)
                sv = src.rearrange("p (h k c) -> p h k c", h=H, k=2)
                dve.tensor_scalar(dv[:, :, 0, :], sv[:, :, 1, :], -1.0, None, ALU.mult)
                return dve.tensor_copy(dv[:, :, 1, :], sv[:, :, 0, :])

            fr = f_raw[:].rearrange("p (h k c) -> p k h c", h=H, k=3)
            for k, at in enumerate((0, 2, 4)):
                last = dve.tensor_copy(f_w[:, at, :].rearrange("p (h c) -> p h c", h=H), fr[:, k])
            last.then_inc(w_copied, 1)
            dve.wait_ge(w_copied, 1)
            rotate(f_w[:, 1, :], f_w[:, 0, :])
            rotate(f_w[:, 3, :], f_w[:, 2, :]).then_inc(w_ready, 1)

            def spread_keys(u, src, bias, head, count):
                n = const(head).shape[1]
                out_v = k_bd[u][:, 0:n * P].rearrange("p (h t) -> p h t", h=n)
                in_v = src.unsqueeze(1).broadcast_to([P, n, P])
                mask = const(head).unsqueeze(2).broadcast_to([P, n, P])
                dve.scalar_tensor_tensor(out_v, in_v, bias, mask, ALU.add, ALU.mult).then_inc(count, 1)

            def softmax_shift(m, u):
                dve.wait_ge(s["scores_done"], m + 2)
                sc = scores_ps[:, u].rearrange("p g (h t) -> p (g h) t", t=S)
                dve.tensor_reduce(row_max[u], sc, AX, ALU.max)\
                   .then_inc(s["max_done"], 1)
                dve.wait_ge(s["max_done"], m + 2)
                dve.wait_ge(s["turn1_done"], m)
                mx = row_max[u].unsqueeze(2).broadcast_to([P, H, S])
                dve.tensor_tensor(probs[u].rearrange("p (h t) -> p h t", t=S), sc, mx,
                                  ALU.subtract).then_inc(s["shifted"], 1)

            def normalise(m, u):
                dve.wait_ge(s["pv_done"], m + 2)
                hv = heads_ps[:, 0:288].rearrange("p (g b h c) -> p g b h c", g=8, b=NB, h=2)
                for b in range(NB):
                    rows = slice(S * b, S * b + S)
                    last = dve.reciprocal(recip[u][rows].rearrange("p (g h) -> p g h", g=8), hv[rows, :, b, :, HD])
                last.then_inc(s["recip_done"], 1)
                dve.wait_ge(s["recip_done"], m + 2)
                for b in range(NB):
                    rows = slice(S * b, S * b + S)
                    r = recip[u][rows].rearrange("p (g h) -> p g h", g=8).unsqueeze(3).broadcast_to([S, 8, 2, HD])
                    last = dve.tensor_tensor(ctx_o[u][rows].rearrange("p (g h c) -> p g h c", g=8, h=2),
                                             hv[rows, :, b, :, 0:HD], r, ALU.mult)
                last.then_inc(s["normed"], 1)

            def copy_values(use, u, bias):
                dve.wait_ge(desk_full, use + 1)
                vv = v_bd[u].rearrange("p (g b h c) -> p g b h c", g=8, b=NB, h=2)
                pv = desk_ps[:, 0:P].rearrange("p (b g c) -> p g b c", b=NB, g=8)
                bv = bias.rearrange("p (g h c) -> p g h c", g=8, h=2) if bias is not None else None
                for par in range(2):
                    rows = slice(S * par, S * par + S)
                    if bias is None:
                        last = dve.tensor_copy(vv[rows, :, :, par, 0:HD], pv[rows])
                        continue
                    last = dve.tensor_tensor(vv[rows, :, :, par, 0:HD], pv[rows],
                                             bv[rows, :, par, :].unsqueeze(2).broadcast_to([S, 8, NB, HD]),
                                             ALU.add)
                last.then_inc(desk_empty, 1)

            def ln_stats(o, u, src):
                dve.bn_stats(stat[u], src).then_inc(s["stat_done"], 1)
                o2 = dve.to_reg(o + 2)
                dve.wait_ge(w_turned, 1)
                dve.wait_ge(s["stat_done"], o2)
                dve.bn_aggr(mv[u], stat[u]).then_inc(s["mv_done"], 1)

            def ln_apply(o, u, dst, src):
                dve.wait_ge(s["rstd_done"], o + 2)
                dve.tensor_scalar(dst, src, mv[u][:, 0:1], rstd[u], ALU.subtract, ALU.mult)\
                   .then_inc(s["ln_done"], 1)

            with dve.Fori(0, NT // U) as r:
                t = U * r
                for u in range(U):
                    dve.wait_ge(s["qk_done"], t + u + 3)
                    spread_keys(u, scores_ps[:, u, 1, 0:P], a_col[:, 1:2], "head16", s["k_copied"])
                for u in range(U):
                    copy_values(4 * t + 2 + u, u, a_row[:, 0, :])
                for u in range(U):
                    softmax_shift(2 * t + u + 1, u)
                for u in range(U):
                    normalise(2 * t + u + 1, u)
                for u in range(U):
                    softmax_shift(2 * t + 2 + u + 1, u)
                for u in range(U):
                    normalise(2 * t + 2 + u + 1, u)
                for u in range(U):
                    dve.wait_ge(s["out_done"], t + u + 3)
                    dve.wait_ge(s["x_res_done"], t + u + 3)
                    dve.tensor_tensor(y[u], scores_ps[:, u, 0, 0:P], x_res[u], ALU.add).then_inc(s["y_done"], 1)
                for u in range(U):
                    dve.wait_ge(s["y_done"], t + u + 3)
                    ln_stats(t + u + 1, u, y[u])
                for u in range(U):
                    dve.wait_ge(x_stored[u], 8 * t + 16)
                    ln_apply(t + u + 1, u, x_out[u], y[u])

            for c in range(HOPS // 4):
                dve.wait_ge(hop_turned, c + 1)
                dve.tensor_copy(hop_T[:, 4 * c:4 * c + 4, :], setup_ps[:, 4 * (c % 4):4 * (c % 4) + 4, :])\
                   .then_inc(hop_copied, 1)
            dve.wait_ge(hop_copied, HOPS // 4)
            hop_by_query = hop_T[:].rearrange("p j (v m) -> p (j v) m", v=2)
            with dve.Fori(0, S // U) as r:
                v = U * r
                for u in range(U):
                    dve.wait_ge(s["hop_done"], v + u + 1)
                    dve.tensor_tensor(hop_bd[u].rearrange("p (h m) -> p h m", h=4),
                                      hop_by_query[:, bass.ds(v + u, 1), :].broadcast_to([P, 4, S]),
                                      const("head4").unsqueeze(2).broadcast_to([P, 4, S]), ALU.mult)\
                       .then_inc(s["hb_done"], 1)
                for u in range(U):
                    dve.wait_ge(s["hop_done"], v + u + 3)
                    dve.wait_ge(hop_stored[u], 8 * v + 16)
                    dve.tensor_copy(hop_out[u][0:B, 4 * S:8 * S], scores_ps[0:B, u, 1, 0:4 * S])\
                       .then_inc(s["hop_out1"], 1)

            base = BASE[3]

            def rope(n, u):
                dve.wait_ge(s["qk_done"], n + 2)
                qk = scores_ps[:, u].rearrange("p g (r n) -> p r g n", n=P)
                for k, (dst, table) in enumerate(((rope_c, "cos"), (rope_s, "sin"))):
                    last = dve.tensor_tensor(dst[u].rearrange("p (g n) -> p g n", g=2), qk[:, k],
                                             const(table).unsqueeze(1).broadcast_to([P, 2, P]), ALU.mult)
                last.then_inc(s["rope_done"], 1)

            with dve.Fori(0, NT // U) as r:
                t = U * r
                n = t + 1
                d = base["desk"] + 9 * t
                m = base["att"] + 2 * t
                ln = base["ln"] + 3 * t
                for u in range(U):
                    dve.wait_ge(desk_full, d + 4 + u + 1)
                    dve.tensor_tensor(gates[u], desk_ps[:, 0:16], g_row[:], ALU.add).then_inc(s["gates_done"], 1)
                    dve.wait_ge(s["gates_done"], n + u + 2)
                    dve.sem_inc(desk_empty, 1)
                    dve.scalar_tensor_tensor(neg_abs[u], gates[u][:, 8:16], -1.0, gates[u][:, 8:16],
                                             ALU.mult, ALU.min).then_inc(s["neg_abs_done"], 1)
                for u in range(U):
                    dve.wait_ge(s["soft_done"], n + u + 2)
                    dve.scalar_tensor_tensor(log_f[u], gates[u][:, 8:16], 0.0, soft[u],
                                             ALU.min, ALU.subtract).then_inc(s["log_f_done"], 1)
                for u in range(U):
                    dve.wait_ge(desk_full, d + 6 + u + 1)
                    dve.tensor_copy(csum[u], desk_ps[:, 0:8])
                    dve.tensor_tensor(g_key[u], gates[u][:, 0:8], desk_ps[:, 0:8], ALU.subtract)\
                       .then_inc(s["g_key_done"], 1)
                    dve.wait_ge(s["g_key_done"], n + u + 2)
                    dve.sem_inc(desk_empty, 1)
                for u in range(U):
                    dve.wait_ge(s["turn1_done"], m + u + 3)
                    gm = turned_ps[:, 1, :].rearrange("p (h t) -> p h t", t=S)
                    dve.tensor_reduce(row_max[u][:, 0:8], gm, AX, ALU.max).then_inc(s["max_done"], 1)
                    dve.wait_ge(s["max_done"], m + u + 3)
                    dve.tensor_tensor(decay[u].rearrange("p (h t) -> p h t", t=S), gm,
                                      row_max[u][:, 0:8].unsqueeze(2).broadcast_to([P, 8, S]), ALU.subtract)\
                       .then_inc(s["turn1_copied"], 1)
                    dve.tensor_tensor(cmax[u], csum[u], row_max[u][:, 0:8], ALU.add).then_inc(s["cmax_done"], 1)
                for u in range(U):
                    dve.wait_ge(s["scores_done"], m + u + 3)
                    dve.tensor_tensor(probs[u][:, 0:512], scores_ps[:, u, 0, :], hop_in[u], ALU.add)\
                       .then_inc(s["shifted"], 1)
                    dve.wait_ge(s["shifted"], m + u + 3)
                    dve.wait_ge(s["decay_done"], n + u + 2)
                    dve.tensor_tensor(probs[u][:, 0:512], probs[u][:, 0:512], decay[u], ALU.mult)\
                       .then_inc(s["exp_done"], 1)
                for u in range(U):
                    dve.wait_ge(s["pv_done"], m + u + 3)
                    dve.wait_ge(s["floor_done"], n + u + 2)
                    hv = heads_ps[:, 0:272].rearrange("p (g b h c) -> p g b h c", g=4, b=NB, h=2)
                    for b in range(NB):
                        rows = slice(S * b, S * b + S)
                        last = dve.scalar_tensor_tensor(
                            denom[u][rows].rearrange("p (g h) -> p g h", g=4), hv[rows, :, b, :, MD], -1.0,
                            floor[u][rows].rearrange("p (g h) -> p g h", g=4), ALU.mult, ALU.max)
                    last.then_inc(s["denom_done"], 1)
                    dve.wait_ge(s["denom_done"], n + u + 2)
                    for b in range(NB):
                        rows = slice(S * b, S * b + S)
                        last = dve.tensor_tensor(
                            denom3[u][rows].rearrange("p (g h) -> p g h", g=4), hv[rows, :, b, :, MD],
                            denom[u][rows].rearrange("p (g h) -> p g h", g=4), ALU.max)
                    last.then_inc(s["denom3_done"], 1)
                    dve.wait_ge(s["denom3_done"], n + u + 2)
                    dve.tensor_scalar(denom2[u], denom3[u], 1e-6, None, ALU.add).then_inc(s["denom2_done"], 1)
                    dve.wait_ge(s["denom2_done"], n + u + 2)
                    dve.reciprocal(recip[u][:, 0:8], denom2[u]).then_inc(s["recip_done"], 1)
                    dve.wait_ge(s["recip_done"], m + u + 3)
                    for b in range(NB):
                        rows = slice(S * b, S * b + S)
                        rv = recip[u][rows, 0:8].rearrange("p (g h) -> p g h", g=4).unsqueeze(3)
                        last = dve.tensor_tensor(ctx_o[u][rows].rearrange("p (g h c) -> p g h c", g=4, h=2),
                                                 hv[rows, :, b, :, 0:MD], rv.broadcast_to([S, 4, 2, MD]), ALU.mult)
                    last.then_inc(s["normed"], 1)
                for u in range(U):
                    by_head = ctx_o[u].rearrange("p (h c) -> p h c", c=MD)
                    dve.wait_ge(s["normed"], m + u + 3)
                    dve.tensor_reduce(h_sum[u], by_head, AX, ALU.add).then_inc(s["h_sum_done"], 1)
                    dve.wait_ge(s["h_sum_done"], n + u + 2)
                    dve.scalar_tensor_tensor(h_mid[u].rearrange("p (h c) -> p h c", c=MD),
                                             h_sum[u].unsqueeze(2).broadcast_to([P, MH, MD]), -1.0 / MD, by_head,
                                             ALU.mult, ALU.add).then_inc(s["h_mid_done"], 1)
                for u in range(U):
                    dve.wait_ge(s["h_sq_done"], n + u + 2)
                    dve.tensor_reduce(h_var[u], h_sq[u].rearrange("p (h c) -> p h c", c=MD), AX, ALU.add)\
                       .then_inc(s["h_var_done"], 1)
                for u in range(U):
                    dve.wait_ge(s["z_done"], n + u + 2)
                    ln_stats(ln + u + 1, u, z[u])
                for u in range(U):
                    dve.wait_ge(s["r4_done"], n + u)
                    ln_apply(ln + u + 1, u, x2[u], z[u])
                for u in range(U):
                    dve.wait_ge(s["ln_done"], ln + u + 3)
                    ln_stats(ln + U + u + 1, u, x2[u])
                for u in range(U):
                    dve.wait_ge(xn_stored[u], 16 * t + 32)
                    ln_apply(ln + U + u + 1, u, xn[u], x2[u])
                for u in range(U):
                    rope(base["qk"] + n + u, u)
                for u in range(U):
                    dve.wait_ge(s["rope_k_done"], n + u + 2)
                    spread_keys(u, rope_k[u], 0.0, "head16", s["k_copied"])
                for u in range(U):
                    copy_values(d + 10 + u, u, None)
                for u in range(U):
                    softmax_shift(m + 2 + u + 1, u)
                for u in range(U):
                    normalise(m + 2 + u + 1, u)
                for u in range(U):
                    dve.wait_ge(s["out_done"], base["out"] + n + u + 2)
                    dve.tensor_tensor(y[u], scores_ps[:, u, 0, 0:P], x2[u], ALU.add).then_inc(s["y_done"], 1)
                for u in range(U):
                    dve.wait_ge(s["y_done"], base["out"] + n + u + 2)
                    ln_stats(ln + 2 * U + u + 1, u, y[u])
                for u in range(U):
                    ln_apply(ln + 2 * U + u + 1, u, xn[u], y[u])

            dve.wait_ge(late, 16 * len(late_loads))
            for k, at in enumerate((2, 4)):
                dve.tensor_copy(l_w[:, at, :].rearrange("p (g n) -> p g n", g=4),
                                l_raw[:, 32 * k:32 * k + 32].unsqueeze(1).broadcast_to([P, 4, 32]))
            dve.tensor_scalar(c_col[:, 2:3], c_col[:, 0:1], SCALE, None, ALU.mult).then_inc(w_ready, 1)
            dve.wait_ge(w_ready, W_READY + 1)
            rotate(l_w[:, 1, :], l_w[:, 0, :])
            rotate(l_w[:, 3, :], l_w[:, 2, :]).then_inc(w_ready, 1)

            links = [0]

            def link(ins):
                links[0] += 1
                ins.then_inc(route_chain, 1)
                dve.wait_ge(route_chain, links[0])

            def one_hot(dst, values, best, E):
                em = const("expert")[:, 0:E].unsqueeze(1).broadcast_to([P, NT, E])
                tmp = r_tmp[:, :, 0:E]
                link(dve.tensor_tensor(tmp, values, best.unsqueeze(2).broadcast_to([P, NT, E]), ALU.is_equal))
                link(dve.tensor_tensor(tmp, tmp, em, ALU.mult))
                link(dve.tensor_reduce(r_b[:], tmp, AX, ALU.min))
                link(dve.tensor_tensor(dst, em, r_b[:].unsqueeze(2).broadcast_to([P, NT, E]), ALU.is_equal))

            def route(n, E, logits, capped):
                gate, tmp, one, two, pos = (a[:, :, 0:E] for a in (r_gate, r_tmp, r_one, r_two, r_pos))
                wide = [P, NT, E]
                link(dve.tensor_reduce(r_a[:], logits[:], AX, ALU.max))
                dve.tensor_tensor(gate, logits[:], r_a[:].unsqueeze(2).broadcast_to(wide), ALU.subtract)\
                   .then_inc(route_shifted, 1)
                dve.wait_ge(route_exp, n)
                link(dve.tensor_reduce(r_a[:], gate, AX, ALU.add))
                link(dve.reciprocal(r_b[:], r_a[:]))
                link(dve.tensor_tensor(gate, gate, r_b[:].unsqueeze(2).broadcast_to(wide), ALU.mult))
                link(dve.tensor_reduce(weight[:, 0, :], gate, AX, ALU.max))
                one_hot(one, gate, weight[:, 0, :], E)
                link(dve.scalar_tensor_tensor(gate, one, -2.0, gate, ALU.mult, ALU.add))
                link(dve.tensor_reduce(weight[:, 1, :], gate, AX, ALU.max))
                one_hot(two, gate, weight[:, 1, :], E)
                dve.tensor_tensor(r_mask[:, 0:NT * E].rearrange("p (t e) -> p t e", e=E), one, two, ALU.add)\
                   .then_inc(route_masked, 1)
                dve.wait_ge(route_counted, n)
                tiles_in_bank = 512 // E
                scan = [r_scan, r_scan2]
                for c in range(-(-NT * E // 512)):
                    n_t = min(tiles_in_bank, NT - tiles_in_bank * c)
                    part = slice(tiles_in_bank * c, tiles_in_bank * c + n_t)
                    dve.tensor_copy(pos[:, part], scores_ps[:, 0, c, 0:n_t * E].rearrange("p (t e) -> p t e", e=E))
                    last = dve.tensor_copy(r_scan[:, part, 0:E],
                                           scores_ps[:, 1, c, 0:n_t * E].rearrange("p (t e) -> p t e", e=E))
                    link(last)
                dve.sem_inc(counts_read, 1)
                link(dve.tensor_tensor(pos, pos, r_scan[:, :, 0:E], ALU.subtract))
                step = 1
                while step < NT:
                    a, b = scan
                    dve.tensor_copy(b[:, 0:step, 0:E], a[:, 0:step, 0:E])
                    link(dve.tensor_tensor(b[:, step:NT, 0:E], a[:, step:NT, 0:E], a[:, 0:NT - step, 0:E], ALU.add))
                    scan = [b, a]
                    step *= 2
                total = scan[0]
                link(dve.scalar_tensor_tensor(pos, pos, -1.0, total[:, :, 0:E], ALU.add, ALU.add))
                if capped:
                    link(dve.tensor_scalar(tmp, pos, float(CAP), FAR, ALU.is_ge, ALU.mult))
                    link(dve.tensor_tensor(pos, pos, tmp, ALU.add))
                    region = const("region0")
                else:
                    link(dve.tensor_scalar(r_int[:], total[:, NT - 1, 0:E], float(P - 1), None, ALU.add))
                    link(dve.tensor_scalar(r_int[:], r_int[:], 7, 7, ALU.logical_shift_right,
                                           ALU.logical_shift_left))
                    link(dve.tensor_copy(r_cnt[:], r_int[:]))
                    link(dve.tensor_copy(r_end[:], r_cnt[:]))
                    ends, step = [r_end, r_cnt2], 1
                    while step < E:
                        a, b = ends
                        dve.tensor_copy(b[:, 0:step], a[:, 0:step])
                        link(dve.tensor_tensor(b[:, step:E], a[:, step:E], a[:, 0:E - step], ALU.add))
                        ends = [b, a]
                        step *= 2
                    end = ends[0]
                    link(dve.tensor_tensor(r_base[:], end[:], r_cnt[:], ALU.subtract))
                    link(dve.tensor_tensor(r_le, end[:].unsqueeze(1).broadcast_to([P, NJ, E]),
                                           const("tile_start").unsqueeze(2).broadcast_to([P, NJ, E]), ALU.is_le))
                    link(dve.tensor_reduce(r_ej[:], r_le, AX, ALU.add))
                    link(dve.tensor_scalar(expert_of[:], r_ej[:], float(E - 1), None, ALU.min))
                    region = r_base[:]
                link(dve.tensor_tensor(pos, pos, region.unsqueeze(1).broadcast_to(wide), ALU.add))
                for k, hot in enumerate((one, two)):
                    link(dve.tensor_tensor(tmp, hot, pos, ALU.mult))
                    link(dve.tensor_reduce(slot_f[:, k, :], tmp, AX, ALU.add))
                n_slots = NSLOT0 if capped else NSLOT1
                if capped:
                    link(dve.tensor_scalar(slot_put[:], slot_f[:], 0.0, None, ALU.add))
                    link(dve.scalar_tensor_tensor(weight[:], slot_f[:], FAR / 2, weight[:], ALU.is_lt, ALU.mult))
                else:
                    link(dve.tensor_scalar(r_slot[:], slot_f[:], 0.0, None, ALU.add))
                    link(dve.tensor_scalar(r_low[:], r_slot[:], P - 1, None, ALU.bitwise_and))
                    link(dve.tensor_scalar(r_slot[:], r_slot[:], 7, None, ALU.logical_shift_right))
                    link(dve.scalar_tensor_tensor(slot_put[:], r_low[:], float(NJ), r_slot[:], ALU.mult, ALU.add))
                    link(dve.tensor_tensor(r_a[:], weight[:, 0, :], weight[:, 1, :], ALU.add))
                    link(dve.tensor_scalar(r_a[:], r_a[:], 1e-9, None, ALU.max))
                    link(dve.reciprocal(r_b[:], r_a[:]))
                    link(dve.tensor_tensor(weight[:], weight[:], r_b[:].unsqueeze(1).broadcast_to([P, 2, NT]), ALU.mult))
                link(dve.tensor_scalar(slot_get[:], slot_f[:], float(n_slots - 1), None, ALU.min))

            dve.wait_ge(desk_empty, BASE[5]["desk"] + 1)
            route(1, E0, logits0, True)
            dve.sem_inc(routed, 1)

            with dve.Fori(0, E0 // 2) as r:
                for i in range(2 * GE):
                    w, u, q = i // GE, i % 2, 2 * GE * r + i
                    dve.wait_ge(s["down_done"], q + 3)
                    dve.wait_ge(e_stored[u], 16 * (GE * r + i // 2) + 16)
                    dve.wait_ge(e_loaded[w], 64 * r + 64)
                    dve.tensor_tensor(e_out[u].rearrange("p (j d) -> p j d", d=D),
                                      (heads_ps, desk_ps)[u][:, 0:GS].rearrange("p (j d) -> p j d", d=D),
                                      e_b2[w][:].unsqueeze(1).broadcast_to([P, J, D]), ALU.add)\
                       .then_inc(s["e_out_done"], 1)
                    if i % GE == GE - 1:
                        dve.wait_ge(s["e_out_done"], q + 3)
                        dve.sem_inc(s["expert_done"], 1)

            def combine(n, u, loads, dst):
                dve.wait_ge(got_loaded[u], loads)
                dve.scalar_tensor_tensor(y[u], got[u][:, 0:D], got_w[u][:, 0:1], x_in[u], ALU.mult, ALU.add)\
                   .then_inc(s["c1_done"], 1)
                dve.wait_ge(s["c1_done"], n + 2)
                dve.scalar_tensor_tensor(dst[u], got[u][:, D:2 * D], got_w[u][:, 1:2], y[u], ALU.mult, ALU.add)\
                   .then_inc(s["c2_done"], 1)

            def get_tables(n, tile, u):
                dve.wait_ge(s["c2_done"], n)
                dve.tensor_copy(got_w[u], weight[:, :, bass.ds(tile, 1)].rearrange("p k t -> p (k t)"))
                dve.tensor_copy(got_at[u], slot_get[:, :, bass.ds(tile, 1)].rearrange("p k t -> p (k t)"))\
                   .then_inc(s["got_ready"], 1)

            base = BASE[5]
            with dve.Fori(0, NT // U) as r:
                t = U * r
                n = t + 1
                d = base["desk"] + 9 * t
                m = base["att"] + 2 * t
                ln = base["ln"] + 3 * t
                o2 = base["out"] + 2 * t
                for u in range(U):
                    get_tables(n + u, t + u, u)
                for u in range(U):
                    dve.wait_ge(in_loaded[u], 16 * NT + 8 * t + 16)
                    combine(n + u, u, 16 * t + 32, z)
                for u in range(U):
                    dve.wait_ge(s["c2_done"], n + u + 2)
                    ln_stats(ln + u + 1, u, z[u])
                for u in range(U):
                    ln_apply(ln + u + 1, u, x4[u], z[u])
                for u in range(U):
                    rope(o2 + u + 1, u)
                for u in range(U):
                    dve.wait_ge(s["rope_k_done"], NT + n + u + 2)
                    spread_keys(u, rope_k[u], 0.0, "head16", s["k_copied"])
                for u in range(U):
                    copy_values(d + 2 + u, u, None)
                for u in range(U):
                    softmax_shift(m + u + 1, u)
                for u in range(U):
                    normalise(m + u + 1, u)
                for u in range(U):
                    dve.wait_ge(s["out_done"], o2 + u + 3)
                    dve.tensor_tensor(y[u], scores_ps[:, u, 0, 0:P], x4[u], ALU.add).then_inc(s["y_done"], 1)
                for u in range(U):
                    copy_values(d + 8 + u, u, c_row[:, 0, :])
                for u in range(U):
                    dve.wait_ge(s["y_done"], o2 + u + 3)
                    ln_stats(ln + U + u + 1, u, y[u])
                for u in range(U):
                    dve.wait_ge(s["x5b_done"], n + u)
                    ln_apply(ln + U + u + 1, u, x5[u], y[u])
                for u in range(U):
                    dve.wait_ge(s["qk_done"], base["qk"] + 2 * t + 2 + u + 3)
                    spread_keys(u, scores_ps[:, u, 1, 0:P], c_col[:, 1:2], "head16", s["k_copied"])
                for u in range(U):
                    mm = m + 2 + u + 1
                    dve.wait_ge(s["scores_done"], mm + 2)
                    dve.wait_ge(s["turn1_done"], mm)
                    dve.wait_ge(s["fm_done"], n + u + 2)
                    pv = probs[u].rearrange("p (h t) -> p h t", t=S)
                    dve.tensor_tensor(pv, scores_ps[:, u].rearrange("p g (h t) -> p (g h) t", t=S),
                                      fm[u].unsqueeze(1).broadcast_to([P, H, S]), ALU.add).then_inc(s["biased"], 1)
                    dve.wait_ge(s["biased"], n + u + 2)
                    dve.tensor_reduce(row_max[u], pv, AX, ALU.max).then_inc(s["max_done"], 1)
                    dve.wait_ge(s["max_done"], mm + 2)
                    dve.tensor_tensor(pv, pv, row_max[u].unsqueeze(2).broadcast_to([P, H, S]), ALU.subtract)\
                       .then_inc(s["shifted"], 1)
                for u in range(U):
                    normalise(m + 2 + u + 1, u)
                for u in range(U):
                    dve.wait_ge(s["out_done"], o2 + 2 + u + 3)
                    dve.wait_ge(s["x5b_done"], n + u + 2)
                    dve.tensor_tensor(y[u], scores_ps[:, u, 0, 0:P], x5b[u], ALU.add).then_inc(s["y_done"], 1)
                for u in range(U):
                    dve.wait_ge(s["y_done"], o2 + 2 + u + 3)
                    ln_stats(ln + 2 * U + u + 1, u, y[u])
                for u in range(U):
                    dve.wait_ge(x6_stored[u], 8 * t + 16)
                    ln_apply(ln + 2 * U + u + 1, u, x6[u], y[u])
                for u in range(U):
                    dve.wait_ge(desk_full, d + 16 + u + 1)
                    dve.tensor_tensor(logits1[:, bass.ds(t + u, 1), :].rearrange("p t e -> p (t e)"),
                                      desk_ps[:, 0:E1], rt_row[:], ALU.add).then_inc(desk_empty, 1)

            dve.wait_ge(desk_empty, BASE[5]["desk"] + 9 * NT + 1)
            route(2, E1, logits1, False)
            dve.sem_inc(routed, 1)
            with dve.Fori(0, NJ // U) as r:
                for u in range(U):
                    n = U * r + u + 1
                    e = dve.value_load(expert_of[0:1, bass.ds(U * r + u, 1)], min_val=0, max_val=E1 - 1)
                    dve.wait_ge(s["o_up"], n + 2)
                    dve.tensor_tensor(o_h[u], scores_ps[:, u, 0, 0:P],
                                      o_b1[:, bass.ds(e, 1), :].rearrange("p e h -> p (e h)"), ALU.add)\
                       .then_inc(s["o_h_done"], 1)
                for u in range(U):
                    n = U * r + u + 1
                    dve.wait_ge(s["o_h_done"], n + 2)
                    ln_stats(7 * NT + n, u, o_h[u])
                for u in range(U):
                    n = U * r + u + 1
                    dve.wait_ge(s["o_hturned"], n)
                    ln_apply(7 * NT + n, u, o_hn[u], o_h[u])
                for u in range(U):
                    n = U * r + u + 1
                    e = dve.value_load(expert_of[0:1, bass.ds(U * r + u, 1)], min_val=0, max_val=E1 - 1)
                    dve.wait_ge(s["o_down"], n + 2)
                    dve.wait_ge(o_stored[u], 16 * r + 16)
                    dve.tensor_tensor(o_out[u], (heads_ps, desk_ps)[u][:, 0:P],
                                      o_b2[:, bass.ds(e, 1), :].rearrange("p e h -> p (e h)"), ALU.add)\
                       .then_inc(s["o_out_done"], 1)

            with dve.Fori(0, NT // U) as r:
                t = U * r
                n = NT + t + 1
                for u in range(U):
                    get_tables(n + u, t + u, u)
                for u in range(U):
                    dve.wait_ge(z_loaded[u], 8 * t + 16)
                    combine(n + u, u, 16 * NT + 16 * t + 32, z)
                for u in range(U):
                    dve.wait_ge(s["c2_done"], n + u + 2)
                    ln_stats(7 * NT + NJ + t + u + 1, u, z[u])
                for u in range(U):
                    dve.wait_ge(z_stored[u], 8 * t + 16)
                    ln_apply(7 * NT + NJ + t + u + 1, u, x_out[u], z[u])

        @block.gpsimd
        def _(pool):
            for k in pool_done:
                pool.sem_inc(s[k], CREDIT)
            pool.memset(minus_half[:], -0.5)
            pool.memset(ln_eps[:], EPS_LN)
            pool.memset(zeros_i[:], 0).then_inc(zero_sem, 1)
            pool.iota(token[:], [[P, NT]], base=0, channel_multiplier=1)
            for u in range(U):
                pool.memset(pad_T[u], 0.0)
                pool.memset(m_vbd[u], 0.0)
                pool.memset(v_bd[u], 0.0).then_inc(zeroed, 1)
            pool.wait_ge(zeroed, U)
            pool.wait_ge(loaded, 16 * len(w_loads))
            for u in range(U):
                vv = v_bd[u].rearrange("p (g b h c) -> p g b h c", g=8, b=NB, h=2)
                for par in range(2):
                    last = pool.memset(vv[S * par:S * par + S, :, :, par, HD:HD + 1], 1.0)
                mvv = m_vbd[u].rearrange("p (g b h c) -> p g b h c", g=4, b=NB, h=2)
                for par in range(2):
                    last = pool.memset(mvv[S * par:S * par + S, :, :, par, MD:MD + 1], 1.0)
            last.then_inc(zeroed, 1)
            for j in range(HOPS):
                pool.indirect_dma_start(out=hop_rows[:, j, :], out_offset=None, in_=T["L0_xattn_rpe"],
                                        in_offset=bass.IndirectOffsetOnAxis(ap=hop_at[:, j:j + 1], axis=0))\
                    .then_inc(hop_gathered, 16)

            def ln_rstd(o, u):
                pool.wait_ge(s["mv_done"], o + 2)
                pool.tensor_tensor(veps[u], mv[u][:, 1:2], ln_eps[:, 0:1], ALU.add).then_inc(s["veps_done"], 1)
                pool.wait_ge(s["veps_done"], o + 2)
                pool.tensor_tensor(rstd[u], veps[u], minus_half[:, 0:1], ALU.pow).then_inc(s["rstd_done"], 1)

            with pool.Fori(0, NT // U) as r:
                t = U * r
                for u in range(U):
                    pool.wait_ge(in_loaded[u], 8 * t + 16)
                    pool.wait_ge(desk_full, 4 * t + u + 1)
                    pool.wait_ge(s["y_done"], t + u + 1)
                    pool.tensor_tensor(x_res[u], x_in[u], a_row[:, 1, :], ALU.add).then_inc(s["x_res_done"], 1)
                for u in range(U):
                    ln_rstd(t + u + 1, u)

            base = BASE[3]
            with pool.Fori(0, NT // U) as r:
                t = U * r
                n = t + 1
                d = base["desk"] + 9 * t
                m = base["att"] + 2 * t
                ln = base["ln"] + 3 * t
                for u in range(U):
                    pool.wait_ge(desk_empty, d + 2 + u + 2)
                    pool.wait_ge(s["scores_done"], m + u + 1)
                    pool.tensor_tensor(k_bd[u][:, 0:MH * P].rearrange("p (h t) -> p h t", h=MH),
                                       c_T[u].unsqueeze(1).broadcast_to([P, MH, P]),
                                       const("head8q").unsqueeze(2).broadcast_to([P, MH, P]), ALU.mult)\
                        .then_inc(s["k_copied"], 1)
                for u in range(U):
                    pool.wait_ge(s["g_key_done"], n + u + 2)
                    pool.tensor_tensor(g_diag[u].rearrange("p (h t) -> p h t", t=S),
                                       g_key[u].unsqueeze(2).broadcast_to([P, MH, S]),
                                       const("diag64").unsqueeze(1).broadcast_to([P, MH, S]), ALU.mult)\
                        .then_inc(s["g_diag_done"], 1)
                for u in range(U):
                    pool.wait_ge(s["h_mid_done"], n + u + 2)
                    pool.tensor_tensor(h_sq[u], h_mid[u], h_mid[u], ALU.mult).then_inc(s["h_sq_done"], 1)
                for u in range(U):
                    nu = pool.to_reg(n + u + 2)
                    pool.wait_ge(w_ready, 1)
                    pool.wait_ge(s["h_var_done"], nu)
                    pool.tensor_scalar(h_veps[u], h_var[u], 1.0 / MD, EPS_LN, ALU.mult, ALU.add)\
                        .then_inc(s["h_veps_done"], 1)
                    pool.wait_ge(s["h_veps_done"], n + u + 2)
                    pool.tensor_tensor(h_rstd[u], h_veps[u], minus_half[:, 0:8], ALU.pow)\
                        .then_inc(s["h_rstd_done"], 1)
                for u in range(U):
                    by_head = h_mid[u].rearrange("p (h c) -> p h c", c=MD)
                    zv = z[u].rearrange("p (h c) -> p h c", c=MD)
                    pool.wait_ge(s["ln_done"], ln - 2 * U + u + 1 + U)
                    pool.wait_ge(s["h_rstd_done"], n + u + 2)
                    pool.tensor_tensor(zv, by_head, h_rstd[u].unsqueeze(2).broadcast_to([P, MH, MD]), ALU.mult)\
                        .then_inc(s["z1_done"], 1)
                    pool.wait_ge(s["z1_done"], n + u + 2)
                    pool.tensor_tensor(z[u], z[u], m_row[:, 0, :], ALU.mult).then_inc(s["z2_done"], 1)
                    pool.wait_ge(s["z2_done"], n + u + 2)
                    pool.tensor_tensor(z[u], z[u], m_row[:, 1, :], ALU.add).then_inc(s["z3_done"], 1)
                    pool.wait_ge(s["z3_done"], n + u + 2)
                    pool.tensor_tensor(z[u], z[u], x_in[u], ALU.add).then_inc(s["z_done"], 1)
                for u in range(U):
                    ln_rstd(ln + u + 1, u)
                for u in range(U):
                    ln_rstd(ln + U + u + 1, u)
                for u in range(U):
                    pool.wait_ge(s["rope_done"], n + u + 2)
                    pool.tensor_tensor(q_T[u], rope_c[u][:, 0:P], rope_s[u][:, 0:P], ALU.add)\
                        .then_inc(s["q_copied"], 1)
                    pool.tensor_tensor(rope_k[u], rope_c[u][:, P:2 * P], rope_s[u][:, P:2 * P], ALU.add)\
                        .then_inc(s["rope_k_done"], 1)
                for u in range(U):
                    pool.wait_ge(s["y_done"], base["out"] + n + u + 2)
                    pool.wait_ge(xn_stored[u], 16 * t + 32)
                    pool.tensor_tensor(r4[u], y[u], x2[u], ALU.add).then_inc(s["r4_done"], 1)
                for u in range(U):
                    ln_rstd(ln + 2 * U + u + 1, u)

            def put(n0):
                table, n_slots = (token_of0, NSLOT0) if n0 == 0 else (token_of1, NSLOT1)
                with pool.Fori(0, NT // U) as r:
                    for u in range(U):
                        pool.wait_ge(s["put_free"], n0 + U * r + u + 1)
                        pool.tensor_copy(put_at[u], slot_put[:, :, bass.ds(U * r + u, 1)].rearrange("p k t -> p (k t)"))
                        pool.tensor_copy(put_tok[u], token[:, bass.ds(U * r + u, 1)]).then_inc(s["put_ready"], 1)
                        nu = pool.to_reg(n0 + U * r + u + 3)
                        pool.wait_ge(table_sem, 32)
                        pool.wait_ge(s["put_ready"], nu)
                        for k in range(2):
                            pool.indirect_dma_start(
                                out=table, out_offset=bass.IndirectOffsetOnAxis(ap=put_at[u][:, k:k + 1], axis=0),
                                in_=put_tok[u], in_offset=None, bounds_check=n_slots - 1, oob_is_err=False)\
                                .then_inc(put_done[u], 16)

            for u in range(U):
                pool.wait_ge(xn_stored[u], 32 * (NT // U) + 32)
            pool.wait_ge(routed, 1)
            put(0)

            def load_expert(r, w):
                pool.wait_ge(s["expert_done"], 2 * r + w + 1)
                e = 2 * r + w
                for dst, src in (
                    (e_w1[w][:], T["L0_ffn_W1"][bass.ds(e, 1)].rearrange("e c f -> c (e f)")),
                    (e_w2[w][:], T["L0_ffn_W2"][bass.ds(e, 1)].rearrange("e (f p) d -> p (e f) d", p=P)),
                    (e_b1[w][:], T["L0_ffn_b1"][bass.ds(e, 1)].rearrange("e (f p) -> p (e f)", p=P)),
                    (e_b2[w][:], T["L0_ffn_b2"][bass.ds(e, 1)].rearrange("e d -> (e d)").partition_broadcast(P)),
                ):
                    pool.dma_start(dst, src, allow_slow_non_contiguous=True).then_inc(e_loaded[w], 16)

            pool.wait_ge(at_loaded, 16)
            with pool.Fori(0, E0 // 2) as r:
                for i in range(2 * GE):
                    u, q = i % 2, 2 * GE * r + i
                    if i % GE == 0:
                        load_expert(r, i // GE)
                    pool.wait_ge(s["e_turned"], q + 1)
                    pool.tensor_copy(e_at[u], at0_all[:, bass.ds(q, 1), :].rearrange("p q j -> p (q j)"))\
                        .then_inc(s["at_done"], 1)
                    nq = pool.to_reg(q + 3)
                    pool.wait_ge(routed, 1)
                    pool.wait_ge(s["at_done"], nq)
                    for j in range(J):
                        pool.indirect_dma_start(out=e_in[u][:, P * j:P * j + P], out_offset=None, in_=xn_dram,
                                                in_offset=bass.IndirectOffsetOnAxis(ap=e_at[u][:, j:j + 1], axis=0))\
                            .then_inc(e_in_loaded[u], 16)

            def get(n, u, rows):
                nu = pool.to_reg(n + 2)
                pool.wait_ge(routed, 1)
                pool.wait_ge(s["got_ready"], nu)
                for k in range(2):
                    pool.indirect_dma_start(out=got[u][:, D * k:D * k + D], out_offset=None, in_=rows,
                                            in_offset=bass.IndirectOffsetOnAxis(ap=got_at[u][:, k:k + 1], axis=0))\
                        .then_inc(got_loaded[u], 16)

            for u in range(U):
                pool.wait_ge(e_stored[u], 16 * GE * E0 // 2 + 16)
            base = BASE[5]
            with pool.Fori(0, NT // U) as r:
                t = U * r
                n = t + 1
                ln = base["ln"] + 3 * t
                m = base["att"] + 2 * t
                for u in range(U):
                    get(n + u, u, moe0)
                for u in range(U):
                    ln_rstd(ln + u + 1, u)
                for u in range(U):
                    pool.wait_ge(s["rope_done"], NT + n + u + 2)
                    pool.tensor_tensor(q_T[u], rope_c[u][:, 0:P], rope_s[u][:, 0:P], ALU.add)\
                        .then_inc(s["q_copied"], 1)
                    pool.tensor_tensor(rope_k[u], rope_c[u][:, P:2 * P], rope_s[u][:, P:2 * P], ALU.add)\
                        .then_inc(s["rope_k_done"], 1)
                for u in range(U):
                    pool.wait_ge(c_loaded[u], 32 * NT + 24 * t + 48)
                    pool.wait_ge(s["biased"], n + u)
                    pool.tensor_tensor(fm[u], fm_in[u][:, 0:S], fm_in[u][:, S:2 * S], ALU.add)\
                        .then_inc(s["fm_done"], 1)
                for u in range(U):
                    ln_rstd(ln + U + u + 1, u)
                for u in range(U):
                    pool.wait_ge(s["ln_done"], ln + U + u + 3)
                    pool.wait_ge(s["y_done"], base["out"] + 2 * t + u + 1)
                    pool.tensor_tensor(x5b[u], x5[u], c_row[:, 1, :], ALU.add).then_inc(s["x5b_done"], 1)
                for u in range(U):
                    ln_rstd(ln + 2 * U + u + 1, u)

            pool.wait_ge(routed, 2)
            put(NT)
            for u in range(U):
                pool.wait_ge(x6_stored[u], 16 * (NT // U) + 16)
            pool.wait_ge(at_loaded, 32)
            with pool.Fori(0, NJ // U) as r:
                for u in range(U):
                    pool.wait_ge(s["o_turned"], U * r + u + 1)
                    pool.tensor_copy(o_at[u], at1_all[:, bass.ds(U * r + u, 1)]).then_inc(s["at_done"], 1)
                    nq = pool.to_reg(NSLOT0 // GS + U * r + u + 3)
                    pool.wait_ge(routed, 2)
                    pool.wait_ge(s["at_done"], nq)
                    pool.indirect_dma_start(out=o_in[u], out_offset=None, in_=x6_dram,
                                            in_offset=bass.IndirectOffsetOnAxis(ap=o_at[u], axis=0))\
                        .then_inc(o_in_loaded[u], 16)
                for u in range(U):
                    ln_rstd(7 * NT + U * r + u + 1, u)
            for u in range(U):
                pool.wait_ge(o_stored[u], 16 * (NJ // U) + 16)
            with pool.Fori(0, NT // U) as r:
                t = U * r
                for u in range(U):
                    get(NT + t + u + 1, u, moe1)
                for u in range(U):
                    ln_rstd(7 * NT + NJ + t + u + 1, u)


def launch_args(nc, inputs):
    cf, cb = constants(inputs["x"].shape[0] * S)
    arrays, T = {}, {}
    given = dict(inputs)
    given["consts"] = np.concatenate(list(cf.values()), axis=1)
    given["consts16"] = np.concatenate(list(cb.values()), axis=1).astype(np.float32)
    for name, a in given.items():
        a = np.ascontiguousarray(a)
        arrays[f"in_{name}"] = a
        T[name] = nc.dram_tensor(f"in_{name}", a.shape, mybir.dt.from_np(a.dtype), kind="ExternalInput").ap()
    return arrays, T


def kernel(**inputs):
    import concourse.bacc as bacc
    from concourse.bass_utils import run_bass_kernel_spmd

    nc = bacc.Bacc("TRN2", target_bir_lowering=False, num_devices=1)
    arrays, T = launch_args(nc, inputs)
    out = nc.dram_tensor("out_0", inputs["x"].shape, F32, kind="ExternalOutput").ap()
    build(nc, T, out)
    return run_bass_kernel_spmd(nc, [arrays], core_ids=[0]).results[0]["out_0"]
```

```python
from contextlib import ExitStack

import numpy as np
import concourse.bass as bass
from concourse import mybir

F32 = mybir.dt.float32
BF16 = mybir.dt.bfloat16
I32 = mybir.dt.int32
U32 = mybir.dt.uint32
ACT = mybir.ActivationFunctionType
ALU = mybir.AluOpType
AX = mybir.AxisListType.X

P = 128
S = 64
D = 128
NB = P // S
H = 16
HD = D // H
MH = 8
MD = D // MH
NR = 2
V = 4
U = 2
CREDIT = 2
E0, F0 = 8, 4
E1 = 16
BELOW = 64.0
FAR = 2.0 ** 20
EPS_LN = 1e-5
NEG = -1e30
SCALE = HD ** -0.5


def capacity(n_tokens):
    return -(-2 * n_tokens // E0)


def slot_tiles(n_tokens):
    return 2 * n_tokens // P + E1


def constants(n_tokens):
    p = np.arange(P)
    same = (p[:, None] // S) == (p[None, :] // S)
    t = np.arange(S)
    half = HD // 2
    inv_freq = (1.0 / np.float32(10000.0) ** (np.arange(half, dtype=np.float32) / half)).astype(np.float32)
    ang = (p % S).astype(np.float32)[None, :] * inv_freq[p % half][:, None]
    f = {
        "ident": np.eye(P),
        "tri2": same & (p[:, None] <= p[None, :]),
        "ones2": same,
        "diag64": (p[:, None] % S) == t[None, :],
        "head16": p[:, None] // HD == np.arange(H)[None, :],
        "head8": p[:, None] // MD == np.arange(MH)[None, :],
        "head4": (p[:, None] % 64) // MD == np.arange(64 // MD)[None, :],
        "cos": np.cos(ang.astype(np.float64)),
        "sin": np.sin(ang.astype(np.float64)),
    }
    f["head8q"] = f["head8"] * MD ** -0.5
    b = {"tri16": p[:, None] <= p[None, :], "ones16": np.ones((P, P)), "ident16": np.eye(P), "causal16": np.where(t[None, :] <= (p % S)[:, None], 0.0, NEG)}
    f["expert"] = np.tile(np.arange(E1) - BELOW, (P, 1))
    f["region0"] = np.tile(np.arange(E0) * capacity(n_tokens), (P, 1))
    n = slot_tiles(n_tokens)
    f["tile_start"] = np.tile(np.arange(n) * P, (P, 1))
    return ({k: v.astype(np.float32) for k, v in f.items()}, b)


def offsets(pieces):
    at, out = 0, {}
    for name, a in pieces.items():
        out[name] = (at, a.shape[1])
        at += a.shape[1]
    return out, at


def build(nc, T, out):
    B = T["x"].shape[0]
    NT = B * S // P
    cf, cb = constants(B * S)
    cf_at, cf_n = offsets(cf)
    cb_at, cb_n = offsets(cb)

    with ExitStack() as ctx:
        def sb(name, shape, dt=F32):
            return ctx.enter_context(nc.sbuf_tensor(name, shape, dt))

        def ps(name, shape, dt=F32):
            return ctx.enter_context(nc.psum_tensor(name, shape, dt))

        def sem(name):
            return ctx.enter_context(nc.semaphore(name))

        def dram(name, shape, dt=F32):
            return nc.dram_tensor(name, shape, dt, kind="Internal").ap()

        consts = sb("consts", [P, cf_n])
        consts16 = sb("consts16", [P, cb_n], BF16)

        def const(name):
            at, n = cf_at[name]
            return consts[:, at:at + n]

        def const16(name):
            at, n = cb_at[name]
            return consts16[:, at:at + n]

        ident, ident16, causal16 = const("ident"), const16("ident16"), const16("causal16")

        scores_ps = ps("scores_ps", [P, U, NR, 512])
        turned_ps = ps("turned_ps", [P, 2, 512])
        heads_ps = ps("heads_ps", [P, 512])
        desk_ps = ps("desk_ps", [P, 512])
        trans_ps = desk_ps[:, 0:P]
        setup_ps = scores_ps[:].rearrange("p u g (k n) -> p (u g k) n", n=P)

        whole = {}

        def both(name, n, dt=F32):
            b = whole[name] = sb(name, [P, U, n], dt)
            return [b[:, u, :] for u in range(U)]

        x_in, x_out, x_res = both("x_in", D), both("x_out", D), both("x_res", D)
        x_T, q_T, o_T, ctx_o, y = both("x_T", P), both("q_T", P), both("o_T", P), both("ctx_o", D), both("y", D)
        turned, probs = both("turned", H * S), both("probs", H * S)
        k_bd, v_bd = both("k_bd", H * P), both("v_bd", 8 * NB * 2 * (HD + 1))
        row_max, recip = both("row_max", H), both("recip", H)
        pad_T = both("pad_T", NB * (S + 2))
        stat, mv, veps, rstd = both("stat", 6), both("mv", 2), both("veps", 1), both("rstd", 1)
        minus_half = sb("minus_half", [P, 16])

        w_raw = sb("w_raw", [P, 7, P])
        a_w = sb("a_w", [P, 7, P])
        a_col = sb("a_col", [P, 3])
        a_row = sb("a_row", [P, 2, D])

        HOPS = S // 2
        hop_at = sb("hop_at", [P, HOPS], I32)
        assert HOPS == 2 * E1
        hop_rows = sb("hop_rows", [P, HOPS, D])
        hop_T = sb("hop_T", [P, HOPS, P])
        o_w1, o_w2 = hop_rows[:, 0:E1, :], hop_rows[:, E1:2 * E1, :]
        o_b1, o_b2 = hop_T[:, 0:E1, :], hop_T[:, E1:2 * E1, :]
        GS = min(512, capacity(B * S))
        NJ = slot_tiles(B * S)
        pool_n = max(NJ * E1, 6 * V * P)
        shared = sb("shared", [P, max(U * F0 * GS, pool_n, U * (2 * P + 12 * S))])

        def views(at, n):
            return [shared[:, at + n * u:at + n * u + n] for u in range(U)]
        hx_in, hx_T, hop_bd, hop_out = (views(U * at, n) for at, n in (
            (0, D), (D, P), (D + P, 4 * S), (D + P + 4 * S, MH * S)))
        g_raw, g_w = sb("gate_raw", [2 * MH, 3, D]), sb("gate_w", [P, 3, 2 * MH])
        g_row = sb("gate_bias", [P, 2 * MH])
        m_row = sb("mlstm_ln", [P, 2, D])
        c_in, c_two, hop_in = both("c_in", D), both("c_two", NB * D), both("hop_in", MH * S)
        c_T = both("c_T", P)
        gates, neg_abs, exp_abs, soft = both("gates", 16), both("neg_abs", 8), both("exp_abs", 8), both("soft", 8)
        log_f, csum, g_key = both("log_f", 8), both("csum", 8), both("g_key", 8)
        g_diag, decay = both("g_diag", MH * S), both("decay", MH * S)
        cmax, floor, denom, denom2, denom3 = (both(k, 8) for k in ("cmax", "floor", "denom", "denom2", "denom3"))
        m_vbd = both("m_vbd", 4 * NB * 2 * (MD + 1))
        h_sum, h_mid, h_sq, h_var = both("h_sum", 8), both("h_mid", D), both("h_sq", D), both("h_var", 8)
        h_veps, h_rstd, z = both("h_veps", 8), both("h_rstd", 8), both("z", D)
        xb = both("xb", D)
        f_raw = sb("ffn_qkv_raw", [P, 3 * D])
        f_w = sb("ffn_attn_w", [P, 6, D])
        f_col = sb("ffn_ln", [P, 4])
        f_gate = sb("ffn_gate", [P, 8])
        x2, xn, r4 = both("x2", D), both("xn", D), both("r4", D)
        h_T = both("h_T", P)
        rope_c, rope_s, rope_k = both("rope_c", 2 * P), both("rope_s", 2 * P), both("rope_k", P)
        logits0 = sb("logits0", [P, NT, 8])

        NSLOT0 = E0 * capacity(B * S)
        NSLOT1 = NJ * P
        assert NT * E1 <= H * S
        r_gate, r_tmp, r_pos = (sb(k, [P, NT, E1]) for k in ("r_gate", "r_tmp", "r_pos"))
        r_scan, r_scan2, r_one, r_two = (a[:, 0:NT * E1].rearrange("p (t e) -> p t e", e=E1) for a in turned + probs)
        r_mask = sb("r_mask", [P, NT * E1], BF16)
        r_a, r_b = sb("r_a", [P, NT]), sb("r_b", [P, NT])
        r_cnt, r_cnt2, r_end, r_base = (sb(k, [P, E1]) for k in ("r_cnt", "r_cnt2", "r_end", "r_base"))
        r_int = sb("r_int", [P, E1], I32)
        r_le, r_ej = shared[:, 0:NJ * E1].rearrange("p (j e) -> p j e", e=E1), sb("r_ej", [P, NJ])
        assert NJ % V == 0
        expert_of = sb("expert_of", [P, NJ], I32)
        slot_f, weight = sb("slot_f", [P, 2, NT]), sb("weight", [P, 2, NT])
        slot_put, slot_get = sb("slot_put", [P, 2, NT], U32), sb("slot_get", [P, 2, NT + U], U32)
        r_slot, r_low = sb("r_slot", [P, 2, NT], I32), sb("r_low", [P, 2, NT], I32)
        token = sb("token", [P, NT], I32)
        put_at, put_tok = both("put_at", 2, U32), both("put_tok", 1, I32)
        zeros_i = sb("zeros_i", [P, NSLOT1 // P if NSLOT1 > NSLOT0 else NSLOT0 // P], I32)
        CAP = capacity(B * S)
        GE, J = CAP // GS, GS // P
        assert CAP % GS == 0 and GS % P == 0 and (GE == 1 or GE % 2 == 0)
        e_w1 = [sb(f"e_w1{w}", [P, F0 * P]) for w in range(2)]
        e_w2 = [sb(f"e_w2{w}", [P, F0, D]) for w in range(2)]
        e_b1 = [sb(f"e_b1{w}", [P, F0]) for w in range(2)]
        e_b2 = [sb(f"e_b2{w}", [P, D]) for w in range(2)]
        at0_all, at1_all = sb("at0_all", [P, NSLOT0 // GS, J], I32), sb("at1_all", [P, NJ + V], I32)
        e_at, e_in, e_T, e_out = both("e_at", J, I32), both("e_in", GS), both("e_T", GS), both("e_out", GS)
        e_mid = [a.rearrange("p (f n) -> p f n", f=F0) for a in views(0, F0 * GS)]
        l_raw = sb("l_raw", [P, 2 * 32])
        l_w = sb("l_w", [P, 6, D])
        c_w = sb("c_w", [P, 4, D])
        c_col, c_row = sb("c_col", [P, 3]), sb("c_row", [P, 2, D])
        rt_w, rt_row = sb("rt_w", [P, E1]), sb("rt_row", [P, E1])
        got, got_at, got_w = both("got", 2 * D), both("got_at", 2, U32), both("got_w", 2)
        fm_in, fm = both("fm_in", 2 * S), both("fm", S)
        x4, x5, x5b, x6 = both("x4", D), both("x5", D), both("x5b", D), both("x6", D)
        logits1 = sb("logits1", [P, NT, E1])
        o_g, o_b = sb("o_g", [P, E1]), sb("o_b", [P, E1])
        o_at = both("o_at", 2, I32)
        o_in, o_in_T, o_h, o_hn, o_g_T, o_out = (views(U * 2 * P * k, 2 * P) for k in range(6))
        o_stat, o_mv, o_veps, o_rstd = both("o_stat", 12), both("o_mv", 4), both("o_veps", 2), both("o_rstd", 2)

        loaded, w_turned, w_ready = sem("loaded"), sem("weights_turned"), sem("weights_ready")
        w_copied = sem("weights_copied")
        zeroed = sem("constants_set")
        dve_done = ["veps_done", "k_copied", "max_done", "shifted", "recip_done", "normed",  "y_done",
                    "stat_done", "mv_done", "ln_done"]
        act_done = ["q_copied", "exp_done", "turn0_copied", "turn1_copied"]
        pe_done = ["qk_done", "scores_done", "turn0_done", "turn1_done", "pv_done", "conv_done",
                   "out_done"]
        pool_done = ["x_res_done", "rstd_done"]
        s = {k: sem(k) for k in dve_done + act_done + pe_done + pool_done}
        desk_full, desk_empty = sem("desk_full"), sem("desk_empty")
        in_loaded = [sem(f"x_in_loaded{u}") for u in range(U)]
        x_stored = [sem(f"x_out_stored{u}") for u in range(U)]

        hop_idx, hop_gathered = sem("hop_index_loaded"), sem("hop_rows_gathered")
        hop_turned, hop_copied = sem("hop_turned"), sem("hop_copied")
        hx_loaded = [sem(f"hx_loaded{u}") for u in range(U)]
        hop_stored = [sem(f"hop_stored{u}") for u in range(U)]
        c_loaded = [sem(f"c_loaded{u}") for u in range(U)]
        xn_stored = [sem(f"xn_stored{u}") for u in range(U)]
        route_shifted, route_exp = sem("route_shifted"), sem("route_exp")
        route_masked, route_counted, route_chain = sem("route_masked"), sem("route_counted"), sem("route_chain")
        counts_read = sem("route_counts_read")
        zero_sem, table_sem, routed = sem("zeros_set"), sem("tables_cleared"), sem("routed")
        put_done = [sem(f"put_done{u}") for u in range(U)]
        e_loaded = [sem(f"e_weights_loaded{w}") for w in range(2)]
        e_in_loaded = [sem(f"e_in_loaded{u}") for u in range(U)]
        at_loaded = sem("slot_tables_loaded")
        e_stored = [sem(f"e_out_stored{u}") for u in range(U)]
        gelu_done, up_done = sem("gelu_done"), sem("up_done")
        got_loaded, x6_stored = ([sem(f"{k}{u}") for u in range(U)] for k in ("got_loaded", "x6_stored"))
        late = sem("late_weights_loaded")
        o_in_loaded, o_stored = ([sem(f"{k}{u}") for u in range(U)] for k in ("o_in_loaded", "o_stored"))
        z_loaded, z_stored = ([sem(f"{k}{u}") for u in range(U)] for k in ("z_loaded", "z_stored"))
        dve2 = ["o_stat_done", "o_mv_done", "o_veps_done", "weights_got", "h_sq_done", "h_veps_done", "z1_done", "z2_done", "z_done", "e_out_done", "expert_done", "c1_done", "c2_done", "biased",
                "o_h_done", "o_hn_done", "o_out_done",
                "hb_done", "hop_out1", "gates_done", "neg_abs_done", "log_f_done", "g_key_done", "cmax_done",
                "denom_done", "denom2_done", "denom3_done", "h_sum_done", "h_mid_done", "h_var_done", "rope_done", "x3_done"]
        act2 = ["e_T_done", "o_T_done", "o_g_done", "hop_out0", "m_v_done", "exp_abs_done", "soft_done", "decay_done", "floor_done"]
        pe2 = ["e_turned", "down_done", "o_turned", "o_up", "o_hturned", "o_down", "hop_done"]
        pool2 = ["o_rstd_done", "got_ready", "put_ready", "at_done", "fm_done", "x5b_done", "g_diag_done", "h_rstd_done", "xb_done", "rope_k_done", "r4_done"]
        s["put_free"] = sem("put_free")
        s |= {k: sem(k) for k in dve2 + act2 + pe2 + pool2}
        dve_done, act_done, pe_done, pool_done = dve_done + dve2, act_done + act2, pe_done + pe2, pool_done + pool2

        by_half = {"k_copied", "scores_done", "max_done", "shifted", "exp_done", "biased"}

        USES = {1: 7, 3: 13, 5: 17}
        HOP_DESK = USES[1] * NT // U
        BASE = {1: dict(att=0, q=0, k=0, qk=0, out=0, ln=0, desk=0),
                3: dict(att=2 * NT, q=2 * NT, k=NT, qk=NT, out=NT, ln=NT, desk=HOP_DESK + S),
                5: dict(att=4 * NT, q=3 * NT, k=3 * NT, qk=2 * NT, out=2 * NT, ln=4 * NT,
                        desk=HOP_DESK + S + USES[3] * NT // U)}
        hop_dram = dram("hop_dram", [B * S, MH * S])
        xn_dram, r4_dram = dram("xn_dram", [B * S, D]), dram("r4_dram", [B * S, D])
        x6_dram = dram("x6_dram", [B * S, D])
        token_of0, token_of1 = dram("token_of0", [NSLOT0, 1], I32), dram("token_of1", [NSLOT1, 1], I32)
        moe0, moe1 = dram("moe0", [NSLOT0, D]), dram("moe1", [NSLOT1, D])
        c_flat = T["ctx_1024"].rearrange("b s d -> (b s) d")

        x1 = dram("x1", [B * S, D])
        x0 = T["x"].rearrange("b s d -> (b s) d")
        w_loads = [
            (consts[:], T["consts"]), (shared[:, 0:cb_n], T["consts16"]),
            (w_raw[:, 0:3, :], T["L0_attn_Wqkv_w"].rearrange("(k o) c -> o k c", k=3)),
            (w_raw[:, 3:6, :].rearrange("p a b -> p (a b)"), T["L0_attn_conv_w"].rearrange("o i k -> o (i k)")),
            (w_raw[:, 6, :], T["L0_attn_out_w"]),
            (a_col[:, 0:2], T["L0_attn_Wqkv_b"][0:2 * D].rearrange("(k o) -> o k", k=2)),
            (a_col[:, 2:3], T["L0_attn_conv_b"].rearrange("(o k) -> o k", k=1)),
            (a_row[:, 0, :], T["L0_attn_Wqkv_b"][2 * D:3 * D].partition_broadcast(P)),
            (a_row[:, 1, :], T["L0_attn_out_b"].partition_broadcast(P)),
        ]

        def column(name):
            return T[name].rearrange("(o k) -> o k", k=1)

        w_loads += [
            (hop_at[:], T["itok_SxS2_0_2016"].rearrange("(j v) m -> (v m) j", v=2)),
            (g_raw[0:MH].rearrange("p k c -> p (k c)"), T["L0_xattn_igate_w"]),
            (g_raw[MH:2 * MH].rearrange("p k c -> p (k c)"), T["L0_xattn_fgate_w"]),
            (g_row[:, 0:MH], T["L0_xattn_igate_b"].partition_broadcast(P)),
            (g_row[:, MH:2 * MH], T["L0_xattn_fgate_b"].partition_broadcast(P)),
            (m_row[:, 0, :], T["L0_xattn_ln_w"].partition_broadcast(P)),
            (m_row[:, 1, :], T["L0_xattn_ln_b"].partition_broadcast(P)),
            (f_raw[:], T["L0_ffn_Wqkv"]), (f_w[:, 5, :], T["L0_ffn_Wproj"]), (f_gate[:], T["L0_ffn_Wgate"]),
            (f_col[:, 0:1], column("L0_ffn_ln1_g")), (f_col[:, 1:2], column("L0_ffn_ln1_b")),
            (f_col[:, 2:3], column("L0_ffn_ln2_g")), (f_col[:, 3:4], column("L0_ffn_ln2_b")),
        ]

        late_loads = [
            (l_w[:, 0, :], T["L1_attn_wq"]), (l_raw[:, 0:32], T["L1_attn_wk"]), (l_raw[:, 32:64], T["L1_attn_wv"]),
            (l_w[:, 5, :], T["L1_attn_wo"]),
            (c_w[:, 0, :], T["L1_xattn_Wq"]), (c_w[:, 1, :], T["L1_xattn_Wk"]), (c_w[:, 2, :], T["L1_xattn_Wv"]),
            (c_w[:, 3, :], T["L1_xattn_Wo"]), (c_col[:, 0:1], column("L1_xattn_bq")),
            (c_col[:, 1:2], column("L1_xattn_bk")),
            (c_row[:, 0, :], T["L1_xattn_bv"].partition_broadcast(P)),
            (c_row[:, 1, :], T["L1_xattn_bo"].partition_broadcast(P)),
            (rt_w[:], T["L1_ffn_Wr"]), (rt_row[:], T["L1_ffn_br"].partition_broadcast(P)),
            (o_w1, T["L1_ffn_W1"].rearrange("e c h -> c e h")),
            (o_w2, T["L1_ffn_W2"].rearrange("e c h -> c e h")),
            (o_b1.rearrange("p e h -> p (e h)"), T["L1_ffn_b1"].rearrange("e h -> (e h)").partition_broadcast(P)),
            (o_b2.rearrange("p e h -> p (e h)"), T["L1_ffn_b2"].rearrange("e h -> (e h)").partition_broadcast(P)),
            (o_g[:], T["L1_ffn_g1"].rearrange("e h -> h e")), (o_b[:], T["L1_ffn_be1"].rearrange("e h -> h e")),
        ]

        def tile_rows(a, n):
            return a[bass.ds(n * P, P), :]

        W_READY = 5
        SPARE, LONG = 4, 4
        block = ctx.enter_context(nc.Block())

        @block.sync
        def _(sp):
            for u in range(U):
                sp.sem_inc(x_stored[u], 16)
            for dst, src in w_loads:
                sp.dma_start(dst, src, allow_slow_non_contiguous=True).then_inc(loaded, 16)

            def load1(t, u):
                sp.wait_ge(s["x_res_done"], t + u + 1)
                sp.dma_start(x_in[u], tile_rows(x0, t + u)).then_inc(in_loaded[u], 16)

            def store1(t, u):
                sp.wait_ge(s["ln_done"], t + u + 1 + 2)
                sp.dma_start(tile_rows(x1, t + u), x_out[u]).then_inc(x_stored[u], 16)

            for u in range(U):
                load1(0, u)
            sp.wait_ge(zero_sem, 1)
            sp.dma_start(token_of0.rearrange("(p n) x -> p (n x)", p=P), zeros_i[:, 0:NSLOT0 // P])\
              .then_inc(table_sem, 16)
            sp.dma_start(token_of1.rearrange("(p n) x -> p (n x)", p=P), zeros_i[:, 0:NSLOT1 // P])\
              .then_inc(table_sem, 16)
            with sp.Fori(0, NT // U - 1) as r:
                t = U * r
                for u in range(U):
                    load1(t + U, u)
                for u in range(U):
                    store1(t, u)
            for u in range(U):
                store1(NT - U, u)
            for u in range(U):
                sp.wait_ge(x_stored[u], 16 * (NT // U) + 16)

            x1_rows = x1.rearrange("(b v) d -> b v d", v=S)
            hop_rows_dram = hop_dram.rearrange("(b v) k -> b v k", v=S)

            def load2(v, u):
                sp.wait_ge(desk_full, HOP_DESK + v + u - 1)
                sp.dma_start(hx_in[u][0:B], x1_rows[:, bass.ds(v + u, 1), :].rearrange("b v d -> b (v d)"))\
                  .then_inc(hx_loaded[u], 16)

            def store2(v, u):
                sp.wait_ge(s["hop_out0"], v + u + 3)
                sp.wait_ge(s["hop_out1"], v + u + 3)
                sp.dma_start(hop_rows_dram[:, bass.ds(v + u, 1), :].rearrange("b v k -> b (v k)"),
                             hop_out[u][0:B]).then_inc(hop_stored[u], 16)

            for u in range(U):
                sp.sem_inc(hop_stored[u], 16)
                load2(0, u)
            with sp.Fori(0, S // U - 1) as r:
                for u in range(U):
                    load2(U * r + U, u)
                for u in range(U):
                    store2(U * r, u)
            for u in range(U):
                store2(S - U, u)
            for u in range(U):
                sp.wait_ge(hop_stored[u], 16 * (S // U) + 16)

            def load3(t, u):
                sp.wait_ge(s["z_done"], t + u + 1)
                sp.dma_start(x_in[u], tile_rows(x1, t + u)).then_inc(in_loaded[u], 16)
                sp.dma_start(c_in[u], tile_rows(c_flat, t + u)).then_inc(c_loaded[u], 16)
                two = c_flat[bass.ds((t + u) * P, P), :].rearrange("(b t) d -> t b d", b=NB)
                for par in range(2):
                    sp.dma_start(c_two[u][S * par:S * par + S].rearrange("p (b d) -> p b d", b=NB), two)\
                      .then_inc(c_loaded[u], 16)
                sp.dma_start(hop_in[u], tile_rows(hop_dram, t + u)).then_inc(c_loaded[u], 16)

            def store3(t, u):
                sp.wait_ge(s["ln_done"], NT + 3 * t + 2 * U + u + 3)
                sp.dma_start(tile_rows(xn_dram, t + u), xn[u]).then_inc(xn_stored[u], 16)
                sp.wait_ge(s["r4_done"], t + u + 3)
                sp.dma_start(tile_rows(r4_dram, t + u), r4[u]).then_inc(xn_stored[u], 16)

            per = 32
            for u in range(U):
                sp.sem_inc(xn_stored[u], per)
                load3(0, u)
            for dst, src in late_loads:
                sp.dma_start(dst, src, allow_slow_non_contiguous=True).then_inc(late, 16)
            with sp.Fori(0, NT // U - 1) as r:
                for u in range(U):
                    load3(U * r + U, u)
                for u in range(U):
                    store3(U * r, u)
            for u in range(U):
                store3(NT - U, u)
            for u in range(U):
                sp.wait_ge(xn_stored[u], per * (NT // U) + per)

            def watch_puts(n0):
                with sp.Fori(0, NT // U) as r:
                    for u in range(U):
                        sp.wait_ge(put_done[u], 16 * n0 + 32 * r + 32)
                        sp.sem_inc(s["put_free"], 1)

            for u in range(U):
                sp.sem_inc(e_stored[u], 16)
            sp.sem_inc(s["put_free"], CREDIT)
            watch_puts(0)
            sp.dma_start(at0_all[:], token_of0.rearrange("(q p j) x -> p q (j x)", p=P, j=J),
                         allow_slow_non_contiguous=True).then_inc(at_loaded, 16)
            out0 = moe0.rearrange("(q p j) d -> q p (j d)", p=P, j=J)

            with sp.Fori(0, E0 // 2) as r:
                for i in range(2 * GE):
                    if i >= 2:
                        sp.wait_ge(s["e_out_done"], 2 * GE * r + i - 2 + 3)
                        sp.dma_start(out0[bass.ds(2 * GE * r + i - 2, 1)].rearrange("q p n -> p (q n)"),
                                     e_out[i % 2]).then_inc(e_stored[i % 2], 16)
                for i in range(2 * GE - 2, 2 * GE):
                    sp.wait_ge(s["e_out_done"], 2 * GE * r + i + 3)
                    sp.dma_start(out0[bass.ds(2 * GE * r + i, 1)].rearrange("q p n -> p (q n)"),
                                 e_out[i % 2]).then_inc(e_stored[i % 2], 16)

            for u in range(U):
                sp.wait_ge(e_stored[u], 16 * GE * E0 // 2 + 16)

            for u in range(U):
                sp.sem_inc(x6_stored[u], 16)
            fs_flat = T["fside_BxSxS2_0"].rearrange("b s t -> (b s) t")
            mask_flat = T["mask_BxSxS2_ff0"].rearrange("b s t -> (b s) t")

            def load5(t, u):
                sp.wait_ge(s["x5b_done"], t + u + 1)
                sp.wait_ge(s["c2_done"], t + u + 1)
                sp.wait_ge(s["fm_done"], t + u + 1)
                sp.dma_start(x_in[u], tile_rows(r4_dram, t + u)).then_inc(in_loaded[u], 16)
                sp.dma_start(c_in[u], tile_rows(c_flat, t + u)).then_inc(c_loaded[u], 16)
                sp.dma_start(fm_in[u][:, 0:S], tile_rows(fs_flat, t + u)).then_inc(c_loaded[u], 16)
                sp.dma_start(fm_in[u][:, S:2 * S], tile_rows(mask_flat, t + u)).then_inc(c_loaded[u], 16)

            def store5(t, u):
                sp.wait_ge(s["ln_done"], BASE[5]["ln"] + 3 * t + 2 * U + u + 3)
                sp.dma_start(tile_rows(x6_dram, t + u), x6[u])\
                  .then_inc(x6_stored[u], 16)

            for u in range(U):
                load5(0, u)
            with sp.Fori(0, NT // U - 1) as r:
                for u in range(U):
                    load5(U * r + U, u)
                for u in range(U):
                    store5(U * r, u)
            for u in range(U):
                store5(NT - U, u)
            for u in range(U):
                sp.wait_ge(x6_stored[u], 16 * (NT // U) + 16)

            for u in range(U):
                sp.sem_inc(o_stored[u], 16)
                sp.sem_inc(z_stored[u], 16)
            watch_puts(NT)
            sp.dma_start(at1_all[:, 0:NJ], token_of1.rearrange("(p q) x -> p (q x)", p=P)).then_inc(at_loaded, 16)

            def store6(r, w):
                sp.wait_ge(s["o_out_done"], U * r + w + 3)
                sp.dma_start(moe1[bass.ds((V * r + 2 * w) * P, 2 * P), :].rearrange("(i p) d -> p i d", p=P),
                             o_out[w].rearrange("p (i d) -> p i d", i=2)).then_inc(o_stored[w], 16)

            with sp.Fori(0, NJ // V) as r:
                for w in range(2):
                    store6(r, w)
            for w in range(2):
                sp.wait_ge(o_stored[w], 16 * (NJ // V) + 16)

            def load7(t, u):
                sp.wait_ge(s["c1_done"], NT + t + u + 1)
                sp.dma_start(x_in[u], tile_rows(x6_dram, t + u)).then_inc(z_loaded[u], 16)

            def store7(t, u):
                sp.wait_ge(s["ln_done"], 7 * NT + t + u + 3)
                sp.dma_start(tile_rows(out.rearrange("b s d -> (b s) d"), t + u), x_out[u]).then_inc(z_stored[u], 16)

            for u in range(U):
                load7(0, u)
            with sp.Fori(0, NT // U - 1) as r:
                for u in range(U):
                    load7(U * r + U, u)
                for u in range(U):
                    store7(U * r, u)
            for u in range(U):
                store7(NT - U, u)
            for u in range(U):
                sp.wait_ge(z_stored[u], 16 * (NT // U) + 16)

        @block.tensor
        def _(pe):
            for k in pe_done:
                pe.sem_inc(s[k], 2 * CREDIT if k in by_half else CREDIT)
            pe.wait_ge(loaded, 16 * len(w_loads))
            taps = w_raw[:, 3:6, :].rearrange("p a b -> p (a b)").rearrange("p (i k) -> p k i", k=3)
            for k in range(7):
                last = pe.transpose(setup_ps[:, k, :], taps[:, k - 3, :] if 3 <= k < 6 else w_raw[:, k, :], ident)
            for k in range(3):
                last = pe.transpose(setup_ps[:, 8 + k, 0:2 * MH], g_raw[:, k, :], ident[0:2 * MH, 0:2 * MH])
            last.then_inc(w_turned, 1)
            pe.wait_ge(w_ready, W_READY)
            pe.wait_ge(zeroed, U + 1)

            def keep_busy(m, products):
                pe.wait_ge(s["turn0_copied"], m + 1)
                for _ in range(products):
                    pe.matmul(turned_ps[:, 0, :], ident16, causal16.unsqueeze(1).broadcast_to([P, 8, S]),
                              start=True, stop=True, skip_group_check=True)

            def scores(m, u, q, k_done, causal):
                pe.wait_ge(s["q_copied"], q + 2)
                pe.wait_ge(s["shifted"], 2 * m)
                keys = k_bd[u].rearrange("p (h t) -> p h t", t=P)
                for g in range(NR):
                    pe.wait_ge(s["k_copied"], 2 * k_done + g + 3)
                    if causal:
                        pe.matmul(scores_ps[:, u, g, :], ident16,
                                  causal16.unsqueeze(1).broadcast_to([P, 8, S]),
                                  start=True, stop=False, skip_group_check=True)
                    for b in range(NB):
                        last = pe.matmul(scores_ps[S * b:S * b + S, u, g, :],
                                         q_T[u][:, S * b:S * b + S],
                                         keys[:, 8 * g:8 * g + 8, S * b:S * b + S],
                                         start=not causal, stop=True, skip_group_check=True)
                    last.then_inc(s["scores_done"], 1)

            def mix(m, u, v_use):
                if u == 0:
                    keep_busy(m, SPARE)
                for half in range(2):
                    pe.wait_ge(s["exp_done"], 2 * m + half + 3)
                    pe.wait_ge(s[f"turn{half}_copied"], m + 1)
                    for k in range(4):
                        hp = 4 * half + k
                        last = pe.transpose(turned_ps[:, half, P * k:P * k + P],
                                            probs[u][:, P * hp:P * hp + P], ident)
                    last.then_inc(s[f"turn{half}_done"], 1)
                pe.wait_ge(desk_empty, v_use + 2)
                pe.wait_ge(s["normed"], m + 1)
                for hp in range(8):
                    if hp % 4 == 0:
                        pe.wait_ge(s[f"turn{hp // 4}_copied"], m + 2)
                    last = pe.matmul(heads_ps[:, 36 * hp:36 * hp + 36], turned[u][:, P * hp:P * hp + P],
                                     v_bd[u][:, 36 * hp:36 * hp + 36], start=True, stop=True,
                                     skip_group_check=True)
                last.then_inc(s["pv_done"], 1)

            def turn(use, src):
                pe.wait_ge(desk_empty, use + 1)
                pe.transpose(trans_ps, src, ident).then_inc(desk_full, 1)

            def turn_all(use, sources):
                pe.wait_ge(desk_empty, use + 1)
                for k, src in enumerate(sources):
                    last = pe.transpose(desk_ps[:, P * k:P * k + P], src, ident)
                last.then_inc(desk_full, 1)

            def values(use, u, src_T, w):
                pe.wait_ge(desk_empty, use + 1)
                wv = w.rearrange("p (g h c) -> p h g c", g=8, h=2)
                for b in range(NB):
                    for par in range(2):
                        last = pe.matmul(desk_ps[S * par:S * par + S, S * b:S * b + S],
                                         src_T[u][:, S * b:S * b + S], wv[:, par], start=True, stop=True,
                                         skip_group_check=True)
                last.then_inc(desk_full, 1)

            with pe.Fori(0, NT // U) as r:
                t = U * r
                d = USES[1] * r
                for u in range(U):
                    pe.wait_ge(in_loaded[u], 8 * t + 16)
                turn_all(d, x_in)
                pe.wait_ge(desk_empty, d + 2)
                for u in range(U):
                    pe.wait_ge(s["y_done"], t + u + 1)
                    for k in range(2):
                        last = pe.matmul(scores_ps[:, u, k, 0:P], a_w[:, k, :], x_T[u],
                                         start=True, stop=True, skip_group_check=True)
                    last.then_inc(s["qk_done"], 1)
                for u in range(U):
                    values(d + 1 + u, u, x_T, a_w[:, 2, :])
                for u in range(U):
                    scores(2 * t + u + 1, u, 2 * t + u + 1, t + u + 1, True)
                for u in range(U):
                    mix(2 * t + u + 1, u, d + 1 + u)
                for u in range(U):
                    pe.wait_ge(s["normed"], 2 * t + u + 3)
                    turn(d + 3 + u, ctx_o[u])
                for u in range(U):
                    pe.wait_ge(desk_empty, d + 3 + u + 2)
                    pad = pad_T[u].rearrange("p (b s) -> p b s", b=NB)
                    for k in range(3):
                        last = pe.matmul(scores_ps[:, u, 0, 0:P], a_w[:, 3 + k, :], pad[:, :, k:k + S],
                                         start=(k == 0), stop=(k == 2), skip_group_check=True)
                    last.then_inc(s["conv_done"], 1)
                for u in range(U):
                    scores(2 * t + 2 + u + 1, u, 2 * t + 2 + u + 1, t + u + 1, True)
                for u in range(U):
                    mix(2 * t + 2 + u + 1, u, d + 1 + u)
                for u in range(U):
                    pe.wait_ge(s["normed"], 2 * t + 2 + u + 3)
                    turn(d + 5 + u, ctx_o[u])
                for u in range(U):
                    pe.wait_ge(desk_empty, d + 5 + u + 2)
                    pe.matmul(scores_ps[:, u, 0, 0:P], o_T[u], a_w[:, 6, :], start=True, stop=True,
                              skip_group_check=True).then_inc(s["out_done"], 1)

            pe.wait_ge(hop_gathered, 16 * HOPS)
            pe.wait_ge(s["y_done"], NT + 2)
            for c in range(HOPS // 4):
                if c >= 4:
                    pe.wait_ge(hop_copied, c - 3)
                for k in range(4):
                    last = pe.transpose(setup_ps[:, 4 * (c % 4) + k, :], hop_rows[:, 4 * c + k, :], ident)
                last.then_inc(hop_turned, 1)
            with pe.Fori(0, S // U) as r:
                v = U * r
                for u in range(U):
                    pe.wait_ge(hx_loaded[u], 8 * v + 16)
                    pe.wait_ge(desk_empty, HOP_DESK + v + u + 1)
                    pe.transpose(desk_ps[:, 0:B], hx_in[u][0:B], ident[0:B, 0:B]).then_inc(desk_full, 1)
                for u in range(U):
                    pe.wait_ge(desk_empty, HOP_DESK + v + u + 2)
                    pe.wait_ge(s["hb_done"], v + u + 3)
                    pe.wait_ge(s["hop_out0"], v + u + 1)
                    vu = pe.to_reg(v + u + 1)
                    pe.wait_ge(hop_copied, HOPS // 4)
                    pe.wait_ge(s["hop_out1"], vu)
                    for g in range(NR):
                        last = pe.matmul(scores_ps[0:B, u, g, 0:4 * S], hx_T[u][64 * g:64 * g + 64, 0:B],
                                         hop_bd[u][64 * g:64 * g + 64, :], start=True, stop=True,
                                         skip_group_check=True)
                    last.then_inc(s["hop_done"], 1)

            base = BASE[3]

            def rope_products(n, u, hT, w):
                for k in range(4):
                    last = pe.matmul(scores_ps[:, u, k // 2, P * (k % 2):P * (k % 2) + P], w[:, k, :], hT[u],
                                     start=True, stop=True, skip_group_check=True)
                last.then_inc(s["qk_done"], 1)

            with pe.Fori(0, NT // U) as r:
                t = U * r
                d = base["desk"] + USES[3] * r
                m = base["att"] + 2 * t
                for u in range(U):
                    pe.wait_ge(in_loaded[u], 8 * t + 8 * NT + 16)
                    pe.wait_ge(c_loaded[u], 32 * t + 64)
                turn_all(d, x_in + c_in)
                pe.wait_ge(desk_empty, d + 2)
                for u in range(U):
                    for k, src in enumerate((x_T, c_T, c_T)):
                        last = pe.matmul(desk_ps[:, 16 * u:16 * u + 16], src[u], g_w[:, k, :], start=(k == 0),
                                         stop=(k == 2), skip_group_check=True)
                last.then_inc(desk_full, 1)
                for u in range(U):
                    pe.wait_ge(s["k_copied"], 2 * (base["k"] + 2 * t + u + 1) + 4)
                    pe.wait_ge(s["shifted"], 2 * (m + u + 1))
                    keys = k_bd[u][:, 0:MH * P].rearrange("p (h t) -> p h t", t=P)
                    for b in range(NB):
                        last = pe.matmul(scores_ps[S * b:S * b + S, u, 0, :], x_T[u][:, S * b:S * b + S],
                                         keys[:, :, S * b:S * b + S], start=True, stop=True, skip_group_check=True)
                    last.then_inc(s["scores_done"], 2)
                pe.wait_ge(s["log_f_done"], t + U + 2)
                pe.wait_ge(desk_empty, d + 3)
                pe.matmul(desk_ps[:, 0:U * MH], const("tri2"), whole["log_f"][:].rearrange("p u h -> p (u h)"),
                          start=True, stop=True).then_inc(desk_full, 1)
                for u in range(U):
                    pe.wait_ge(s["g_diag_done"], t + u + 3)
                    pe.wait_ge(s["turn1_copied"], m + u + 2)
                    pe.matmul(turned_ps[:, 1, :], const("ones2"), g_diag[u], start=True, stop=False)
                    pe.matmul(turned_ps[:, 1, :], ident16, causal16.unsqueeze(1).broadcast_to([P, MH, S]),
                              start=False, stop=True).then_inc(s["turn1_done"], 1)
                for u in range(U):
                    pe.wait_ge(s["exp_done"], 2 * (m + u + 1) + 4)
                    pe.wait_ge(s["turn0_copied"], m + u + 2)
                    for k in range(4):
                        last = pe.transpose(turned_ps[:, 0, P * k:P * k + P], probs[u][:, P * k:P * k + P], ident)
                    last.then_inc(s["turn0_done"], 1)
                    pe.wait_ge(s["m_v_done"], t + u + 3)
                    pe.wait_ge(s["normed"], m + u + 2)
                    pe.wait_ge(s["turn0_copied"], m + u + 3)
                    w = NB * 2 * (MD + 1)
                    for k in range(4):
                        last = pe.matmul(heads_ps[:, w * k:w * k + w], turned[u][:, P * k:P * k + P],
                                         m_vbd[u][:, w * k:w * k + w], start=True, stop=True, skip_group_check=True)
                    last.then_inc(s["pv_done"], 1)
                for u in range(U):
                    pe.wait_ge(s["ln_done"], base["ln"] + 3 * t + U + u + 3)
                    turn(d + 3 + u, xn[u])
                for u in range(U):
                    pe.wait_ge(desk_empty, d + 3 + u + 2)
                    rope_products(base["qk"] + t + u + 1, u, h_T, f_w)
                for u in range(U):
                    values(d + 5 + u, u, h_T, f_w[:, 4, :])
                for u in range(U):
                    scores(m + 2 + u + 1, u, base["q"] + t + u + 1, base["k"] + 2 * t + 2 + u + 1, True)
                for u in range(U):
                    mix(m + 2 + u + 1, u, d + 5 + u)
                for u in range(U):
                    pe.wait_ge(s["normed"], m + 2 + u + 3)
                    turn(d + 7 + u, ctx_o[u])
                for u in range(U):
                    pe.wait_ge(desk_empty, d + 7 + u + 2)
                    pe.matmul(scores_ps[:, u, 0, 0:P], o_T[u], f_w[:, 5, :], start=True, stop=True,
                              skip_group_check=True).then_inc(s["out_done"], 1)
                for u in range(U):
                    pe.wait_ge(s["ln_done"], base["ln"] + 3 * t + 2 * U + u + 3)
                    turn(d + 9 + u, xn[u])
                for u in range(U):
                    pe.wait_ge(desk_empty, d + 11 + u + 1)
                    pe.matmul(desk_ps[:, 0:8], h_T[u], f_gate[:], start=True, stop=True).then_inc(desk_full, 1)


            def count(n, E):
                pe.wait_ge(route_masked, n)
                cols = NT * E
                for c in range(-(-cols // 512)):
                    w = min(512, cols - 512 * c)
                    for k, lhs in enumerate(("tri16", "ones16")):
                        last = pe.matmul(scores_ps[:, k, c, 0:w], const16(lhs), r_mask[:, 512 * c:512 * c + w],
                                         start=True, stop=True)
                last.then_inc(route_counted, 1)

            count(1, E0)
            pe.wait_ge(counts_read, 1)

            with pe.Fori(0, E0 // 2) as r:
                for i in range(2 * GE):
                    w, u, q = i // GE, i % 2, 2 * GE * r + i
                    pe.wait_ge(e_in_loaded[u], 16 * J * (GE * r + i // 2 + 1))
                    pe.wait_ge(s["e_T_done"], q + 1)
                    for j in range(J):
                        last = pe.transpose(turned_ps[:, u, P * j:P * j + P], e_in[u][:, P * j:P * j + P], ident)
                    last.then_inc(s["e_turned"], 1)
                    pe.wait_ge(s["e_T_done"], q + 3)
                    pe.wait_ge(e_loaded[w], 64 * r + 64)
                    for f in range(F0):
                        pe.wait_ge(gelu_done, F0 * q + f + 1)
                        pe.matmul(scores_ps[:, f // 2, f % 2, 0:GS], e_w1[w][:, P * f:P * f + P], e_T[u],
                                  start=True, stop=True).then_inc(up_done, 1)
                    pe.wait_ge(s["e_out_done"], q + 1)
                    bank = (heads_ps, desk_ps)[u]
                    for f in range(F0):
                        pe.wait_ge(gelu_done, F0 * q + f + 1 + F0)
                        for j in range(J):
                            last = pe.matmul(bank[:, P * j:P * j + P], e_mid[u][:, f, P * j:P * j + P],
                                             e_w2[w][:, f, :], start=(f == 0 and j == 0),
                                             stop=(f == F0 - 1 and j == J - 1), skip_group_check=True)
                    last.then_inc(s["down_done"], 1)

            base = BASE[5]
            pe.wait_ge(late, 16 * len(late_loads))
            pe.wait_ge(w_ready, W_READY + 2)
            with pe.Fori(0, NT // U) as r:
                t = U * r
                d = base["desk"] + USES[5] * r
                m = base["att"] + 2 * t
                ln = base["ln"] + 3 * t
                o2 = base["qk"] + 2 * t
                for u in range(U):
                    pe.wait_ge(s["ln_done"], ln + u + 3)
                    turn(d + u, x4[u])
                for u in range(U):
                    pe.wait_ge(desk_empty, d + u + 2)
                    rope_products(o2 + u + 1, u, x_T, l_w)
                for u in range(U):
                    values(d + 2 + u, u, x_T, l_w[:, 4, :])
                for u in range(U):
                    scores(m + u + 1, u, base["q"] + 2 * t + u + 1, base["k"] + 2 * t + u + 1, True)
                for u in range(U):
                    mix(m + u + 1, u, d + 2 + u)
                for u in range(U):
                    pe.wait_ge(s["normed"], m + u + 3)
                    turn(d + 4 + u, ctx_o[u])
                for u in range(U):
                    pe.wait_ge(desk_empty, d + 4 + u + 2)
                    pe.matmul(scores_ps[:, u, 0, 0:P], o_T[u], l_w[:, 5, :], start=True, stop=True,
                              skip_group_check=True).then_inc(s["out_done"], 1)
                for u in range(U):
                    pe.wait_ge(c_loaded[u], 32 * NT + 24 * t + 48)
                turn_all(d + 6, c_in)
                for u in range(U):
                    values(d + 7 + u, u, c_T, c_w[:, 2, :])
                keep_busy(m + 3, LONG)
                for u in range(U):
                    pe.wait_ge(s["ln_done"], ln + U + u + 3)
                    turn(d + 9 + u, x5[u])
                for u in range(U):
                    pe.wait_ge(desk_empty, d + 9 + u + 2)
                    for k, src in enumerate((x_T, c_T)):
                        last = pe.matmul(scores_ps[:, u, k, 0:P], c_w[:, k, :], src[u], start=True, stop=True,
                                         skip_group_check=True)
                    last.then_inc(s["qk_done"], 1)
                for u in range(U):
                    scores(m + 2 + u + 1, u, base["q"] + 2 * t + 2 + u + 1, base["k"] + 2 * t + 2 + u + 1, False)
                for u in range(U):
                    mix(m + 2 + u + 1, u, d + 7 + u)
                for u in range(U):
                    pe.wait_ge(s["normed"], m + 2 + u + 3)
                    turn(d + 11 + u, ctx_o[u])
                for u in range(U):
                    pe.wait_ge(desk_empty, d + 11 + u + 2)
                    pe.matmul(scores_ps[:, u, 0, 0:P], o_T[u], c_w[:, 3, :], start=True, stop=True,
                              skip_group_check=True).then_inc(s["out_done"], 1)
                for u in range(U):
                    pe.wait_ge(s["ln_done"], ln + 2 * U + u + 3)
                    turn(d + 13 + u, x6[u])
                for u in range(U):
                    pe.wait_ge(desk_empty, d + 15 + u + 1)
                    pe.matmul(desk_ps[:, 0:E1], x_T[u], rt_w[:], start=True, stop=True).then_inc(desk_full, 1)

            count(2, E1)
            pe.wait_ge(counts_read, 2)
            def expert(r, w, i):
                return pe.value_load(expert_of[0:1, bass.ds(V * r + 2 * w + i, 1)], min_val=0, max_val=E1 - 1)

            def cols(i):
                return slice(P * i, P * i + P)

            with pe.Fori(0, NJ // V) as r:
                for w in range(2):
                    q = 2 * r + w + 1
                    pe.wait_ge(o_in_loaded[w], 32 * r + 32)
                    pe.wait_ge(s["o_T_done"], q)
                    for i in range(2):
                        last = pe.transpose(turned_ps[:, w, cols(i)], o_in[w][:, cols(i)], ident)
                    last.then_inc(s["o_turned"], 1)
                for w in range(2):
                    q = 2 * r + w + 1
                    experts = [expert(r, w, i) for i in range(2)]
                    pe.wait_ge(s["o_T_done"], q + 2)
                    pe.wait_ge(s["o_h_done"], q)
                    for i, e in enumerate(experts):
                        last = pe.matmul(scores_ps[:, w, 0, cols(i)], o_in_T[w][:, cols(i)],
                                         o_w1[:, bass.ds(e, 1), :].rearrange("p e h -> p (e h)"),
                                         start=True, stop=True, skip_group_check=True)
                    last.then_inc(s["o_up"], 1)
                for w in range(2):
                    q = 2 * r + w + 1
                    pe.wait_ge(s["o_hn_done"], q + 2)
                    pe.wait_ge(s["o_g_done"], q)
                    for i in range(2):
                        last = pe.transpose(scores_ps[:, w, 1, cols(i)], o_hn[w][:, cols(i)], ident)
                    last.then_inc(s["o_hturned"], 1)
                for w in range(2):
                    q = 2 * r + w + 1
                    experts = [expert(r, w, i) for i in range(2)]
                    pe.wait_ge(s["o_g_done"], q + 2)
                    pe.wait_ge(s["o_out_done"], q)
                    for i, e in enumerate(experts):
                        last = pe.matmul((heads_ps, desk_ps)[w][:, cols(i)], o_g_T[w][:, cols(i)],
                                         o_w2[:, bass.ds(e, 1), :].rearrange("p e h -> p (e h)"),
                                         start=True, stop=True, skip_group_check=True)
                    last.then_inc(s["o_down"], 1)

        @block.scalar
        def _(act):
            for k in act_done:
                act.sem_inc(s[k], 2 * CREDIT if k in by_half else CREDIT)
            act.sem_inc(desk_empty, 1)
            act.wait_ge(loaded, 16 * len(w_loads))
            act.wait_ge(zeroed, U + 1)

            def copy_turned(use, dst, src=None, **kw):
                act.wait_ge(desk_full, use + 1)
                act.activation(dst, trans_ps if src is None else src, ACT.Identity, **kw).then_inc(desk_empty, 1)

            def exp(m, u, scale):
                for g in range(NR):
                    act.wait_ge(s["shifted"], 2 * m + g + 3)
                    half = probs[u][:, 512 * g:512 * g + 512]
                    act.activation(half, half, ACT.Exp, scale=scale).then_inc(s["exp_done"], 1)

            def copy_probs(m, u):
                act.wait_ge(s["pv_done"], m)
                for half in range(2):
                    act.wait_ge(s[f"turn{half}_done"], m + 2)
                    act.activation(turned[u][:, 512 * half:512 * half + 512], turned_ps[:, half, :],
                                   ACT.Identity).then_inc(s[f"turn{half}_copied"], 1)

            with act.Fori(0, NT // U) as r:
                t = U * r
                d = USES[1] * r
                copy_turned(d, whole["x_T"][:], desk_ps[:, 0:U * P].rearrange("p (u n) -> p u n", u=U))
                for u in range(U):
                    act.wait_ge(s["qk_done"], t + u + 3)
                    act.activation(q_T[u], scores_ps[:, u, 0, 0:P], ACT.Identity,
                                   bias=a_col[:, 0:1]).then_inc(s["q_copied"], 1)
                for u in range(U):
                    exp(2 * t + u + 1, u, SCALE)
                    copy_probs(2 * t + u + 1, u)
                for u in range(U):
                    pad = pad_T[u].rearrange("p (b s) -> p b s", b=NB)
                    copy_turned(d + 3 + u, pad[:, :, 1:1 + S], trans_ps.rearrange("p (b s) -> p b s", b=NB))
                for u in range(U):
                    act.wait_ge(s["conv_done"], t + u + 3)
                    act.activation(q_T[u], scores_ps[:, u, 0, 0:P], ACT.Identity,
                                   bias=a_col[:, 2:3]).then_inc(s["q_copied"], 1)
                for u in range(U):
                    exp(2 * t + 2 + u + 1, u, SCALE)
                    copy_probs(2 * t + 2 + u + 1, u)
                for u in range(U):
                    copy_turned(d + 5 + u, o_T[u])

            with act.Fori(0, S // U) as r:
                v = U * r
                for u in range(U):
                    copy_turned(HOP_DESK + v + u, hx_T[u][:, 0:B], desk_ps[:, 0:B])
                for u in range(U):
                    act.wait_ge(s["hop_done"], v + u + 3)
                    act.wait_ge(hop_stored[u], 8 * v + 16)
                    act.activation(hop_out[u][0:B, 0:4 * S], scores_ps[0:B, u, 0, 0:4 * S], ACT.Identity)\
                       .then_inc(s["hop_out0"], 1)

            base = BASE[3]
            with act.Fori(0, NT // U) as r:
                t = U * r
                d = base["desk"] + USES[3] * r
                m = base["att"] + 2 * t
                act.wait_ge(desk_full, d + 1)
                act.activation(whole["x_T"][:], desk_ps[:, 0:U * P].rearrange("p (u n) -> p u n", u=U), ACT.Identity)
                copy_turned(d, whole["c_T"][:], desk_ps[:, U * P:2 * U * P].rearrange("p (u n) -> p u n", u=U))
                for u in range(U):
                    act.wait_ge(s["pv_done"], m + u + 1)
                    act.wait_ge(c_loaded[u], 32 * t + 64)
                    mvv = m_vbd[u].rearrange("p (g b h c) -> p g b h c", g=4, b=NB, h=2)
                    cv = c_two[u].rearrange("p (b g h c) -> p g b h c", b=NB, g=4, h=2)
                    for par in range(2):
                        rows = slice(S * par, S * par + S)
                        last = act.activation(mvv[rows, :, :, par, 0:MD], cv[rows, :, :, par, :], ACT.Identity)
                    last.then_inc(s["m_v_done"], 1)
                act.wait_ge(s["neg_abs_done"], t + U + 2)
                act.activation(whole["exp_abs"][:], whole["neg_abs"][:], ACT.Exp).then_inc(s["exp_abs_done"], U)
                act.wait_ge(s["exp_abs_done"], t + U + 2)
                act.activation(whole["soft"][:], whole["exp_abs"][:], ACT.Ln, bias=1.0).then_inc(s["soft_done"], U)
                for u in range(U):
                    act.wait_ge(s["turn1_copied"], m + u + 3)
                    act.activation(decay[u], decay[u], ACT.Exp).then_inc(s["decay_done"], 1)
                    act.wait_ge(s["cmax_done"], t + u + 3)
                    act.activation(floor[u], cmax[u], ACT.Exp, scale=-1.0).then_inc(s["floor_done"], 1)
                for u in range(U):
                    act.wait_ge(s["turn0_done"], m + u + 3)
                    act.activation(turned[u][:, 0:512], turned_ps[:, 0, :], ACT.Identity)\
                       .then_inc(s["turn0_copied"], 1)
                for u in range(U):
                    copy_turned(d + 3 + u, h_T[u], scale=f_col[:, 0:1], bias=f_col[:, 1:2])
                for u in range(U):
                    exp(m + 2 + u + 1, u, SCALE)
                    copy_probs(m + 2 + u + 1, u)
                for u in range(U):
                    copy_turned(d + 7 + u, o_T[u])
                for u in range(U):
                    copy_turned(d + 9 + u, h_T[u], scale=f_col[:, 2:3], bias=f_col[:, 3:4])
                for u in range(U):
                    copy_turned(d + 11 + u, logits0[:, bass.ds(t + u, 1), :].rearrange("p t e -> p (t e)"),
                                desk_ps[:, 0:8])


            def route_exponentials(n, E):
                act.wait_ge(route_shifted, n)
                act.activation(r_gate[:, :, 0:E], r_gate[:, :, 0:E], ACT.Exp).then_inc(route_exp, 1)

            route_exponentials(1, E0)
            act.sem_inc(gelu_done, F0)
            with act.Fori(0, E0 // 2) as r:
                for i in range(2 * GE):
                    w, u, q = i // GE, i % 2, 2 * GE * r + i
                    act.wait_ge(s["e_turned"], q + 3)
                    act.activation(e_T[u], turned_ps[:, u, 0:GS], ACT.Identity, scale=f_col[:, 2:3],
                                   bias=f_col[:, 3:4]).then_inc(s["e_T_done"], 1)
                    act.wait_ge(s["down_done"], q + 1)
                    act.wait_ge(e_loaded[w], 64 * r + 64)
                    for f in range(F0):
                        act.wait_ge(up_done, F0 * q + f + 1)
                        act.activation(e_mid[u][:, f, :], scores_ps[:, f // 2, f % 2, 0:GS], ACT.Gelu,
                                       bias=e_b1[w][:, f:f + 1]).then_inc(gelu_done, 1)

            base = BASE[5]
            act.wait_ge(late, 16 * len(late_loads))
            act.wait_ge(w_ready, W_READY + 2)
            with act.Fori(0, NT // U) as r:
                t = U * r
                d = base["desk"] + USES[5] * r
                m = base["att"] + 2 * t
                for u in range(U):
                    copy_turned(d + u, x_T[u])
                for u in range(U):
                    exp(m + u + 1, u, SCALE)
                    copy_probs(m + u + 1, u)
                for u in range(U):
                    copy_turned(d + 4 + u, o_T[u])
                copy_turned(d + 6, whole["c_T"][:], desk_ps[:, 0:U * P].rearrange("p (u n) -> p u n", u=U))
                for u in range(U):
                    copy_turned(d + 9 + u, x_T[u])
                for u in range(U):
                    act.wait_ge(s["qk_done"], base["qk"] + 2 * t + 2 + u + 3)
                    act.activation(q_T[u], scores_ps[:, u, 0, 0:P], ACT.Identity, bias=c_col[:, 2:3],
                                   scale=SCALE).then_inc(s["q_copied"], 1)
                for u in range(U):
                    exp(m + 2 + u + 1, u, 1.0)
                    copy_probs(m + 2 + u + 1, u)
                for u in range(U):
                    copy_turned(d + 11 + u, o_T[u])
                for u in range(U):
                    copy_turned(d + 13 + u, x_T[u])

            route_exponentials(2, E1)
            with act.Fori(0, NJ // V) as r:
                for w in range(2):
                    act.wait_ge(s["o_turned"], 2 * r + w + 3)
                    act.activation(o_in_T[w], turned_ps[:, w, 0:2 * P], ACT.Identity).then_inc(s["o_T_done"], 1)
                for w in range(2):
                    experts = [act.value_load(expert_of[0:1, bass.ds(V * r + 2 * w + i, 1)], min_val=0, max_val=E1 - 1)
                               for i in range(2)]
                    act.wait_ge(s["o_down"], 2 * r + w + 1)
                    act.wait_ge(s["o_hturned"], 2 * r + w + 3)
                    for i, e in enumerate(experts):
                        cols = slice(P * i, P * i + P)
                        last = act.activation(o_g_T[w][:, cols], scores_ps[:, w, 1, cols], ACT.Gelu,
                                              scale=o_g[:, bass.ds(e, 1)], bias=o_b[:, bass.ds(e, 1)])
                    last.then_inc(s["o_g_done"], 1)

        @block.vector
        def _(dve):
            for k in dve_done:
                dve.sem_inc(s[k], 2 * CREDIT if k in by_half else CREDIT)
            dve.wait_ge(w_turned, 1)
            dve.wait_ge(loaded, 16 * len(w_loads))
            dve.tensor_copy(consts16[:], shared[:, 0:cb_n]).then_inc(w_ready, 1)
            dve.tensor_copy(a_w[:], setup_ps[:, 0:7, :]).then_inc(w_ready, 1)
            dve.tensor_copy(g_w[:], setup_ps[:, 8:11, 0:2 * MH]).then_inc(w_ready, 1)
            dve.tensor_scalar(m_row[:, 0, :], m_row[:, 0, :], 1.0, None, ALU.add).then_inc(w_ready, 1)

            def rotate(dst, src):
                dv = dst.rearrange("p (h k c) -> p h k c", h=H, k=2)
                sv = src.rearrange("p (h k c) -> p h k c", h=H, k=2)
                dve.tensor_scalar(dv[:, :, 0, :], sv[:, :, 1, :], -1.0, None, ALU.mult)
                return dve.tensor_copy(dv[:, :, 1, :], sv[:, :, 0, :])

            fr = f_raw[:].rearrange("p (h k c) -> p k h c", h=H, k=3)
            for k, at in enumerate((0, 2, 4)):
                last = dve.tensor_copy(f_w[:, at, :].rearrange("p (h c) -> p h c", h=H), fr[:, k])
            last.then_inc(w_copied, 1)
            dve.wait_ge(w_copied, 1)
            rotate(f_w[:, 1, :], f_w[:, 0, :])
            rotate(f_w[:, 3, :], f_w[:, 2, :]).then_inc(w_ready, 1)

            def spread_keys(u, src, bias, head, count):
                for g in range(NR):
                    hs = slice(8 * g, 8 * g + 8)
                    out_v = k_bd[u].rearrange("p (h t) -> p h t", h=H)[:, hs]
                    in_v = src.unsqueeze(1).broadcast_to([P, 8, P])
                    mask = const(head)[:, hs].unsqueeze(2).broadcast_to([P, 8, P])
                    dve.scalar_tensor_tensor(out_v, in_v, bias, mask, ALU.add, ALU.mult).then_inc(count, 1)

            def softmax_shift(m, u):
                for g in range(NR):
                    dve.wait_ge(s["scores_done"], 2 * m + g + 3)
                    sc = scores_ps[:, u, g, :].rearrange("p (h t) -> p h t", t=S)
                    best = row_max[u][:, 8 * g:8 * g + 8]
                    dve.tensor_reduce(best, sc, AX, ALU.max).then_inc(s["max_done"], 1)
                    dve.wait_ge(s["max_done"], 2 * m + g + 3)
                    dve.wait_ge(s["turn1_done"], m)
                    dve.tensor_tensor(probs[u][:, 512 * g:512 * g + 512].rearrange("p (h t) -> p h t", t=S), sc,
                                      best.unsqueeze(2).broadcast_to([P, 8, S]), ALU.subtract)\
                       .then_inc(s["shifted"], 1)

            def normalise(m, u):
                dve.wait_ge(s["pv_done"], m + 2)
                hv = heads_ps[:, 0:288].rearrange("p (g b h c) -> p g b h c", g=8, b=NB, h=2)
                for b in range(NB):
                    rows = slice(S * b, S * b + S)
                    last = dve.reciprocal(recip[u][rows].rearrange("p (g h) -> p g h", g=8), hv[rows, :, b, :, HD])
                last.then_inc(s["recip_done"], 1)
                dve.wait_ge(s["recip_done"], m + 2)
                for b in range(NB):
                    rows = slice(S * b, S * b + S)
                    r = recip[u][rows].rearrange("p (g h) -> p g h", g=8).unsqueeze(3).broadcast_to([S, 8, 2, HD])
                    last = dve.tensor_tensor(ctx_o[u][rows].rearrange("p (g h c) -> p g h c", g=8, h=2),
                                             hv[rows, :, b, :, 0:HD], r, ALU.mult)
                last.then_inc(s["normed"], 1)

            def copy_values(use, u, bias):
                dve.wait_ge(desk_full, use + 1)
                vv = v_bd[u].rearrange("p (g b h c) -> p g b h c", g=8, b=NB, h=2)
                pv = desk_ps[:, 0:P].rearrange("p (b g c) -> p g b c", b=NB, g=8)
                bv = bias.rearrange("p (g h c) -> p g h c", g=8, h=2) if bias is not None else None
                for par in range(2):
                    rows = slice(S * par, S * par + S)
                    if bias is None:
                        last = dve.tensor_copy(vv[rows, :, :, par, 0:HD], pv[rows])
                        continue
                    last = dve.tensor_tensor(vv[rows, :, :, par, 0:HD], pv[rows],
                                             bv[rows, :, par, :].unsqueeze(2).broadcast_to([S, 8, NB, HD]),
                                             ALU.add)
                last.then_inc(desk_empty, 1)

            def ln_stats(o, u, src):
                dve.bn_stats(stat[u], src).then_inc(s["stat_done"], 1)
                o2 = dve.to_reg(o + 2)
                dve.wait_ge(w_turned, 1)
                dve.wait_ge(s["stat_done"], o2)
                dve.bn_aggr(mv[u], stat[u]).then_inc(s["mv_done"], 1)
                dve.wait_ge(s["mv_done"], o + 2)
                dve.tensor_scalar(veps[u], mv[u][:, 1:2], EPS_LN, None, ALU.add).then_inc(s["veps_done"], 1)

            def ln_apply(o, u, dst, src):
                dve.wait_ge(s["rstd_done"], o + 2)
                dve.tensor_scalar(dst, src, mv[u][:, 0:1], rstd[u], ALU.subtract, ALU.mult)\
                   .then_inc(s["ln_done"], 1)

            with dve.Fori(0, NT // U) as r:
                t = U * r
                d = USES[1] * r
                for u in range(U):
                    copy_values(d + 1 + u, u, a_row[:, 0, :])
                for u in range(U):
                    dve.wait_ge(s["qk_done"], t + u + 3)
                    spread_keys(u, scores_ps[:, u, 1, 0:P], a_col[:, 1:2], "head16", s["k_copied"])
                for u in range(U):
                    softmax_shift(2 * t + u + 1, u)
                for u in range(U):
                    normalise(2 * t + u + 1, u)
                for u in range(U):
                    softmax_shift(2 * t + 2 + u + 1, u)
                for u in range(U):
                    normalise(2 * t + 2 + u + 1, u)
                for u in range(U):
                    dve.wait_ge(s["out_done"], t + u + 3)
                    dve.wait_ge(s["x_res_done"], t + u + 3)
                    dve.tensor_tensor(y[u], scores_ps[:, u, 0, 0:P], x_res[u], ALU.add).then_inc(s["y_done"], 1)
                for u in range(U):
                    dve.wait_ge(s["y_done"], t + u + 3)
                    ln_stats(t + u + 1, u, y[u])
                for u in range(U):
                    dve.wait_ge(x_stored[u], 8 * t + 16)
                    ln_apply(t + u + 1, u, x_out[u], y[u])

            for c in range(HOPS // 4):
                dve.wait_ge(hop_turned, c + 1)
                dve.tensor_copy(hop_T[:, 4 * c:4 * c + 4, :], setup_ps[:, 4 * (c % 4):4 * (c % 4) + 4, :])\
                   .then_inc(hop_copied, 1)
            dve.wait_ge(hop_copied, HOPS // 4)
            hop_by_query = hop_T[:].rearrange("p j (v m) -> p (j v) m", v=2)
            with dve.Fori(0, S // U) as r:
                v = U * r
                for u in range(U):
                    dve.wait_ge(s["hop_done"], v + u + 1)
                    dve.tensor_tensor(hop_bd[u].rearrange("p (h m) -> p h m", h=4),
                                      hop_by_query[:, bass.ds(v + u, 1), :].broadcast_to([P, 4, S]),
                                      const("head4").unsqueeze(2).broadcast_to([P, 4, S]), ALU.mult)\
                       .then_inc(s["hb_done"], 1)
                for u in range(U):
                    dve.wait_ge(s["hop_done"], v + u + 3)
                    dve.wait_ge(hop_stored[u], 8 * v + 16)
                    dve.tensor_copy(hop_out[u][0:B, 4 * S:8 * S], scores_ps[0:B, u, 1, 0:4 * S])\
                       .then_inc(s["hop_out1"], 1)

            base = BASE[3]

            def rope(n, u):
                dve.wait_ge(s["qk_done"], n + 2)
                qk = scores_ps[:, u].rearrange("p g (r n) -> p r g n", n=P)
                for k, (dst, table) in enumerate(((rope_c, "cos"), (rope_s, "sin"))):
                    last = dve.tensor_tensor(dst[u].rearrange("p (g n) -> p g n", g=2), qk[:, k],
                                             const(table).unsqueeze(1).broadcast_to([P, 2, P]), ALU.mult)
                last.then_inc(s["rope_done"], 1)

            with dve.Fori(0, NT // U) as r:
                t = U * r
                n = t + 1
                d = base["desk"] + USES[3] * r
                m = base["att"] + 2 * t
                ln = base["ln"] + 3 * t
                last_n = n + U - 1
                gate_in, gate_f = whole["gates"][:, :, 0:MH], whole["gates"][:, :, MH:2 * MH]
                dve.wait_ge(desk_full, d + 2)
                dve.tensor_tensor(whole["gates"][:], desk_ps[:, 0:16 * U].rearrange("p (u h) -> p u h", u=U),
                                  g_row[:].unsqueeze(1).broadcast_to([P, U, 16]), ALU.add).then_inc(s["gates_done"], U)
                dve.wait_ge(s["gates_done"], last_n + 2)
                dve.sem_inc(desk_empty, 1)
                dve.scalar_tensor_tensor(whole["neg_abs"][:], gate_f, -1.0, gate_f, ALU.mult, ALU.min)\
                   .then_inc(s["neg_abs_done"], U)
                dve.wait_ge(s["soft_done"], last_n + 2)
                dve.scalar_tensor_tensor(whole["log_f"][:], gate_f, 0.0, whole["soft"][:], ALU.min, ALU.subtract)\
                   .then_inc(s["log_f_done"], U)
                dve.wait_ge(desk_full, d + 3)
                sums = desk_ps[:, 0:U * MH].rearrange("p (u h) -> p u h", u=U)
                dve.tensor_copy(whole["csum"][:], sums)
                dve.tensor_tensor(whole["g_key"][:], gate_in, sums, ALU.subtract).then_inc(s["g_key_done"], U)
                dve.wait_ge(s["g_key_done"], last_n + 2)
                dve.sem_inc(desk_empty, 1)
                for u in range(U):
                    dve.wait_ge(s["turn1_done"], m + u + 3)
                    gm = turned_ps[:, 1, :].rearrange("p (h t) -> p h t", t=S)
                    dve.tensor_reduce(row_max[u][:, 0:8], gm, AX, ALU.max).then_inc(s["max_done"], 2)
                    dve.wait_ge(s["max_done"], 2 * (m + u + 1) + 4)
                    dve.tensor_tensor(decay[u].rearrange("p (h t) -> p h t", t=S), gm,
                                      row_max[u][:, 0:8].unsqueeze(2).broadcast_to([P, 8, S]), ALU.subtract)\
                       .then_inc(s["turn1_copied"], 1)
                    dve.tensor_tensor(cmax[u], csum[u], row_max[u][:, 0:8], ALU.add).then_inc(s["cmax_done"], 1)
                for u in range(U):
                    dve.wait_ge(s["scores_done"], 2 * (m + u + 1) + 4)
                    dve.tensor_tensor(probs[u][:, 0:512], scores_ps[:, u, 0, :], hop_in[u], ALU.add)\
                       .then_inc(s["shifted"], 2)
                    dve.wait_ge(s["shifted"], 2 * (m + u + 1) + 4)
                    dve.wait_ge(s["decay_done"], n + u + 2)
                    dve.tensor_tensor(probs[u][:, 0:512], probs[u][:, 0:512], decay[u], ALU.mult)\
                       .then_inc(s["exp_done"], 2)
                for u in range(U):
                    dve.wait_ge(s["pv_done"], m + u + 3)
                    dve.wait_ge(s["floor_done"], n + u + 2)
                    hv = heads_ps[:, 0:272].rearrange("p (g b h c) -> p g b h c", g=4, b=NB, h=2)
                    for b in range(NB):
                        rows = slice(S * b, S * b + S)
                        last = dve.scalar_tensor_tensor(
                            denom[u][rows].rearrange("p (g h) -> p g h", g=4), hv[rows, :, b, :, MD], -1.0,
                            floor[u][rows].rearrange("p (g h) -> p g h", g=4), ALU.mult, ALU.max)
                    last.then_inc(s["denom_done"], 1)
                    dve.wait_ge(s["denom_done"], n + u + 2)
                    for b in range(NB):
                        rows = slice(S * b, S * b + S)
                        last = dve.tensor_tensor(
                            denom3[u][rows].rearrange("p (g h) -> p g h", g=4), hv[rows, :, b, :, MD],
                            denom[u][rows].rearrange("p (g h) -> p g h", g=4), ALU.max)
                    last.then_inc(s["denom3_done"], 1)
                    dve.wait_ge(s["denom3_done"], n + u + 2)
                    dve.tensor_scalar(denom2[u], denom3[u], 1e-6, None, ALU.add).then_inc(s["denom2_done"], 1)
                    dve.wait_ge(s["denom2_done"], n + u + 2)
                    dve.reciprocal(recip[u][:, 0:8], denom2[u]).then_inc(s["recip_done"], 1)
                    dve.wait_ge(s["recip_done"], m + u + 3)
                    for b in range(NB):
                        rows = slice(S * b, S * b + S)
                        rv = recip[u][rows, 0:8].rearrange("p (g h) -> p g h", g=4).unsqueeze(3)
                        last = dve.tensor_tensor(ctx_o[u][rows].rearrange("p (g h c) -> p g h c", g=4, h=2),
                                                 hv[rows, :, b, :, 0:MD], rv.broadcast_to([S, 4, 2, MD]), ALU.mult)
                    last.then_inc(s["normed"], 1)
                for u in range(U):
                    by_head = ctx_o[u].rearrange("p (h c) -> p h c", c=MD)
                    dve.wait_ge(s["normed"], m + u + 3)
                    dve.tensor_reduce(h_sum[u], by_head, AX, ALU.add).then_inc(s["h_sum_done"], 1)
                    dve.wait_ge(s["h_sum_done"], n + u + 2)
                    dve.scalar_tensor_tensor(h_mid[u].rearrange("p (h c) -> p h c", c=MD),
                                             h_sum[u].unsqueeze(2).broadcast_to([P, MH, MD]), -1.0 / MD, by_head,
                                             ALU.mult, ALU.add).then_inc(s["h_mid_done"], 1)
                for u in range(U):
                    dve.wait_ge(s["h_mid_done"], n + u + 2)
                    dve.tensor_tensor(h_sq[u], h_mid[u], h_mid[u], ALU.mult).then_inc(s["h_sq_done"], 1)
                for u in range(U):
                    dve.wait_ge(s["h_sq_done"], n + u + 2)
                    dve.tensor_reduce(h_var[u], h_sq[u].rearrange("p (h c) -> p h c", c=MD), AX, ALU.add)\
                       .then_inc(s["h_var_done"], 1)
                for u in range(U):
                    dve.wait_ge(s["h_var_done"], n + u + 2)
                    dve.tensor_scalar(h_veps[u], h_var[u], 1.0 / MD, EPS_LN, ALU.mult, ALU.add).then_inc(s["h_veps_done"], 1)
                for u in range(U):
                    dve.wait_ge(s["h_mid_done"], n + u + 2)
                    dve.tensor_tensor(h_sq[u], h_mid[u], m_row[:, 0, :], ALU.mult).then_inc(s["z1_done"], 1)
                for u in range(U):
                    dve.wait_ge(s["z1_done"], n + u + 2)
                    dve.wait_ge(s["h_rstd_done"], n + u + 2)
                    dve.tensor_tensor(z[u].rearrange("p (h c) -> p h c", c=MD),
                                      h_sq[u].rearrange("p (h c) -> p h c", c=MD),
                                      h_rstd[u].unsqueeze(2).broadcast_to([P, MH, MD]), ALU.mult)\
                       .then_inc(s["z2_done"], 1)
                for u in range(U):
                    dve.wait_ge(s["z2_done"], n + u + 2)
                    dve.wait_ge(s["xb_done"], n + u + 2)
                    dve.tensor_tensor(z[u], z[u], xb[u], ALU.add).then_inc(s["z_done"], 1)
                for u in range(U):
                    dve.wait_ge(s["z_done"], n + u + 2)
                    ln_stats(ln + u + 1, u, z[u])
                for u in range(U):
                    dve.wait_ge(s["r4_done"], n + u)
                    ln_apply(ln + u + 1, u, x2[u], z[u])
                for u in range(U):
                    dve.wait_ge(s["ln_done"], ln + u + 3)
                    ln_stats(ln + U + u + 1, u, x2[u])
                for u in range(U):
                    dve.wait_ge(xn_stored[u], 16 * t + 32)
                    ln_apply(ln + U + u + 1, u, xn[u], x2[u])
                for u in range(U):
                    rope(base["qk"] + n + u, u)
                for u in range(U):
                    copy_values(d + 5 + u, u, None)
                for u in range(U):
                    dve.wait_ge(s["rope_k_done"], n + u + 2)
                    spread_keys(u, rope_k[u], 0.0, "head16", s["k_copied"])
                for u in range(U):
                    softmax_shift(m + 2 + u + 1, u)
                for u in range(U):
                    normalise(m + 2 + u + 1, u)
                for u in range(U):
                    dve.wait_ge(s["out_done"], base["out"] + n + u + 2)
                    dve.tensor_tensor(y[u], scores_ps[:, u, 0, 0:P], x2[u], ALU.add).then_inc(s["y_done"], 1)
                for u in range(U):
                    dve.wait_ge(s["y_done"], base["out"] + n + u + 2)
                    ln_stats(ln + 2 * U + u + 1, u, y[u])
                for u in range(U):
                    ln_apply(ln + 2 * U + u + 1, u, xn[u], y[u])

            dve.wait_ge(late, 16 * len(late_loads))
            for k, at in enumerate((2, 4)):
                dve.tensor_copy(l_w[:, at, :].rearrange("p (g n) -> p g n", g=4),
                                l_raw[:, 32 * k:32 * k + 32].unsqueeze(1).broadcast_to([P, 4, 32]))
            dve.tensor_scalar(c_col[:, 2:3], c_col[:, 0:1], SCALE, None, ALU.mult).then_inc(w_ready, 1)
            dve.wait_ge(w_ready, W_READY + 1)
            rotate(l_w[:, 1, :], l_w[:, 0, :])
            rotate(l_w[:, 3, :], l_w[:, 2, :]).then_inc(w_ready, 1)

            links = [0]

            def link(ins):
                links[0] += 1
                ins.then_inc(route_chain, 1)
                dve.wait_ge(route_chain, links[0])

            def one_hot(dst, values, best, E):
                em = const("expert")[:, 0:E].unsqueeze(1).broadcast_to([P, NT, E])
                tmp = r_tmp[:, :, 0:E]
                link(dve.tensor_tensor(tmp, values, best.unsqueeze(2).broadcast_to([P, NT, E]), ALU.is_equal))
                link(dve.tensor_tensor(tmp, tmp, em, ALU.mult))
                link(dve.tensor_reduce(r_b[:], tmp, AX, ALU.min))
                link(dve.tensor_tensor(dst, em, r_b[:].unsqueeze(2).broadcast_to([P, NT, E]), ALU.is_equal))

            def route(n, E, logits, capped):
                gate, tmp, one, two, pos = (a[:, :, 0:E] for a in (r_gate, r_tmp, r_one, r_two, r_pos))
                wide = [P, NT, E]
                link(dve.tensor_reduce(r_a[:], logits[:], AX, ALU.max))
                dve.tensor_tensor(gate, logits[:], r_a[:].unsqueeze(2).broadcast_to(wide), ALU.subtract)\
                   .then_inc(route_shifted, 1)
                dve.wait_ge(route_exp, n)
                link(dve.tensor_reduce(r_a[:], gate, AX, ALU.add))
                link(dve.reciprocal(r_b[:], r_a[:]))
                link(dve.tensor_tensor(gate, gate, r_b[:].unsqueeze(2).broadcast_to(wide), ALU.mult))
                link(dve.tensor_reduce(weight[:, 0, :], gate, AX, ALU.max))
                one_hot(one, gate, weight[:, 0, :], E)
                link(dve.scalar_tensor_tensor(gate, one, -2.0, gate, ALU.mult, ALU.add))
                link(dve.tensor_reduce(weight[:, 1, :], gate, AX, ALU.max))
                one_hot(two, gate, weight[:, 1, :], E)
                dve.tensor_tensor(r_mask[:, 0:NT * E].rearrange("p (t e) -> p t e", e=E), one, two, ALU.add)\
                   .then_inc(route_masked, 1)
                dve.wait_ge(route_counted, n)
                tiles_in_bank = 512 // E
                scan = [r_scan, r_scan2]
                for c in range(-(-NT * E // 512)):
                    n_t = min(tiles_in_bank, NT - tiles_in_bank * c)
                    part = slice(tiles_in_bank * c, tiles_in_bank * c + n_t)
                    dve.tensor_copy(pos[:, part], scores_ps[:, 0, c, 0:n_t * E].rearrange("p (t e) -> p t e", e=E))
                    last = dve.tensor_copy(r_scan[:, part, 0:E],
                                           scores_ps[:, 1, c, 0:n_t * E].rearrange("p (t e) -> p t e", e=E))
                    link(last)
                dve.sem_inc(counts_read, 1)
                link(dve.tensor_tensor(pos, pos, r_scan[:, :, 0:E], ALU.subtract))
                step = 1
                while step < NT:
                    a, b = scan
                    dve.tensor_copy(b[:, 0:step, 0:E], a[:, 0:step, 0:E])
                    link(dve.tensor_tensor(b[:, step:NT, 0:E], a[:, step:NT, 0:E], a[:, 0:NT - step, 0:E], ALU.add))
                    scan = [b, a]
                    step *= 2
                total = scan[0]
                link(dve.scalar_tensor_tensor(pos, pos, -1.0, total[:, :, 0:E], ALU.add, ALU.add))
                if capped:
                    link(dve.tensor_scalar(tmp, pos, float(CAP), FAR, ALU.is_ge, ALU.mult))
                    link(dve.tensor_tensor(pos, pos, tmp, ALU.add))
                    region = const("region0")
                else:
                    link(dve.tensor_scalar(r_int[:], total[:, NT - 1, 0:E], float(P - 1), None, ALU.add))
                    link(dve.tensor_scalar(r_int[:], r_int[:], 7, 7, ALU.logical_shift_right,
                                           ALU.logical_shift_left))
                    link(dve.tensor_copy(r_cnt[:], r_int[:]))
                    link(dve.tensor_copy(r_end[:], r_cnt[:]))
                    ends, step = [r_end, r_cnt2], 1
                    while step < E:
                        a, b = ends
                        dve.tensor_copy(b[:, 0:step], a[:, 0:step])
                        link(dve.tensor_tensor(b[:, step:E], a[:, step:E], a[:, 0:E - step], ALU.add))
                        ends = [b, a]
                        step *= 2
                    end = ends[0]
                    link(dve.tensor_tensor(r_base[:], end[:], r_cnt[:], ALU.subtract))
                    link(dve.tensor_tensor(r_le, end[:].unsqueeze(1).broadcast_to([P, NJ, E]),
                                           const("tile_start").unsqueeze(2).broadcast_to([P, NJ, E]), ALU.is_le))
                    link(dve.tensor_reduce(r_ej[:], r_le, AX, ALU.add))
                    link(dve.tensor_scalar(expert_of[:], r_ej[:], float(E - 1), None, ALU.min))
                    region = r_base[:]
                link(dve.tensor_tensor(pos, pos, region.unsqueeze(1).broadcast_to(wide), ALU.add))
                for k, hot in enumerate((one, two)):
                    link(dve.tensor_tensor(tmp, hot, pos, ALU.mult))
                    link(dve.tensor_reduce(slot_f[:, k, :], tmp, AX, ALU.add))
                n_slots = NSLOT0 if capped else NSLOT1
                if capped:
                    link(dve.tensor_scalar(slot_put[:], slot_f[:], 0.0, None, ALU.add))
                    link(dve.scalar_tensor_tensor(weight[:], slot_f[:], FAR / 2, weight[:], ALU.is_lt, ALU.mult))
                else:
                    link(dve.tensor_scalar(r_slot[:], slot_f[:], 0.0, None, ALU.add))
                    link(dve.tensor_scalar(r_low[:], r_slot[:], P - 1, None, ALU.bitwise_and))
                    link(dve.tensor_scalar(r_slot[:], r_slot[:], 7, None, ALU.logical_shift_right))
                    link(dve.scalar_tensor_tensor(slot_put[:], r_low[:], float(NJ), r_slot[:], ALU.mult, ALU.add))
                    link(dve.tensor_tensor(r_a[:], weight[:, 0, :], weight[:, 1, :], ALU.add))
                    link(dve.tensor_scalar(r_a[:], r_a[:], 1e-9, None, ALU.max))
                    link(dve.reciprocal(r_b[:], r_a[:]))
                    link(dve.tensor_tensor(weight[:], weight[:], r_b[:].unsqueeze(1).broadcast_to([P, 2, NT]), ALU.mult))
                link(dve.tensor_scalar(slot_get[:, :, 0:NT], slot_f[:], float(n_slots - 1), None, ALU.min))

            dve.wait_ge(desk_empty, BASE[5]["desk"] + 1)
            route(1, E0, logits0, True)
            dve.sem_inc(routed, 1)

            with dve.Fori(0, E0 // 2) as r:
                for i in range(2 * GE):
                    w, u, q = i // GE, i % 2, 2 * GE * r + i
                    dve.wait_ge(s["down_done"], q + 3)
                    dve.wait_ge(e_stored[u], 16 * (GE * r + i // 2) + 16)
                    dve.wait_ge(e_loaded[w], 64 * r + 64)
                    dve.tensor_tensor(e_out[u].rearrange("p (j d) -> p j d", d=D),
                                      (heads_ps, desk_ps)[u][:, 0:GS].rearrange("p (j d) -> p j d", d=D),
                                      e_b2[w][:].unsqueeze(1).broadcast_to([P, J, D]), ALU.add)\
                       .then_inc(s["e_out_done"], 1)
                    if i % GE == GE - 1:
                        dve.wait_ge(s["e_out_done"], q + 3)
                        dve.sem_inc(s["expert_done"], 1)

            def combine(n, u, loads, dst):
                dve.wait_ge(got_loaded[u], loads)
                dve.wait_ge(s["weights_got"], n + 2)
                dve.scalar_tensor_tensor(y[u], got[u][:, 0:D], got_w[u][:, 0:1], x_in[u], ALU.mult, ALU.add)\
                   .then_inc(s["c1_done"], 1)
                dve.wait_ge(s["c1_done"], n + 2)
                dve.scalar_tensor_tensor(dst[u], got[u][:, D:2 * D], got_w[u][:, 1:2], y[u], ALU.mult, ALU.add)\
                   .then_inc(s["c2_done"], 1)

            def get_weights(n, tile, u):
                dve.tensor_copy(got_w[u], weight[:, :, bass.ds(tile, 1)].rearrange("p k t -> p (k t)"))\
                   .then_inc(s["weights_got"], 1)

            base = BASE[5]
            with dve.Fori(0, NT // U) as r:
                t = U * r
                n = t + 1
                d = base["desk"] + USES[5] * r
                m = base["att"] + 2 * t
                ln = base["ln"] + 3 * t
                o2 = base["out"] + 2 * t
                for u in range(U):
                    get_weights(n + u, t + u, u)
                for u in range(U):
                    dve.wait_ge(in_loaded[u], 16 * NT + 8 * t + 16)
                    combine(n + u, u, 16 * t + 32, z)
                for u in range(U):
                    dve.wait_ge(s["c2_done"], n + u + 2)
                    ln_stats(ln + u + 1, u, z[u])
                for u in range(U):
                    ln_apply(ln + u + 1, u, x4[u], z[u])
                for u in range(U):
                    rope(o2 + u + 1, u)
                for u in range(U):
                    copy_values(d + 2 + u, u, None)
                for u in range(U):
                    dve.wait_ge(s["rope_k_done"], NT + n + u + 2)
                    spread_keys(u, rope_k[u], 0.0, "head16", s["k_copied"])
                for u in range(U):
                    softmax_shift(m + u + 1, u)
                for u in range(U):
                    normalise(m + u + 1, u)
                for u in range(U):
                    dve.wait_ge(s["out_done"], o2 + u + 3)
                    dve.tensor_tensor(y[u], scores_ps[:, u, 0, 0:P], x4[u], ALU.add).then_inc(s["y_done"], 1)
                for u in range(U):
                    copy_values(d + 7 + u, u, c_row[:, 0, :])
                for u in range(U):
                    dve.wait_ge(s["y_done"], o2 + u + 3)
                    ln_stats(ln + U + u + 1, u, y[u])
                for u in range(U):
                    dve.wait_ge(s["x5b_done"], n + u)
                    ln_apply(ln + U + u + 1, u, x5[u], y[u])
                for u in range(U):
                    dve.wait_ge(s["qk_done"], base["qk"] + 2 * t + 2 + u + 3)
                    spread_keys(u, scores_ps[:, u, 1, 0:P], c_col[:, 1:2], "head16", s["k_copied"])
                for u in range(U):
                    mm = m + 2 + u + 1
                    dve.wait_ge(s["turn1_done"], mm)
                    dve.wait_ge(s["fm_done"], n + u + 2)
                    for g in range(NR):
                        dve.wait_ge(s["scores_done"], 2 * mm + g + 3)
                        pv = probs[u][:, 512 * g:512 * g + 512].rearrange("p (h t) -> p h t", t=S)
                        best = row_max[u][:, 8 * g:8 * g + 8]
                        dve.tensor_tensor(pv, scores_ps[:, u, g, :].rearrange("p (h t) -> p h t", t=S),
                                          fm[u].unsqueeze(1).broadcast_to([P, 8, S]), ALU.add)\
                           .then_inc(s["biased"], 1)
                        dve.wait_ge(s["biased"], 2 * (n + u) + g + 3)
                        dve.tensor_reduce(best, pv, AX, ALU.max).then_inc(s["max_done"], 1)
                        dve.wait_ge(s["max_done"], 2 * mm + g + 3)
                        dve.tensor_tensor(pv, pv, best.unsqueeze(2).broadcast_to([P, 8, S]), ALU.subtract)\
                           .then_inc(s["shifted"], 1)
                for u in range(U):
                    normalise(m + 2 + u + 1, u)
                for u in range(U):
                    dve.wait_ge(s["out_done"], o2 + 2 + u + 3)
                    dve.wait_ge(s["x5b_done"], n + u + 2)
                    dve.tensor_tensor(y[u], scores_ps[:, u, 0, 0:P], x5b[u], ALU.add).then_inc(s["y_done"], 1)
                for u in range(U):
                    dve.wait_ge(s["y_done"], o2 + 2 + u + 3)
                    ln_stats(ln + 2 * U + u + 1, u, y[u])
                for u in range(U):
                    dve.wait_ge(x6_stored[u], 8 * t + 16)
                    ln_apply(ln + 2 * U + u + 1, u, x6[u], y[u])
                for u in range(U):
                    dve.wait_ge(desk_full, d + 15 + u + 1)
                    dve.tensor_tensor(logits1[:, bass.ds(t + u, 1), :].rearrange("p t e -> p (t e)"),
                                      desk_ps[:, 0:E1], rt_row[:], ALU.add).then_inc(desk_empty, 1)

            dve.wait_ge(desk_empty, BASE[5]["desk"] + USES[5] * NT // U + 1)
            route(2, E1, logits1, False)
            dve.sem_inc(routed, 1)
            def expert(r, w, i):
                return dve.value_load(expert_of[0:1, bass.ds(V * r + 2 * w + i, 1)], min_val=0, max_val=E1 - 1)

            def cols(i):
                return slice(P * i, P * i + P)

            with dve.Fori(0, NJ // V) as r:
                for w in range(2):
                    q = 2 * r + w + 1
                    experts = [expert(r, w, i) for i in range(2)]
                    dve.wait_ge(s["o_up"], q + 2)
                    for i, e in enumerate(experts):
                        last = dve.tensor_tensor(o_h[w][:, cols(i)], scores_ps[:, w, 0, cols(i)],
                                                 o_b1[:, bass.ds(e, 1), :].rearrange("p e h -> p (e h)"), ALU.add)
                    last.then_inc(s["o_h_done"], 1)
                    dve.wait_ge(s["o_h_done"], q + 2)
                    for i in range(2):
                        last = dve.bn_stats(o_stat[w][:, 6 * i:6 * i + 6], o_h[w][:, cols(i)])
                    last.then_inc(s["o_stat_done"], 1)
                    q2 = dve.to_reg(q + 2)
                    dve.wait_ge(w_turned, 1)
                    dve.wait_ge(s["o_stat_done"], q2)
                    for i in range(2):
                        last = dve.bn_aggr(o_mv[w][:, 2 * i:2 * i + 2], o_stat[w][:, 6 * i:6 * i + 6])
                    last.then_inc(s["o_mv_done"], 1)
                    dve.wait_ge(s["o_mv_done"], q + 2)
                    dve.tensor_scalar(o_veps[w], o_mv[w].rearrange("p (i k) -> p k i", k=2)[:, 1, :], EPS_LN, None,
                                      ALU.add).then_inc(s["o_veps_done"], 1)
                for w in range(2):
                    q = 2 * r + w + 1
                    dve.wait_ge(s["o_rstd_done"], q + 2)
                    dve.wait_ge(s["o_hturned"], q)
                    for i in range(2):
                        last = dve.tensor_scalar(o_hn[w][:, cols(i)], o_h[w][:, cols(i)], o_mv[w][:, 2 * i:2 * i + 1],
                                                 o_rstd[w][:, i:i + 1], ALU.subtract, ALU.mult)
                    last.then_inc(s["o_hn_done"], 1)
                for w in range(2):
                    q = 2 * r + w + 1
                    experts = [expert(r, w, i) for i in range(2)]
                    dve.wait_ge(s["o_down"], q + 2)
                    dve.wait_ge(o_stored[w], 16 * r + 16)
                    for i, e in enumerate(experts):
                        last = dve.tensor_tensor(o_out[w][:, cols(i)], (heads_ps, desk_ps)[w][:, cols(i)],
                                                 o_b2[:, bass.ds(e, 1), :].rearrange("p e h -> p (e h)"), ALU.add)
                    last.then_inc(s["o_out_done"], 1)

            with dve.Fori(0, NT // U) as r:
                t = U * r
                n = NT + t + 1
                for u in range(U):
                    get_weights(n + u, t + u, u)
                for u in range(U):
                    dve.wait_ge(z_loaded[u], 8 * t + 16)
                    combine(n + u, u, 16 * NT + 32 + 16 * t + 32, z)
                for u in range(U):
                    dve.wait_ge(s["c2_done"], n + u + 2)
                    ln_stats(7 * NT + t + u + 1, u, z[u])
                for u in range(U):
                    dve.wait_ge(z_stored[u], 8 * t + 16)
                    ln_apply(7 * NT + t + u + 1, u, x_out[u], z[u])

        @block.gpsimd
        def _(pool):
            for k in pool_done:
                pool.sem_inc(s[k], CREDIT)
            pool.memset(minus_half[:], -0.5)
            pool.memset(zeros_i[:], 0).then_inc(zero_sem, 1)
            pool.memset(slot_get[:], 0)
            pool.memset(at1_all[:], 0)
            pool.iota(token[:], [[P, NT]], base=0, channel_multiplier=1)
            for u in range(U):
                pool.memset(pad_T[u], 0.0)
                pool.memset(m_vbd[u], 0.0)
                pool.memset(v_bd[u], 0.0).then_inc(zeroed, 1)
            pool.wait_ge(zeroed, U)
            pool.wait_ge(loaded, 16 * len(w_loads))
            for u in range(U):
                vv = v_bd[u].rearrange("p (g b h c) -> p g b h c", g=8, b=NB, h=2)
                for par in range(2):
                    last = pool.memset(vv[S * par:S * par + S, :, :, par, HD:HD + 1], 1.0)
                mvv = m_vbd[u].rearrange("p (g b h c) -> p g b h c", g=4, b=NB, h=2)
                for par in range(2):
                    last = pool.memset(mvv[S * par:S * par + S, :, :, par, MD:MD + 1], 1.0)
            last.then_inc(zeroed, 1)
            for j in range(HOPS):
                pool.indirect_dma_start(out=hop_rows[:, j, :], out_offset=None, in_=T["L0_xattn_rpe"],
                                        in_offset=bass.IndirectOffsetOnAxis(ap=hop_at[:, j:j + 1], axis=0))\
                    .then_inc(hop_gathered, 16)

            def ln_rstd(o, u):
                pool.wait_ge(s["veps_done"], o + 2)
                pool.tensor_tensor(rstd[u], veps[u], minus_half[:, 0:1], ALU.pow).then_inc(s["rstd_done"], 1)

            with pool.Fori(0, NT // U) as r:
                t = U * r
                d = USES[1] * r
                for u in range(U):
                    pool.wait_ge(in_loaded[u], 8 * t + 16)
                    pool.wait_ge(desk_full, d + 1)
                    pool.wait_ge(s["y_done"], t + u + 1)
                    pool.tensor_tensor(x_res[u], x_in[u], a_row[:, 1, :], ALU.add).then_inc(s["x_res_done"], 1)
                for u in range(U):
                    ln_rstd(t + u + 1, u)

            base = BASE[3]
            with pool.Fori(0, NT // U) as r:
                t = U * r
                n = t + 1
                d = base["desk"] + USES[3] * r
                m = base["att"] + 2 * t
                ln = base["ln"] + 3 * t
                for u in range(U):
                    pool.wait_ge(desk_empty, d + 2)
                    pool.wait_ge(s["scores_done"], m + u + 1)
                    pool.tensor_tensor(k_bd[u][:, 0:MH * P].rearrange("p (h t) -> p h t", h=MH),
                                       c_T[u].unsqueeze(1).broadcast_to([P, MH, P]),
                                       const("head8q").unsqueeze(2).broadcast_to([P, MH, P]), ALU.mult)\
                        .then_inc(s["k_copied"], 2)
                for u in range(U):
                    pool.wait_ge(s["ln_done"], ln - 2 * U + u + 1 + U)
                    pool.tensor_tensor(xb[u], x_in[u], m_row[:, 1, :], ALU.add).then_inc(s["xb_done"], 1)
                for u in range(U):
                    pool.wait_ge(s["g_key_done"], n + u + 2)
                    pool.tensor_tensor(g_diag[u].rearrange("p (h t) -> p h t", t=S),
                                       g_key[u].unsqueeze(2).broadcast_to([P, MH, S]),
                                       const("diag64").unsqueeze(1).broadcast_to([P, MH, S]), ALU.mult)\
                        .then_inc(s["g_diag_done"], 1)
                for u in range(U):
                    pool.wait_ge(s["h_veps_done"], n + u + 2)
                    pool.tensor_tensor(h_rstd[u], h_veps[u], minus_half[:, 0:8], ALU.pow)\
                        .then_inc(s["h_rstd_done"], 1)
                for u in range(U):
                    ln_rstd(ln + u + 1, u)
                for u in range(U):
                    ln_rstd(ln + U + u + 1, u)
                for u in range(U):
                    pool.wait_ge(s["rope_done"], n + u + 2)
                    pool.tensor_tensor(q_T[u], rope_c[u][:, 0:P], rope_s[u][:, 0:P], ALU.add)\
                        .then_inc(s["q_copied"], 1)
                    pool.tensor_tensor(rope_k[u], rope_c[u][:, P:2 * P], rope_s[u][:, P:2 * P], ALU.add)\
                        .then_inc(s["rope_k_done"], 1)
                for u in range(U):
                    pool.wait_ge(s["y_done"], base["out"] + n + u + 2)
                    pool.wait_ge(xn_stored[u], 16 * t + 32)
                    pool.tensor_tensor(r4[u], y[u], x2[u], ALU.add).then_inc(s["r4_done"], 1)
                for u in range(U):
                    ln_rstd(ln + 2 * U + u + 1, u)

            def put(n0):
                table, n_slots = (token_of0, NSLOT0) if n0 == 0 else (token_of1, NSLOT1)
                with pool.Fori(0, NT // U) as r:
                    for u in range(U):
                        pool.wait_ge(s["put_free"], n0 + U * r + u + 1)
                        pool.tensor_copy(put_at[u], slot_put[:, :, bass.ds(U * r + u, 1)].rearrange("p k t -> p (k t)"))
                        pool.tensor_copy(put_tok[u], token[:, bass.ds(U * r + u, 1)]).then_inc(s["put_ready"], 1)
                        nu = pool.to_reg(n0 + U * r + u + 3)
                        pool.wait_ge(table_sem, 32)
                        pool.wait_ge(s["put_ready"], nu)
                        for k in range(2):
                            pool.indirect_dma_start(
                                out=table, out_offset=bass.IndirectOffsetOnAxis(ap=put_at[u][:, k:k + 1], axis=0),
                                in_=put_tok[u], in_offset=None, bounds_check=n_slots - 1, oob_is_err=False)\
                                .then_inc(put_done[u], 16)

            for u in range(U):
                pool.wait_ge(xn_stored[u], 32 * (NT // U) + 32)
            pool.wait_ge(routed, 1)
            put(0)

            def load_expert(r, w):
                pool.wait_ge(s["expert_done"], 2 * r + w + 1)
                e = 2 * r + w
                for dst, src in (
                    (e_w1[w][:], T["L0_ffn_W1"][bass.ds(e, 1)].rearrange("e c f -> c (e f)")),
                    (e_w2[w][:], T["L0_ffn_W2"][bass.ds(e, 1)].rearrange("e (f p) d -> p (e f) d", p=P)),
                    (e_b1[w][:], T["L0_ffn_b1"][bass.ds(e, 1)].rearrange("e (f p) -> p (e f)", p=P)),
                    (e_b2[w][:], T["L0_ffn_b2"][bass.ds(e, 1)].rearrange("e d -> (e d)").partition_broadcast(P)),
                ):
                    pool.dma_start(dst, src, allow_slow_non_contiguous=True).then_inc(e_loaded[w], 16)

            pool.wait_ge(at_loaded, 16)
            with pool.Fori(0, E0 // 2) as r:
                for i in range(2 * GE):
                    u, q = i % 2, 2 * GE * r + i
                    if i % GE == 0:
                        load_expert(r, i // GE)
                    pool.wait_ge(s["e_turned"], q + 1)
                    pool.tensor_copy(e_at[u], at0_all[:, bass.ds(q, 1), :].rearrange("p q j -> p (q j)"))\
                        .then_inc(s["at_done"], 1)
                    nq = pool.to_reg(q + 3)
                    pool.wait_ge(routed, 1)
                    pool.wait_ge(s["at_done"], nq)
                    for j in range(J):
                        pool.indirect_dma_start(out=e_in[u][:, P * j:P * j + P], out_offset=None, in_=xn_dram,
                                                in_offset=bass.IndirectOffsetOnAxis(ap=e_at[u][:, j:j + 1], axis=0))\
                            .then_inc(e_in_loaded[u], 16)

            def get(n, c, tile, u, rows):
                pool.wait_ge(s["c2_done"], c + 2)
                pool.tensor_copy(got_at[u], slot_get[:, :, bass.ds(tile, 1)].rearrange("p k t -> p (k t)"))\
                    .then_inc(s["got_ready"], 1)
                nu = pool.to_reg(n + 2)
                pool.wait_ge(routed, 1)
                pool.wait_ge(s["got_ready"], nu)
                for k in range(2):
                    pool.indirect_dma_start(out=got[u][:, D * k:D * k + D], out_offset=None, in_=rows,
                                            in_offset=bass.IndirectOffsetOnAxis(ap=got_at[u][:, k:k + 1], axis=0))\
                        .then_inc(got_loaded[u], 16)

            for u in range(U):
                pool.wait_ge(e_stored[u], 16 * GE * E0 // 2 + 16)
            base = BASE[5]
            for u in range(U):
                get(u + 1, u + 1 - U, u, u, moe0)
            with pool.Fori(0, NT // U) as r:
                t = U * r
                n = t + 1
                ln = base["ln"] + 3 * t
                m = base["att"] + 2 * t
                for u in range(U):
                    ln_rstd(ln + u + 1, u)
                for u in range(U):
                    pool.wait_ge(s["rope_done"], NT + n + u + 2)
                    pool.tensor_tensor(q_T[u], rope_c[u][:, 0:P], rope_s[u][:, 0:P], ALU.add)\
                        .then_inc(s["q_copied"], 1)
                    pool.tensor_tensor(rope_k[u], rope_c[u][:, P:2 * P], rope_s[u][:, P:2 * P], ALU.add)\
                        .then_inc(s["rope_k_done"], 1)
                for u in range(U):
                    get(n + U + u, n + u, t + U + u, u, moe0)
                for u in range(U):
                    pool.wait_ge(c_loaded[u], 32 * NT + 24 * t + 48)
                    pool.wait_ge(s["biased"], 2 * (n + u))
                    pool.tensor_tensor(fm[u], fm_in[u][:, 0:S], fm_in[u][:, S:2 * S], ALU.add)\
                        .then_inc(s["fm_done"], 1)
                for u in range(U):
                    ln_rstd(ln + U + u + 1, u)
                for u in range(U):
                    pool.wait_ge(s["ln_done"], ln + U + u + 3)
                    pool.wait_ge(s["y_done"], base["out"] + 2 * t + u + 1)
                    pool.tensor_tensor(x5b[u], x5[u], c_row[:, 1, :], ALU.add).then_inc(s["x5b_done"], 1)
                for u in range(U):
                    ln_rstd(ln + 2 * U + u + 1, u)

            pool.wait_ge(routed, 2)
            put(NT)
            for u in range(U):
                pool.wait_ge(x6_stored[u], 16 * (NT // U) + 16)
            pool.wait_ge(at_loaded, 32)

            def get_slots(r, w):
                q = 2 * r + w + 1
                pool.wait_ge(s["o_turned"], q)
                pool.tensor_copy(o_at[w], at1_all[:, bass.ds(V * r + 2 * w, 2)]).then_inc(s["at_done"], 1)
                nq = pool.to_reg(NSLOT0 // GS + q + 2)
                pool.wait_ge(routed, 2)
                pool.wait_ge(s["at_done"], nq)
                for i in range(2):
                    pool.indirect_dma_start(out=o_in[w][:, P * i:P * i + P], out_offset=None, in_=x6_dram,
                                            in_offset=bass.IndirectOffsetOnAxis(ap=o_at[w][:, i:i + 1], axis=0))\
                        .then_inc(o_in_loaded[w], 16)

            for w in range(2):
                get_slots(0, w)
            with pool.Fori(0, NJ // V) as r:
                for w in range(2):
                    get_slots(r + 1, w)
                for w in range(2):
                    pool.wait_ge(s["o_veps_done"], 2 * r + w + 3)
                    pool.tensor_tensor(o_rstd[w], o_veps[w], minus_half[:, 0:2], ALU.pow)\
                        .then_inc(s["o_rstd_done"], 1)
            for u in range(U):
                pool.wait_ge(o_stored[u], 16 * (NJ // V) + 16)
            for u in range(U):
                get(NT + U + u + 1, NT + u + 1 - U, u, u, moe1)
            with pool.Fori(0, NT // U) as r:
                t = U * r
                for u in range(U):
                    get(NT + 2 * U + t + u + 1, NT + t + u + 1, t + U + u, u, moe1)
                for u in range(U):
                    ln_rstd(7 * NT + t + u + 1, u)


def launch_args(nc, inputs):
    cf, cb = constants(inputs["x"].shape[0] * S)
    arrays, T = {}, {}
    given = dict(inputs)
    given["consts"] = np.concatenate(list(cf.values()), axis=1)
    given["consts16"] = np.concatenate(list(cb.values()), axis=1).astype(np.float32)
    for name, a in given.items():
        a = np.ascontiguousarray(a)
        arrays[f"in_{name}"] = a
        T[name] = nc.dram_tensor(f"in_{name}", a.shape, mybir.dt.from_np(a.dtype), kind="ExternalInput").ap()
    return arrays, T


def kernel(**inputs):
    import concourse.bacc as bacc
    from concourse.bass_utils import run_bass_kernel_spmd

    nc = bacc.Bacc("TRN2", target_bir_lowering=False, num_devices=1)
    arrays, T = launch_args(nc, inputs)
    out = nc.dram_tensor("out_0", inputs["x"].shape, F32, kind="ExternalOutput").ap()
    build(nc, T, out)
    return run_bass_kernel_spmd(nc, [arrays], core_ids=[0]).results[0]["out_0"]
```

```python
from contextlib import ExitStack

import numpy as np
import concourse.bass as bass
from concourse import mybir

F32 = mybir.dt.float32
BF16 = mybir.dt.bfloat16
I32 = mybir.dt.int32
U32 = mybir.dt.uint32
ACT = mybir.ActivationFunctionType
ALU = mybir.AluOpType
AX = mybir.AxisListType.X

P = 128
S = 64
D = 128
NB = P // S
H = 16
HD = D // H
MH = 8
MD = D // MH
NR = 2
V = 4
U = 2
CREDIT = 2
E0, F0 = 8, 4
E1 = 16
BELOW = 64.0
FAR = 2.0 ** 20
EPS_LN = 1e-5
NEG = -1e30
SCALE = HD ** -0.5


def capacity(n_tokens):
    return -(-2 * n_tokens // E0)


def slot_tiles(n_tokens):
    return 2 * n_tokens // P + E1


def constants(n_tokens):
    p = np.arange(P)
    same = (p[:, None] // S) == (p[None, :] // S)
    t = np.arange(S)
    half = HD // 2
    inv_freq = (1.0 / np.float32(10000.0) ** (np.arange(half, dtype=np.float32) / half)).astype(np.float32)
    ang = (p % S).astype(np.float32)[None, :] * inv_freq[p % half][:, None]
    f = {
        "ident": np.eye(P),
        "tri2": same & (p[:, None] <= p[None, :]),
        "ones2": same,
        "diag64": (p[:, None] % S) == t[None, :],
        "head16": p[:, None] // HD == np.arange(H)[None, :],
        "head8": p[:, None] // MD == np.arange(MH)[None, :],
        "head4": (p[:, None] % 64) // MD == np.arange(64 // MD)[None, :],
        "cos": np.cos(ang.astype(np.float64)),
        "sin": np.sin(ang.astype(np.float64)),
    }
    f["head8q"] = f["head8"] * MD ** -0.5
    b = {"tri16": p[:, None] <= p[None, :], "ones16": np.ones((P, P)), "ident16": np.eye(P), "causal16": np.where(t[None, :] <= (p % S)[:, None], 0.0, NEG)}
    f["expert"] = np.tile(np.arange(E1) - BELOW, (P, 1))
    f["region0"] = np.tile(np.arange(E0) * capacity(n_tokens), (P, 1))
    n = slot_tiles(n_tokens)
    f["tile_start"] = np.tile(np.arange(n) * P, (P, 1))
    return ({k: v.astype(np.float32) for k, v in f.items()}, b)


def offsets(pieces):
    at, out = 0, {}
    for name, a in pieces.items():
        out[name] = (at, a.shape[1])
        at += a.shape[1]
    return out, at


def build(nc, T, out):
    B = T["x"].shape[0]
    NT = B * S // P
    cf, cb = constants(B * S)
    cf_at, cf_n = offsets(cf)
    cb_at, cb_n = offsets(cb)

    with ExitStack() as ctx:
        def sb(name, shape, dt=F32):
            return ctx.enter_context(nc.sbuf_tensor(name, shape, dt))

        def ps(name, shape, dt=F32):
            return ctx.enter_context(nc.psum_tensor(name, shape, dt))

        def sem(name):
            return ctx.enter_context(nc.semaphore(name))

        def dram(name, shape, dt=F32):
            return nc.dram_tensor(name, shape, dt, kind="Internal").ap()

        consts = sb("consts", [P, cf_n])
        consts16 = sb("consts16", [P, cb_n], BF16)

        def const(name):
            at, n = cf_at[name]
            return consts[:, at:at + n]

        def const16(name):
            at, n = cb_at[name]
            return consts16[:, at:at + n]

        ident, ident16, causal16 = const("ident"), const16("ident16"), const16("causal16")

        scores_ps = ps("scores_ps", [P, U, NR, 512])
        turned_ps = ps("turned_ps", [P, 2, 512])
        heads_ps = ps("heads_ps", [P, 512])
        desk_ps = ps("desk_ps", [P, 512])
        trans_ps = desk_ps[:, 0:P]
        setup_ps = scores_ps[:].rearrange("p u g (k n) -> p (u g k) n", n=P)

        whole = {}

        def both(name, n, dt=F32):
            b = whole[name] = sb(name, [P, U, n], dt)
            return [b[:, u, :] for u in range(U)]

        x_in, x_out, x_res = both("x_in", D), both("x_out", D), both("x_res", D)
        x_T, q_T, o_T, ctx_o, y = both("x_T", P), both("q_T", P), both("o_T", P), both("ctx_o", D), both("y", D)
        turned, probs = both("turned", H * S), both("probs", H * S)
        k_bd, v_bd = both("k_bd", H * P), both("v_bd", 8 * NB * 2 * (HD + 1))
        row_max, recip = both("row_max", H), both("recip", H)
        pad_T = both("pad_T", NB * (S + 2))
        stat, mv, veps, rstd = both("stat", 6), both("mv", 2), both("veps", 1), both("rstd", 1)
        minus_half = sb("minus_half", [P, 16])

        w_raw = sb("w_raw", [P, 7, P])
        a_w = sb("a_w", [P, 7, P])
        a_col = sb("a_col", [P, 3])
        a_row = sb("a_row", [P, 2, D])

        HOPS = S // 2
        hop_at = sb("hop_at", [P, HOPS], I32)
        assert HOPS == 2 * E1
        hop_rows = sb("hop_rows", [P, HOPS, D])
        hop_T = sb("hop_T", [P, HOPS, P])
        o_w1, o_w2 = hop_rows[:, 0:E1, :], hop_rows[:, E1:2 * E1, :]
        o_b1, o_b2 = hop_T[:, 0:E1, :], hop_T[:, E1:2 * E1, :]
        GS = min(512, capacity(B * S))
        NJ = slot_tiles(B * S)
        pool_n = max(NJ * E1, 6 * V * P)
        shared = sb("shared", [P, max(U * F0 * GS, pool_n, U * (2 * P + 12 * S))])

        def views(at, n):
            return [shared[:, at + n * u:at + n * u + n] for u in range(U)]
        hx_in, hx_T, hop_bd, hop_out = (views(U * at, n) for at, n in (
            (0, D), (D, P), (D + P, 4 * S), (D + P + 4 * S, MH * S)))
        g_raw, g_w = sb("gate_raw", [2 * MH, 3, D]), sb("gate_w", [P, 3, 2 * MH])
        g_row = sb("gate_bias", [P, 2 * MH])
        m_row = sb("mlstm_ln", [P, 2, D])
        c_in, c_two, hop_in = both("c_in", D), both("c_two", NB * D), both("hop_in", MH * S)
        c_T = both("c_T", P)
        gates, neg_abs, exp_abs, soft = both("gates", 16), both("neg_abs", 8), both("exp_abs", 8), both("soft", 8)
        log_f, csum, g_key = both("log_f", 8), both("csum", 8), both("g_key", 8)
        g_diag, decay = both("g_diag", MH * S), both("decay", MH * S)
        cmax, floor, denom, denom2, denom3 = (both(k, 8) for k in ("cmax", "floor", "denom", "denom2", "denom3"))
        m_vbd = both("m_vbd", 4 * NB * 2 * (MD + 1))
        h_sum, h_mid, h_sq, h_var = both("h_sum", 8), both("h_mid", D), both("h_sq", D), both("h_var", 8)
        h_veps, h_rstd, z = both("h_veps", 8), both("h_rstd", 8), both("z", D)
        xb = both("xb", D)
        f_raw = sb("ffn_qkv_raw", [P, 3 * D])
        f_w = sb("ffn_attn_w", [P, 6, D])
        f_col = sb("ffn_ln", [P, 4])
        f_gate = sb("ffn_gate", [P, 8])
        x2, xn, r4 = both("x2", D), both("xn", D), both("r4", D)
        h_T = both("h_T", P)
        rope_c, rope_s, rope_k = both("rope_c", 2 * P), both("rope_s", 2 * P), both("rope_k", P)
        logits0 = sb("logits0", [P, NT, 8])

        NSLOT0 = E0 * capacity(B * S)
        NSLOT1 = NJ * P
        assert NT * E1 <= H * S
        r_gate, r_tmp, r_pos = (sb(k, [P, NT, E1]) for k in ("r_gate", "r_tmp", "r_pos"))
        r_scan, r_scan2, r_one, r_two = (a[:, 0:NT * E1].rearrange("p (t e) -> p t e", e=E1) for a in turned + probs)
        r_mask = sb("r_mask", [P, NT * E1], BF16)
        r_a, r_b = sb("r_a", [P, NT]), sb("r_b", [P, NT])
        r_cnt, r_cnt2, r_end, r_base = (sb(k, [P, E1]) for k in ("r_cnt", "r_cnt2", "r_end", "r_base"))
        r_int = sb("r_int", [P, E1], I32)
        r_le, r_ej = shared[:, 0:NJ * E1].rearrange("p (j e) -> p j e", e=E1), sb("r_ej", [P, NJ])
        assert NJ % V == 0
        expert_of = sb("expert_of", [P, NJ], I32)
        slot_f, weight = sb("slot_f", [P, 2, NT]), sb("weight", [P, 2, NT])
        slot_put, slot_get = sb("slot_put", [P, 2, NT], U32), sb("slot_get", [P, 2, NT + V], U32)
        r_slot, r_low = sb("r_slot", [P, 2, NT], I32), sb("r_low", [P, 2, NT], I32)
        token = sb("token", [P, NT], I32)
        put_at, put_tok = both("put_at", 2, U32), both("put_tok", 1, I32)
        zeros_i = sb("zeros_i", [P, NSLOT1 // P if NSLOT1 > NSLOT0 else NSLOT0 // P], I32)
        CAP = capacity(B * S)
        GE, J = CAP // GS, GS // P
        assert CAP % GS == 0 and GS % P == 0 and (GE == 1 or GE % 2 == 0)
        e_w1 = [sb(f"e_w1{w}", [P, F0 * P]) for w in range(2)]
        e_w2 = [sb(f"e_w2{w}", [P, F0, D]) for w in range(2)]
        e_b1 = [sb(f"e_b1{w}", [P, F0]) for w in range(2)]
        e_b2 = [sb(f"e_b2{w}", [P, D]) for w in range(2)]
        at0_all, at1_all = sb("at0_all", [P, NSLOT0 // GS, J], I32), sb("at1_all", [P, NJ + V], I32)
        e_at, e_in, e_T, e_out = both("e_at", J, I32), both("e_in", GS), both("e_T", GS), both("e_out", GS)
        e_mid = [a.rearrange("p (f n) -> p f n", f=F0) for a in views(0, F0 * GS)]
        l_raw = sb("l_raw", [P, 2 * 32])
        l_w = sb("l_w", [P, 6, D])
        c_w = sb("c_w", [P, 4, D])
        c_col, c_row = sb("c_col", [P, 3]), sb("c_row", [P, 2, D])
        rt_w, rt_row = sb("rt_w", [P, E1]), sb("rt_row", [P, E1])
        got, got_at, got_w = both("got", 2 * D), both("got_at", 2, U32), both("got_w", 2)
        fm_in, fm = both("fm_in", 2 * S), both("fm", S)
        x4, x5, x5b, x6 = both("x4", D), both("x5", D), both("x5b", D), both("x6", D)
        logits1 = sb("logits1", [P, NT, E1])
        o_g, o_b = sb("o_g", [P, E1]), sb("o_b", [P, E1])
        o_at = both("o_at", 2, I32)
        o_in, o_in_T, o_h, o_hn, o_g_T, o_out = (views(U * 2 * P * k, 2 * P) for k in range(6))
        far_got, far_at = views(0, 2 * 2 * D), both("far_at", 2 * 2, U32)
        far_got = [a[:, 2 * D * i:2 * D * i + 2 * D] for a in far_got for i in range(2)]
        far_at = [a[:, 2 * i:2 * i + 2] for a in far_at for i in range(2)]
        table_for = sb("table_for", [P, 1])
        o_stat, o_mv, o_veps, o_rstd = both("o_stat", 12), both("o_mv", 4), both("o_veps", 2), both("o_rstd", 2)

        loaded, w_turned, w_ready = sem("loaded"), sem("weights_turned"), sem("weights_ready")
        w_copied = sem("weights_copied")
        zeroed = sem("constants_set")
        dve_done = ["veps_done", "k_copied", "max_done", "shifted", "recip_done", "normed",  "y_done",
                    "stat_done", "mv_done", "ln_done"]
        act_done = ["q_copied", "exp_done", "turn0_copied", "turn1_copied"]
        pe_done = ["qk_done", "scores_done", "turn0_done", "turn1_done", "pv_done", "conv_done",
                   "out_done"]
        pool_done = ["x_res_done", "rstd_done"]
        s = {k: sem(k) for k in dve_done + act_done + pe_done + pool_done}
        desk_full, desk_empty = sem("desk_full"), sem("desk_empty")
        in_loaded = [sem(f"x_in_loaded{u}") for u in range(U)]
        x_stored = [sem(f"x_out_stored{u}") for u in range(U)]

        hop_idx, hop_gathered = sem("hop_index_loaded"), sem("hop_rows_gathered")
        hop_turned, hop_copied = sem("hop_turned"), sem("hop_copied")
        hx_loaded = [sem(f"hx_loaded{u}") for u in range(U)]
        hop_stored = [sem(f"hop_stored{u}") for u in range(U)]
        c_loaded = [sem(f"c_loaded{u}") for u in range(U)]
        xn_stored = [sem(f"xn_stored{u}") for u in range(U)]
        route_shifted, route_exp = sem("route_shifted"), sem("route_exp")
        route_masked, route_counted, route_chain = sem("route_masked"), sem("route_counted"), sem("route_chain")
        counts_read = sem("route_counts_read")
        zero_sem, table_sem, routed = sem("zeros_set"), sem("tables_cleared"), sem("routed")
        put_done = [sem(f"put_done{u}") for u in range(U)]
        e_loaded = [sem(f"e_weights_loaded{w}") for w in range(2)]
        e_in_loaded = [sem(f"e_in_loaded{u}") for u in range(U)]
        at_loaded = sem("slot_tables_loaded")
        e_stored = [sem(f"e_out_stored{u}") for u in range(U)]
        gelu_done, up_done = sem("gelu_done"), sem("up_done")
        got_loaded, x6_stored = ([sem(f"{k}{u}") for u in range(U)] for k in ("got_loaded", "x6_stored"))
        far_loaded = [sem(f"far_loaded{k}") for k in range(V)]
        late = sem("late_weights_loaded")
        o_in_loaded, o_stored = ([sem(f"{k}{u}") for u in range(U)] for k in ("o_in_loaded", "o_stored"))
        z_loaded, z_stored = ([sem(f"{k}{u}") for u in range(U)] for k in ("z_loaded", "z_stored"))
        dve2 = ["e_T_done", "o_T_done", "o_stat_done", "o_mv_done", "o_veps_done", "weights_got", "h_sq_done", "h_veps_done", "z1_done", "z2_done", "z_done", "e_out_done", "expert_done", "c1_done", "c2_done", "biased",
                "o_h_done", "o_hn_done", "o_out_done",
                "hb_done", "hop_out1", "gates_done", "neg_abs_done", "log_f_done", "g_key_done", "cmax_done",
                "denom_done", "denom2_done", "denom3_done", "h_sum_done", "h_mid_done", "h_var_done", "rope_done", "x3_done"]
        act2 = ["table_loaded", "o_g_done", "hop_out0", "m_v_done", "exp_abs_done", "soft_done", "decay_done", "floor_done"]
        pe2 = ["e_turned", "down_done", "o_turned", "o_up", "o_hturned", "o_down", "hop_done"]
        pool2 = ["o_rstd_done", "got_ready", "put_ready", "at_done", "fm_done", "x5b_done", "g_diag_done", "h_rstd_done", "xb_done", "rope_k_done", "r4_done"]
        s["put_free"] = sem("put_free")
        s |= {k: sem(k) for k in dve2 + act2 + pe2 + pool2}
        dve_done, act_done, pe_done, pool_done = dve_done + dve2, act_done + act2, pe_done + pe2, pool_done + pool2

        by_half = {"k_copied", "scores_done", "max_done", "shifted", "exp_done", "biased"}

        LAST_LN = 7 * NT + 2 * U
        USES = {1: 7, 3: 11, 5: 15}
        HOP_DESK = USES[1] * NT // U
        BASE = {1: dict(att=0, q=0, k=0, qk=0, out=0, ln=0, desk=0),
                3: dict(att=2 * NT, q=2 * NT, k=NT, qk=NT, out=NT, ln=NT, desk=HOP_DESK + S),
                5: dict(att=4 * NT, q=3 * NT, k=3 * NT, qk=2 * NT, out=2 * NT, ln=4 * NT,
                        desk=HOP_DESK + S + USES[3] * NT // U + 5)}
        hop_dram = dram("hop_dram", [B * S, MH * S])
        xn_dram, r4_dram = dram("xn_dram", [B * S, D]), dram("r4_dram", [B * S, D])
        x6_dram = dram("x6_dram", [B * S, D])
        token_of0, token_of1 = dram("token_of0", [NSLOT0, 1], I32), dram("token_of1", [NSLOT1, 1], I32)
        moe0, moe1 = dram("moe0", [NSLOT0, D]), dram("moe1", [NSLOT1, D])
        c_flat = T["ctx_1024"].rearrange("b s d -> (b s) d")

        x1 = dram("x1", [B * S, D])
        x0 = T["x"].rearrange("b s d -> (b s) d")
        w_loads = [
            (consts[:], T["consts"]), (shared[:, 0:cb_n], T["consts16"]),
            (w_raw[:, 0:3, :], T["L0_attn_Wqkv_w"].rearrange("(k o) c -> o k c", k=3)),
            (w_raw[:, 3:6, :].rearrange("p a b -> p (a b)"), T["L0_attn_conv_w"].rearrange("o i k -> o (i k)")),
            (w_raw[:, 6, :], T["L0_attn_out_w"]),
            (a_col[:, 0:2], T["L0_attn_Wqkv_b"][0:2 * D].rearrange("(k o) -> o k", k=2)),
            (a_col[:, 2:3], T["L0_attn_conv_b"].rearrange("(o k) -> o k", k=1)),
            (a_row[:, 0, :], T["L0_attn_Wqkv_b"][2 * D:3 * D].partition_broadcast(P)),
            (a_row[:, 1, :], T["L0_attn_out_b"].partition_broadcast(P)),
        ]

        def column(name):
            return T[name].rearrange("(o k) -> o k", k=1)

        w_loads += [
            (hop_at[:], T["itok_SxS2_0_2016"].rearrange("(j v) m -> (v m) j", v=2)),
            (g_raw[0:MH].rearrange("p k c -> p (k c)"), T["L0_xattn_igate_w"]),
            (g_raw[MH:2 * MH].rearrange("p k c -> p (k c)"), T["L0_xattn_fgate_w"]),
            (g_row[:, 0:MH], T["L0_xattn_igate_b"].partition_broadcast(P)),
            (g_row[:, MH:2 * MH], T["L0_xattn_fgate_b"].partition_broadcast(P)),
            (m_row[:, 0, :], T["L0_xattn_ln_w"].partition_broadcast(P)),
            (m_row[:, 1, :], T["L0_xattn_ln_b"].partition_broadcast(P)),
            (f_raw[:], T["L0_ffn_Wqkv"]), (f_w[:, 5, :], T["L0_ffn_Wproj"]), (f_gate[:], T["L0_ffn_Wgate"]),
            (f_col[:, 0:1], column("L0_ffn_ln1_g")), (f_col[:, 1:2], column("L0_ffn_ln1_b")),
            (f_col[:, 2:3], column("L0_ffn_ln2_g")), (f_col[:, 3:4], column("L0_ffn_ln2_b")),
        ]

        late_loads = [
            (l_w[:, 0, :], T["L1_attn_wq"]), (l_raw[:, 0:32], T["L1_attn_wk"]), (l_raw[:, 32:64], T["L1_attn_wv"]),
            (l_w[:, 5, :], T["L1_attn_wo"]),
            (c_w[:, 0, :], T["L1_xattn_Wq"]), (c_w[:, 1, :], T["L1_xattn_Wk"]), (c_w[:, 2, :], T["L1_xattn_Wv"]),
            (c_w[:, 3, :], T["L1_xattn_Wo"]), (c_col[:, 0:1], column("L1_xattn_bq")),
            (c_col[:, 1:2], column("L1_xattn_bk")),
            (c_row[:, 0, :], T["L1_xattn_bv"].partition_broadcast(P)),
            (c_row[:, 1, :], T["L1_xattn_bo"].partition_broadcast(P)),
            (rt_w[:], T["L1_ffn_Wr"]), (rt_row[:], T["L1_ffn_br"].partition_broadcast(P)),
            (o_w1, T["L1_ffn_W1"].rearrange("e c h -> c e h")),
            (o_w2, T["L1_ffn_W2"].rearrange("e c h -> c e h")),
            (o_b1.rearrange("p e h -> p (e h)"), T["L1_ffn_b1"].rearrange("e h -> (e h)").partition_broadcast(P)),
            (o_b2.rearrange("p e h -> p (e h)"), T["L1_ffn_b2"].rearrange("e h -> (e h)").partition_broadcast(P)),
            (o_g[:], T["L1_ffn_g1"].rearrange("e h -> h e")), (o_b[:], T["L1_ffn_be1"].rearrange("e h -> h e")),
        ]

        def tile_rows(a, n):
            return a[bass.ds(n * P, P), :]

        W_READY = 5

        def rounds(eng, rest, parts):
            n = NT // U
            for kind, part in parts:
                if kind in ("head", "first"):
                    part(0)
            with eng.Fori(0, n - 1) as r:
                rest(r)
                for kind, part in parts:
                    if kind in ("head", "tail"):
                        part(r + 1 if kind == "head" else r)
            rest(n - 1)
            for kind, part in parts:
                if kind in ("tail", "last"):
                    part(n - 1)

        SPARE, SPARE_VALUES, SPARE_NORM, SPARE_SCORES, SPARE_HOPS = 4, 4, 6, 4, 2
        block = ctx.enter_context(nc.Block())

        @block.sync
        def _(sp):
            for u in range(U):
                sp.sem_inc(x_stored[u], 16)
            for dst, src in w_loads:
                sp.dma_start(dst, src, allow_slow_non_contiguous=True).then_inc(loaded, 16)

            def load1(t, u):
                sp.wait_ge(s["x_res_done"], t + u + 1)
                sp.dma_start(x_in[u], tile_rows(x0, t + u)).then_inc(in_loaded[u], 16)

            def store1(t, u):
                sp.wait_ge(s["ln_done"], t + u + 1 + 2)
                sp.dma_start(tile_rows(x1, t + u), x_out[u]).then_inc(x_stored[u], 16)

            for u in range(U):
                load1(0, u)
            sp.wait_ge(zero_sem, 1)
            sp.dma_start(token_of0.rearrange("(p n) x -> p (n x)", p=P), zeros_i[:, 0:NSLOT0 // P])\
              .then_inc(table_sem, 16)
            sp.dma_start(token_of1.rearrange("(p n) x -> p (n x)", p=P), zeros_i[:, 0:NSLOT1 // P])\
              .then_inc(table_sem, 16)
            with sp.Fori(0, NT // U - 1) as r:
                t = U * r
                for u in range(U):
                    load1(t + U, u)
                for u in range(U):
                    store1(t, u)
            for u in range(U):
                store1(NT - U, u)
            for u in range(U):
                sp.wait_ge(x_stored[u], 16 * (NT // U) + 16)

            x1_rows = x1.rearrange("(b v) d -> b v d", v=S)
            hop_rows_dram = hop_dram.rearrange("(b v) k -> b v k", v=S)

            def load2(v, u):
                sp.wait_ge(desk_full, HOP_DESK + v + u - 1)
                sp.dma_start(hx_in[u][0:B], x1_rows[:, bass.ds(v + u, 1), :].rearrange("b v d -> b (v d)"))\
                  .then_inc(hx_loaded[u], 16)

            def store2(v, u):
                sp.wait_ge(s["hop_out0"], v + u + 3)
                sp.wait_ge(s["hop_out1"], v + u + 3)
                sp.dma_start(hop_rows_dram[:, bass.ds(v + u, 1), :].rearrange("b v k -> b (v k)"),
                             hop_out[u][0:B]).then_inc(hop_stored[u], 16)

            for u in range(U):
                sp.sem_inc(hop_stored[u], 16)
                load2(0, u)
            with sp.Fori(0, S // U - 1) as r:
                for u in range(U):
                    load2(U * r + U, u)
                for u in range(U):
                    store2(U * r, u)
            for u in range(U):
                store2(S - U, u)
            for u in range(U):
                sp.wait_ge(hop_stored[u], 16 * (S // U) + 16)

            def load3(t, u):
                sp.wait_ge(s["z_done"], t + u + 1)
                sp.dma_start(x_in[u], tile_rows(x1, t + u)).then_inc(in_loaded[u], 16)
                sp.dma_start(c_in[u], tile_rows(c_flat, t + u)).then_inc(c_loaded[u], 16)
                two = c_flat[bass.ds((t + u) * P, P), :].rearrange("(b t) d -> t b d", b=NB)
                for par in range(2):
                    sp.dma_start(c_two[u][S * par:S * par + S].rearrange("p (b d) -> p b d", b=NB), two)\
                      .then_inc(c_loaded[u], 16)
                sp.dma_start(hop_in[u], tile_rows(hop_dram, t + u)).then_inc(c_loaded[u], 16)

            def store3(t, u):
                sp.wait_ge(s["ln_done"], NT + 3 * t + 2 * U + u + 3)
                sp.dma_start(tile_rows(xn_dram, t + u), xn[u]).then_inc(xn_stored[u], 16)
                sp.wait_ge(s["r4_done"], t + u + 3)
                sp.dma_start(tile_rows(r4_dram, t + u), r4[u]).then_inc(xn_stored[u], 16)

            per = 32
            for u in range(U):
                sp.sem_inc(xn_stored[u], per)
                load3(0, u)
            for dst, src in late_loads:
                sp.dma_start(dst, src, allow_slow_non_contiguous=True).then_inc(late, 16)
            with sp.Fori(0, NT // U - 1) as r:
                for u in range(U):
                    load3(U * r + U, u)
                for u in range(U):
                    store3(U * r, u)
            for u in range(U):
                store3(NT - U, u)
            for u in range(U):
                sp.wait_ge(xn_stored[u], per * (NT // U) + per)

            def watch_puts(n0):
                with sp.Fori(0, NT // U) as r:
                    for u in range(U):
                        sp.wait_ge(put_done[u], 16 * n0 + 32 * r + 32)
                        sp.sem_inc(s["put_free"], 1)

            for u in range(U):
                sp.sem_inc(e_stored[u], 16)
            sp.sem_inc(s["put_free"], CREDIT)
            watch_puts(0)
            sp.dma_start(at0_all[:], token_of0.rearrange("(q p j) x -> p q (j x)", p=P, j=J),
                         allow_slow_non_contiguous=True).then_inc(at_loaded, 16)
            out0 = moe0.rearrange("(q p j) d -> q p (j d)", p=P, j=J)

            with sp.Fori(0, E0 // 2) as r:
                for i in range(2 * GE):
                    if i >= 2:
                        sp.wait_ge(s["e_out_done"], 2 * GE * r + i - 2 + 3)
                        sp.dma_start(out0[bass.ds(2 * GE * r + i - 2, 1)].rearrange("q p n -> p (q n)"),
                                     e_out[i % 2]).then_inc(e_stored[i % 2], 16)
                for i in range(2 * GE - 2, 2 * GE):
                    sp.wait_ge(s["e_out_done"], 2 * GE * r + i + 3)
                    sp.dma_start(out0[bass.ds(2 * GE * r + i, 1)].rearrange("q p n -> p (q n)"),
                                 e_out[i % 2]).then_inc(e_stored[i % 2], 16)

            for u in range(U):
                sp.wait_ge(e_stored[u], 16 * GE * E0 // 2 + 16)

            for u in range(U):
                sp.sem_inc(x6_stored[u], 16)
            fs_flat = T["fside_BxSxS2_0"].rearrange("b s t -> (b s) t")
            mask_flat = T["mask_BxSxS2_ff0"].rearrange("b s t -> (b s) t")

            def load5(t, u):
                sp.wait_ge(s["x5b_done"], t + u + 1)
                sp.wait_ge(s["c2_done"], t + u + 1)
                sp.wait_ge(s["fm_done"], t + u + 1)
                sp.dma_start(x_in[u], tile_rows(r4_dram, t + u)).then_inc(in_loaded[u], 16)
                sp.dma_start(c_in[u], tile_rows(c_flat, t + u)).then_inc(c_loaded[u], 16)
                sp.dma_start(fm_in[u][:, 0:S], tile_rows(fs_flat, t + u)).then_inc(c_loaded[u], 16)
                sp.dma_start(fm_in[u][:, S:2 * S], tile_rows(mask_flat, t + u)).then_inc(c_loaded[u], 16)

            def store5(t, u):
                sp.wait_ge(s["ln_done"], BASE[5]["ln"] + 3 * t + 4 * U + u + 3)
                sp.dma_start(tile_rows(x6_dram, t + u), x6[u])\
                  .then_inc(x6_stored[u], 16)

            for u in range(U):
                load5(0, u)
            with sp.Fori(0, NT // U - 1) as r:
                for u in range(U):
                    load5(U * r + U, u)
                for u in range(U):
                    store5(U * r, u)
            for u in range(U):
                store5(NT - U, u)
            for u in range(U):
                sp.wait_ge(x6_stored[u], 16 * (NT // U) + 16)

            for u in range(U):
                sp.sem_inc(o_stored[u], 16)
                sp.sem_inc(z_stored[u], 16)
            watch_puts(NT)
            sp.dma_start(at1_all[:, 0:NJ], token_of1.rearrange("(p q) x -> p (q x)", p=P)).then_inc(at_loaded, 16)

            def store6(r, w):
                sp.wait_ge(s["o_out_done"], U * r + w + 3)
                sp.dma_start(moe1[bass.ds((V * r + 2 * w) * P, 2 * P), :].rearrange("(i p) d -> p i d", p=P),
                             o_out[w].rearrange("p (i d) -> p i d", i=2)).then_inc(o_stored[w], 16)

            with sp.Fori(0, NJ // V) as r:
                for w in range(2):
                    store6(r, w)
            for w in range(2):
                sp.wait_ge(o_stored[w], 16 * (NJ // V) + 16)

            def load7(t, u):
                sp.wait_ge(s["c1_done"], NT + t + u + 1)
                sp.dma_start(x_in[u], tile_rows(x6_dram, t + u)).then_inc(z_loaded[u], 16)

            def store7(t, u):
                sp.wait_ge(s["ln_done"], LAST_LN + t + u + 3)
                sp.dma_start(tile_rows(out.rearrange("b s d -> (b s) d"), t + u), x_out[u]).then_inc(z_stored[u], 16)

            for u in range(U):
                load7(0, u)
            with sp.Fori(0, NT // U - 1) as r:
                for u in range(U):
                    load7(U * r + U, u)
                for u in range(U):
                    store7(U * r, u)
            for u in range(U):
                store7(NT - U, u)
            for u in range(U):
                sp.wait_ge(z_stored[u], 16 * (NT // U) + 16)

        @block.tensor
        def _(pe):
            for k in pe_done:
                pe.sem_inc(s[k], 2 * CREDIT if k in by_half else CREDIT)
            pe.wait_ge(loaded, 16 * len(w_loads))
            taps = w_raw[:, 3:6, :].rearrange("p a b -> p (a b)").rearrange("p (i k) -> p k i", k=3)
            for k in range(7):
                last = pe.transpose(setup_ps[:, k, :], taps[:, k - 3, :] if 3 <= k < 6 else w_raw[:, k, :], ident)
            for k in range(3):
                last = pe.transpose(setup_ps[:, 8 + k, 0:2 * MH], g_raw[:, k, :], ident[0:2 * MH, 0:2 * MH])
            last.then_inc(w_turned, 1)
            pe.wait_ge(w_ready, W_READY)
            pe.wait_ge(zeroed, U + 1)

            def keep_busy(m, products):
                pe.wait_ge(s["turn0_copied"], m + 1)
                for _ in range(products):
                    pe.matmul(turned_ps[:, 0, :], ident16, causal16.unsqueeze(1).broadcast_to([P, 8, S]),
                              start=True, stop=True, skip_group_check=True)

            def scores(m, u, q, k_done, causal):
                if u == 0:
                    keep_busy(m, SPARE_SCORES)
                pe.wait_ge(s["q_copied"], q + 2)
                pe.wait_ge(s["shifted"], 2 * m)
                keys = k_bd[u].rearrange("p (h t) -> p h t", t=P)
                for g in range(NR):
                    pe.wait_ge(s["k_copied"], 2 * k_done + g + 3)
                    if causal:
                        pe.matmul(scores_ps[:, u, g, :], ident16,
                                  causal16.unsqueeze(1).broadcast_to([P, 8, S]),
                                  start=True, stop=False, skip_group_check=True)
                    for b in range(NB):
                        last = pe.matmul(scores_ps[S * b:S * b + S, u, g, :],
                                         q_T[u][:, S * b:S * b + S],
                                         keys[:, 8 * g:8 * g + 8, S * b:S * b + S],
                                         start=not causal, stop=True, skip_group_check=True)
                    last.then_inc(s["scores_done"], 1)

            def mix(m, u, v_use):
                if u == 0:
                    keep_busy(m, SPARE)
                for half in range(2):
                    pe.wait_ge(s["exp_done"], 2 * m + half + 3)
                    pe.wait_ge(s[f"turn{half}_copied"], m + 1)
                    for k in range(4):
                        hp = 4 * half + k
                        last = pe.transpose(turned_ps[:, half, P * k:P * k + P],
                                            probs[u][:, P * hp:P * hp + P], ident)
                    last.then_inc(s[f"turn{half}_done"], 1)
                pe.wait_ge(desk_empty, v_use + 2)
                pe.wait_ge(s["normed"], m + 1)
                for hp in range(8):
                    if hp % 4 == 0:
                        pe.wait_ge(s[f"turn{hp // 4}_copied"], m + 2)
                    last = pe.matmul(heads_ps[:, 36 * hp:36 * hp + 36], turned[u][:, P * hp:P * hp + P],
                                     v_bd[u][:, 36 * hp:36 * hp + 36], start=True, stop=True,
                                     skip_group_check=True)
                last.then_inc(s["pv_done"], 1)

            def turn(use, src):
                pe.wait_ge(desk_empty, use + 1)
                pe.transpose(trans_ps, src, ident).then_inc(desk_full, 1)

            def turn_all(use, sources):
                pe.wait_ge(desk_empty, use + 1)
                for k, src in enumerate(sources):
                    last = pe.transpose(desk_ps[:, P * k:P * k + P], src, ident)
                last.then_inc(desk_full, 1)

            def values(use, u, src_T, w):
                pe.wait_ge(desk_empty, use + 1)
                wv = w.rearrange("p (g h c) -> p h g c", g=8, h=2)
                for b in range(NB):
                    for par in range(2):
                        last = pe.matmul(desk_ps[S * par:S * par + S, S * b:S * b + S],
                                         src_T[u][:, S * b:S * b + S], wv[:, par], start=True, stop=True,
                                         skip_group_check=True)
                last.then_inc(desk_full, 1)

            with pe.Fori(0, NT // U) as r:
                t = U * r
                d = USES[1] * r
                for u in range(U):
                    pe.wait_ge(in_loaded[u], 8 * t + 16)
                turn_all(d, x_in)
                pe.wait_ge(desk_empty, d + 2)
                for u in range(U):
                    pe.wait_ge(s["y_done"], t + u + 1)
                    for k in range(2):
                        last = pe.matmul(scores_ps[:, u, k, 0:P], a_w[:, k, :], x_T[u],
                                         start=True, stop=True, skip_group_check=True)
                    last.then_inc(s["qk_done"], 1)
                for u in range(U):
                    values(d + 1 + u, u, x_T, a_w[:, 2, :])
                for u in range(U):
                    scores(2 * t + u + 1, u, 2 * t + u + 1, t + u + 1, True)
                for u in range(U):
                    mix(2 * t + u + 1, u, d + 1 + u)
                for u in range(U):
                    pe.wait_ge(s["normed"], 2 * t + u + 3)
                    turn(d + 3 + u, ctx_o[u])
                for u in range(U):
                    pe.wait_ge(desk_empty, d + 3 + u + 2)
                    pad = pad_T[u].rearrange("p (b s) -> p b s", b=NB)
                    for k in range(3):
                        last = pe.matmul(scores_ps[:, u, 0, 0:P], a_w[:, 3 + k, :], pad[:, :, k:k + S],
                                         start=(k == 0), stop=(k == 2), skip_group_check=True)
                    last.then_inc(s["conv_done"], 1)
                for u in range(U):
                    scores(2 * t + 2 + u + 1, u, 2 * t + 2 + u + 1, t + u + 1, True)
                for u in range(U):
                    mix(2 * t + 2 + u + 1, u, d + 1 + u)
                for u in range(U):
                    pe.wait_ge(s["normed"], 2 * t + 2 + u + 3)
                    turn(d + 5 + u, ctx_o[u])
                for u in range(U):
                    pe.wait_ge(desk_empty, d + 5 + u + 2)
                    pe.matmul(scores_ps[:, u, 0, 0:P], o_T[u], a_w[:, 6, :], start=True, stop=True,
                              skip_group_check=True).then_inc(s["out_done"], 1)

            pe.wait_ge(hop_gathered, 16 * HOPS)
            pe.wait_ge(s["y_done"], NT + 2)
            for c in range(HOPS // 4):
                if c >= 4:
                    pe.wait_ge(hop_copied, c - 3)
                for k in range(4):
                    last = pe.transpose(setup_ps[:, 4 * (c % 4) + k, :], hop_rows[:, 4 * c + k, :], ident)
                last.then_inc(hop_turned, 1)
            with pe.Fori(0, S // U) as r:
                v = U * r
                for u in range(U):
                    pe.wait_ge(hx_loaded[u], 8 * v + 16)
                    pe.wait_ge(desk_empty, HOP_DESK + v + u + 1)
                    pe.transpose(desk_ps[:, 0:B], hx_in[u][0:B], ident[0:B, 0:B]).then_inc(desk_full, 1)
                    keep_busy(2 * NT, SPARE_HOPS)
                for u in range(U):
                    pe.wait_ge(desk_empty, HOP_DESK + v + u + 2)
                    pe.wait_ge(s["hb_done"], v + u + 3)
                    pe.wait_ge(s["hop_out0"], v + u + 1)
                    vu = pe.to_reg(v + u + 1)
                    pe.wait_ge(hop_copied, HOPS // 4)
                    pe.wait_ge(s["hop_out1"], vu)
                    for g in range(NR):
                        last = pe.matmul(scores_ps[0:B, u, g, 0:4 * S], hx_T[u][64 * g:64 * g + 64, 0:B],
                                         hop_bd[u][64 * g:64 * g + 64, :], start=True, stop=True,
                                         skip_group_check=True)
                    last.then_inc(s["hop_done"], 1)

            base = BASE[3]

            def rope_products(n, u, hT, w):
                for k in range(4):
                    last = pe.matmul(scores_ps[:, u, k // 2, P * (k % 2):P * (k % 2) + P], w[:, k, :], hT[u],
                                     start=True, stop=True, skip_group_check=True)
                last.then_inc(s["qk_done"], 1)

            def rest(r):
                t = U * r
                d = base["desk"] + USES[3] * r
                m = base["att"] + 2 * t
                for u in range(U):
                    pe.wait_ge(s["g_diag_done"], t + u + 3)
                    pe.wait_ge(s["turn1_copied"], m + u + 2)
                    pe.matmul(turned_ps[:, 1, :], const("ones2"), g_diag[u], start=True, stop=False)
                    pe.matmul(turned_ps[:, 1, :], ident16, causal16.unsqueeze(1).broadcast_to([P, MH, S]),
                              start=False, stop=True).then_inc(s["turn1_done"], 1)
                for u in range(U):
                    pe.wait_ge(s["exp_done"], 2 * (m + u + 1) + 4)
                    pe.wait_ge(s["turn0_copied"], m + u + 2)
                    for k in range(4):
                        last = pe.transpose(turned_ps[:, 0, P * k:P * k + P], probs[u][:, P * k:P * k + P], ident)
                    last.then_inc(s["turn0_done"], 1)
                    pe.wait_ge(s["m_v_done"], t + u + 3)
                    pe.wait_ge(s["normed"], m + u + 2)
                    pe.wait_ge(s["turn0_copied"], m + u + 3)
                    w = NB * 2 * (MD + 1)
                    for k in range(4):
                        last = pe.matmul(heads_ps[:, w * k:w * k + w], turned[u][:, P * k:P * k + P],
                                         m_vbd[u][:, w * k:w * k + w], start=True, stop=True, skip_group_check=True)
                    last.then_inc(s["pv_done"], 1)
                pe.wait_ge(s["z_done"], t + 3)
                keep_busy(m + U + 1, SPARE_NORM)
                for u in range(U):
                    pe.wait_ge(s["ln_done"], base["ln"] + 3 * t + U + u + 3)
                    turn(d + 5 + u, xn[u])
                for u in range(U):
                    pe.wait_ge(desk_empty, d + 5 + u + 2)
                    rope_products(base["qk"] + t + u + 1, u, h_T, f_w)
                for u in range(U):
                    values(d + 7 + u, u, h_T, f_w[:, 4, :])
                for u in range(U):
                    scores(m + 2 + u + 1, u, base["q"] + t + u + 1, base["k"] + 2 * t + 2 + u + 1, True)
                for u in range(U):
                    mix(m + 2 + u + 1, u, d + 7 + u)
                for u in range(U):
                    pe.wait_ge(s["normed"], m + 2 + u + 3)
                    turn(d + 9 + u, ctx_o[u])
                for u in range(U):
                    pe.wait_ge(desk_empty, d + 9 + u + 2)
                    pe.matmul(scores_ps[:, u, 0, 0:P], o_T[u], f_w[:, 5, :], start=True, stop=True,
                              skip_group_check=True).then_inc(s["out_done"], 1)

            def products(r):
                t = U * r
                d = base["desk"] + USES[3] * r
                m = base["att"] + 2 * t
                pe.wait_ge(s["y_done"], base["out"] + t + 2)
                for u in range(U):
                    pe.wait_ge(s["k_copied"], 2 * (base["k"] + 2 * t + u + 1) + 4)
                    pe.wait_ge(s["shifted"], 2 * (m + u + 1))
                    keys = k_bd[u][:, 0:MH * P].rearrange("p (h t) -> p h t", t=P)
                    for b in range(NB):
                        last = pe.matmul(scores_ps[S * b:S * b + S, u, 0, :], x_T[u][:, S * b:S * b + S],
                                         keys[:, :, S * b:S * b + S], start=True, stop=True, skip_group_check=True)
                    last.then_inc(s["scores_done"], 2)

            def head(r):
                t = U * r
                d = base["desk"] + USES[3] * r
                m = base["att"] + 2 * t
                for u in range(U):
                    pe.wait_ge(in_loaded[u], 8 * t + 8 * NT + 16)
                    pe.wait_ge(c_loaded[u], 32 * t + 64)
                turn_all(d, x_in + c_in)
                pe.wait_ge(desk_empty, d + 2)
                for u in range(U):
                    for k, src in enumerate((x_T, c_T, c_T)):
                        last = pe.matmul(desk_ps[:, 16 * u:16 * u + 16], src[u], g_w[:, k, :], start=(k == 0),
                                         stop=(k == 2), skip_group_check=True)
                last.then_inc(desk_full, 1)

            def sums(r):
                t = U * r
                d = base["desk"] + USES[3] * r
                m = base["att"] + 2 * t
                pe.wait_ge(s["log_f_done"], t + U + 2)
                pe.wait_ge(desk_empty, d + 3)
                pe.matmul(desk_ps[:, 0:U * MH], const("tri2"), whole["log_f"][:].rearrange("p u h -> p (u h)"),
                          start=True, stop=True).then_inc(desk_full, 1)

            def tail(r):
                t = U * r
                d = base["desk"] + USES[3] * r
                m = base["att"] + 2 * t
                pe.wait_ge(s["ln_done"], base["ln"] + 3 * t + 2 * U + U + 2)
                turn_all(d + 14, xn)
                pe.wait_ge(desk_empty, d + 16)
                for u in range(U):
                    last = pe.matmul(desk_ps[:, 8 * u:8 * u + 8], h_T[u], f_gate[:], start=True, stop=True,
                                     skip_group_check=True)
                last.then_inc(desk_full, 1)

            def no_tail(r):
                pe.wait_ge(desk_empty, base["desk"] + USES[3] * (r + 0) + 4)
                pe.sem_inc(desk_full, 2)
                pe.sem_inc(desk_empty, 2)

            def no_head(r):
                pe.wait_ge(desk_empty, base["desk"] + USES[3] * (r + 1) + 1)
                pe.sem_inc(desk_full, 3)
                pe.sem_inc(desk_empty, 3)

            rounds(pe, rest, [("head", head), ("head", sums), ("head", products), ("first", no_tail), ("last", no_head),
                              ("tail", tail)])


            def count(n, E):
                pe.wait_ge(route_masked, n)
                cols = NT * E
                for c in range(-(-cols // 512)):
                    w = min(512, cols - 512 * c)
                    for k, lhs in enumerate(("tri16", "ones16")):
                        last = pe.matmul(scores_ps[:, k, c, 0:w], const16(lhs), r_mask[:, 512 * c:512 * c + w],
                                         start=True, stop=True)
                last.then_inc(route_counted, 1)

            count(1, E0)
            pe.wait_ge(counts_read, 1)

            with pe.Fori(0, E0 // 2) as r:
                for i in range(2 * GE):
                    w, u, q = i // GE, i % 2, 2 * GE * r + i
                    pe.wait_ge(e_in_loaded[u], 16 * J * (GE * r + i // 2 + 1))
                    pe.wait_ge(s["e_T_done"], q + 1)
                    for j in range(J):
                        last = pe.transpose(turned_ps[:, u, P * j:P * j + P], e_in[u][:, P * j:P * j + P], ident)
                    last.then_inc(s["e_turned"], 1)
                    pe.wait_ge(s["e_T_done"], q + 3)
                    pe.wait_ge(e_loaded[w], 64 * r + 64)
                    for f in range(F0):
                        pe.wait_ge(gelu_done, F0 * q + f + 1)
                        pe.matmul(scores_ps[:, f // 2, f % 2, 0:GS], e_w1[w][:, P * f:P * f + P], e_T[u],
                                  start=True, stop=True).then_inc(up_done, 1)
                    pe.wait_ge(s["e_out_done"], q + 1)
                    bank = (heads_ps, desk_ps)[u]
                    for f in range(F0):
                        pe.wait_ge(gelu_done, F0 * q + f + 1 + F0)
                        for j in range(J):
                            last = pe.matmul(bank[:, P * j:P * j + P], e_mid[u][:, f, P * j:P * j + P],
                                             e_w2[w][:, f, :], start=(f == 0 and j == 0),
                                             stop=(f == F0 - 1 and j == J - 1), skip_group_check=True)
                    last.then_inc(s["down_done"], 1)

            base = BASE[5]
            pe.wait_ge(late, 16 * len(late_loads))
            pe.wait_ge(w_ready, W_READY + 2)
            def rest(r):
                t = U * r
                d = base["desk"] + USES[5] * r
                m = base["att"] + 2 * t
                ln = base["ln"] + 3 * t
                o2 = base["qk"] + 2 * t
                for u in range(U):
                    values(d + 4 + u, u, x_T, l_w[:, 4, :])
                    scores(m + u + 1, u, base["q"] + 2 * t + u + 1, base["k"] + 2 * t + u + 1, True)
                for u in range(U):
                    mix(m + u + 1, u, d + 4 + u)
                for u in range(U):
                    pe.wait_ge(s["normed"], m + u + 3)
                    turn(d + 6 + u, ctx_o[u])
                for u in range(U):
                    pe.wait_ge(desk_empty, d + 6 + u + 2)
                    pe.matmul(scores_ps[:, u, 0, 0:P], o_T[u], l_w[:, 5, :], start=True, stop=True,
                              skip_group_check=True).then_inc(s["out_done"], 1)
                for u in range(U):
                    pe.wait_ge(c_loaded[u], 32 * NT + 24 * t + 48)
                turn_all(d + 8, c_in)
                for u in range(U):
                    values(d + 9 + u, u, c_T, c_w[:, 2, :])
                keep_busy(m + 3, SPARE_VALUES)
                for u in range(U):
                    pe.wait_ge(s["ln_done"], ln + 2 * U + u + 3)
                    turn(d + 11 + u, x5[u])
                for u in range(U):
                    pe.wait_ge(desk_empty, d + 11 + u + 2)
                    for k, src in enumerate((x_T, c_T)):
                        last = pe.matmul(scores_ps[:, u, k, 0:P], c_w[:, k, :], src[u], start=True, stop=True,
                                         skip_group_check=True)
                    last.then_inc(s["qk_done"], 1)
                for u in range(U):
                    scores(m + 2 + u + 1, u, base["q"] + 2 * t + 2 + u + 1, base["k"] + 2 * t + 2 + u + 1, False)
                for u in range(U):
                    mix(m + 2 + u + 1, u, d + 9 + u)
                for u in range(U):
                    pe.wait_ge(s["normed"], m + 2 + u + 3)
                    turn(d + 13 + u, ctx_o[u])
                for u in range(U):
                    pe.wait_ge(desk_empty, d + 13 + u + 2)
                    pe.matmul(scores_ps[:, u, 0, 0:P], o_T[u], c_w[:, 3, :], start=True, stop=True,
                              skip_group_check=True).then_inc(s["out_done"], 1)

            def head(r):
                t = U * r
                d = base["desk"] + USES[5] * r
                m = base["att"] + 2 * t
                ln = base["ln"] + 3 * t
                o2 = base["qk"] + 2 * t
                for u in range(U):
                    pe.wait_ge(s["ln_done"], ln + u + 3)
                    turn(d + u, x4[u])

            def products(r):
                t = U * r
                d = base["desk"] + USES[5] * r
                m = base["att"] + 2 * t
                ln = base["ln"] + 3 * t
                o2 = base["qk"] + 2 * t
                pe.wait_ge(desk_empty, d + 1 + 2)
                pe.wait_ge(s["y_done"], base["out"] + 2 * t + 2)
                for u in range(U):
                    rope_products(o2 + u + 1, u, x_T, l_w)

            def tail(r):
                t = U * r
                d = base["desk"] + USES[5] * r
                m = base["att"] + 2 * t
                ln = base["ln"] + 3 * t
                o2 = base["qk"] + 2 * t
                pe.wait_ge(s["ln_done"], ln + 5 * U + 2)
                turn_all(d + 17, x6)
                pe.wait_ge(desk_empty, d + 17 + 2)
                for u in range(U):
                    last = pe.matmul(desk_ps[:, E1 * u:E1 * u + E1], o_T[u], rt_w[:], start=True, stop=True,
                                     skip_group_check=True)
                last.then_inc(desk_full, 1)

            def no_tail(r):
                pe.wait_ge(desk_empty, base["desk"] + USES[5] * (r + 0) + 3)
                pe.sem_inc(desk_full, 2)
                pe.sem_inc(desk_empty, 2)

            def no_head(r):
                pe.wait_ge(desk_empty, base["desk"] + USES[5] * (r + 1) + 1)
                pe.sem_inc(desk_full, 2)
                pe.sem_inc(desk_empty, 2)

            rounds(pe, rest, [("head", head), ("head", products), ("first", no_tail), ("last", no_head), ("tail", tail)])

            count(2, E1)
            pe.wait_ge(counts_read, 2)
            def expert(r, w, i):
                return pe.value_load(expert_of[0:1, bass.ds(V * r + 2 * w + i, 1)], min_val=0, max_val=E1 - 1)

            def cols(i):
                return slice(P * i, P * i + P)

            with pe.Fori(0, NJ // V) as r:
                for w in range(2):
                    q = 2 * r + w + 1
                    pe.wait_ge(o_in_loaded[w], 32 * r + 32)
                    pe.wait_ge(s["o_T_done"], q)
                    for i in range(2):
                        last = pe.transpose(turned_ps[:, w, cols(i)], o_in[w][:, cols(i)], ident)
                    last.then_inc(s["o_turned"], 1)
                for w in range(2):
                    q = 2 * r + w + 1
                    experts = [expert(r, w, i) for i in range(2)]
                    pe.wait_ge(s["o_T_done"], q + 2)
                    pe.wait_ge(s["o_h_done"], q)
                    for i, e in enumerate(experts):
                        last = pe.matmul(scores_ps[:, w, 0, cols(i)], o_in_T[w][:, cols(i)],
                                         o_w1[:, bass.ds(e, 1), :].rearrange("p e h -> p (e h)"),
                                         start=True, stop=True, skip_group_check=True)
                    last.then_inc(s["o_up"], 1)
                for w in range(2):
                    q = 2 * r + w + 1
                    pe.wait_ge(s["o_hn_done"], q + 2)
                    pe.wait_ge(s["o_g_done"], q)
                    for i in range(2):
                        last = pe.transpose(scores_ps[:, w, 1, cols(i)], o_hn[w][:, cols(i)], ident)
                    last.then_inc(s["o_hturned"], 1)
                for w in range(2):
                    q = 2 * r + w + 1
                    experts = [expert(r, w, i) for i in range(2)]
                    pe.wait_ge(s["o_g_done"], q + 2)
                    pe.wait_ge(s["o_out_done"], q)
                    for i, e in enumerate(experts):
                        last = pe.matmul((heads_ps, desk_ps)[w][:, cols(i)], o_g_T[w][:, cols(i)],
                                         o_w2[:, bass.ds(e, 1), :].rearrange("p e h -> p (e h)"),
                                         start=True, stop=True, skip_group_check=True)
                    last.then_inc(s["o_down"], 1)

        @block.scalar
        def _(act):
            for k in act_done:
                act.sem_inc(s[k], 2 * CREDIT if k in by_half else CREDIT)
            act.sem_inc(desk_empty, 1)
            act.wait_ge(loaded, 16 * len(w_loads))
            act.wait_ge(zeroed, U + 1)

            def copy_turned(use, dst, src=None, **kw):
                act.wait_ge(desk_full, use + 1)
                act.activation(dst, trans_ps if src is None else src, ACT.Identity, **kw).then_inc(desk_empty, 1)

            def exp(m, u, scale):
                for g in range(NR):
                    act.wait_ge(s["shifted"], 2 * m + g + 3)
                    half = probs[u][:, 512 * g:512 * g + 512]
                    act.activation(half, half, ACT.Exp, scale=scale).then_inc(s["exp_done"], 1)

            def copy_probs(m, u):
                act.wait_ge(s["pv_done"], m)
                for half in range(2):
                    act.wait_ge(s[f"turn{half}_done"], m + 2)
                    act.activation(turned[u][:, 512 * half:512 * half + 512], turned_ps[:, half, :],
                                   ACT.Identity).then_inc(s[f"turn{half}_copied"], 1)

            with act.Fori(0, NT // U) as r:
                t = U * r
                d = USES[1] * r
                copy_turned(d, whole["x_T"][:], desk_ps[:, 0:U * P].rearrange("p (u n) -> p u n", u=U))
                for u in range(U):
                    act.wait_ge(s["qk_done"], t + u + 3)
                    act.activation(q_T[u], scores_ps[:, u, 0, 0:P], ACT.Identity,
                                   bias=a_col[:, 0:1]).then_inc(s["q_copied"], 1)
                for u in range(U):
                    exp(2 * t + u + 1, u, SCALE)
                    copy_probs(2 * t + u + 1, u)
                for u in range(U):
                    pad = pad_T[u].rearrange("p (b s) -> p b s", b=NB)
                    copy_turned(d + 3 + u, pad[:, :, 1:1 + S], trans_ps.rearrange("p (b s) -> p b s", b=NB))
                for u in range(U):
                    act.wait_ge(s["conv_done"], t + u + 3)
                    act.activation(q_T[u], scores_ps[:, u, 0, 0:P], ACT.Identity,
                                   bias=a_col[:, 2:3]).then_inc(s["q_copied"], 1)
                for u in range(U):
                    exp(2 * t + 2 + u + 1, u, SCALE)
                    copy_probs(2 * t + 2 + u + 1, u)
                for u in range(U):
                    copy_turned(d + 5 + u, o_T[u])

            with act.Fori(0, S // U) as r:
                v = U * r
                for u in range(U):
                    copy_turned(HOP_DESK + v + u, hx_T[u][:, 0:B], desk_ps[:, 0:B])
                for u in range(U):
                    act.wait_ge(s["hop_done"], v + u + 3)
                    act.wait_ge(hop_stored[u], 8 * v + 16)
                    act.activation(hop_out[u][0:B, 0:4 * S], scores_ps[0:B, u, 0, 0:4 * S], ACT.Identity)\
                       .then_inc(s["hop_out0"], 1)

            base = BASE[3]
            def rest(r):
                t = U * r
                d = base["desk"] + USES[3] * r
                m = base["att"] + 2 * t
                for u in range(U):
                    act.wait_ge(s["turn1_copied"], m + u + 3)
                    act.activation(decay[u], decay[u], ACT.Exp).then_inc(s["decay_done"], 1)
                    act.wait_ge(s["cmax_done"], t + u + 3)
                    act.activation(floor[u], cmax[u], ACT.Exp, scale=-1.0).then_inc(s["floor_done"], 1)
                for u in range(U):
                    act.wait_ge(s["turn0_done"], m + u + 3)
                    act.activation(turned[u][:, 0:512], turned_ps[:, 0, :], ACT.Identity)\
                       .then_inc(s["turn0_copied"], 1)
                for u in range(U):
                    copy_turned(d + 5 + u, h_T[u], scale=f_col[:, 0:1], bias=f_col[:, 1:2])
                for u in range(U):
                    exp(m + 2 + u + 1, u, SCALE)
                    copy_probs(m + 2 + u + 1, u)
                for u in range(U):
                    copy_turned(d + 9 + u, o_T[u])

            def head(r):
                t = U * r
                d = base["desk"] + USES[3] * r
                m = base["att"] + 2 * t
                act.wait_ge(desk_full, d + 1)
                act.activation(whole["x_T"][:], desk_ps[:, 0:U * P].rearrange("p (u n) -> p u n", u=U), ACT.Identity)
                copy_turned(d, whole["c_T"][:], desk_ps[:, U * P:2 * U * P].rearrange("p (u n) -> p u n", u=U))
                for u in range(U):
                    act.wait_ge(s["pv_done"], m + u + 1)
                    act.wait_ge(c_loaded[u], 32 * t + 64)
                    mvv = m_vbd[u].rearrange("p (g b h c) -> p g b h c", g=4, b=NB, h=2)
                    cv = c_two[u].rearrange("p (b g h c) -> p g b h c", b=NB, g=4, h=2)
                    for par in range(2):
                        rows = slice(S * par, S * par + S)
                        last = act.activation(mvv[rows, :, :, par, 0:MD], cv[rows, :, :, par, :], ACT.Identity)
                    last.then_inc(s["m_v_done"], 1)
                act.wait_ge(s["neg_abs_done"], t + U + 2)
                act.activation(whole["exp_abs"][:], whole["neg_abs"][:], ACT.Exp).then_inc(s["exp_abs_done"], U)
                act.wait_ge(s["exp_abs_done"], t + U + 2)
                act.activation(whole["soft"][:], whole["exp_abs"][:], ACT.Ln, bias=1.0).then_inc(s["soft_done"], U)

            def tail(r):
                t = U * r
                d = base["desk"] + USES[3] * r
                m = base["att"] + 2 * t
                copy_turned(d + 14, whole["h_T"][:], desk_ps[:, 0:U * P].rearrange("p (u n) -> p u n", u=U),
                            scale=f_col[:, 2:3], bias=f_col[:, 3:4])
                copy_turned(d + 15, logits0[:, bass.ds(t, U), :], desk_ps[:, 0:U * 8].rearrange("p (u n) -> p u n", u=U))

            rounds(act, rest, [("head", head), ("tail", tail)])


            def route_exponentials(n, E):
                act.wait_ge(route_shifted, n)
                act.activation(r_gate[:, :, 0:E], r_gate[:, :, 0:E], ACT.Exp).then_inc(route_exp, 1)

            route_exponentials(1, E0)
            act.sem_inc(gelu_done, F0)
            with act.Fori(0, E0 // 2) as r:
                for i in range(2 * GE):
                    w, u, q = i // GE, i % 2, 2 * GE * r + i
                    act.wait_ge(s["down_done"], q + 1)
                    act.wait_ge(e_loaded[w], 64 * r + 64)
                    for f in range(F0):
                        act.wait_ge(up_done, F0 * q + f + 1)
                        act.activation(e_mid[u][:, f, :], scores_ps[:, f // 2, f % 2, 0:GS], ACT.Gelu,
                                       bias=e_b1[w][:, f:f + 1]).then_inc(gelu_done, 1)

            base = BASE[5]
            act.wait_ge(late, 16 * len(late_loads))
            act.wait_ge(w_ready, W_READY + 2)
            def rest(r):
                t = U * r
                d = base["desk"] + USES[5] * r
                m = base["att"] + 2 * t
                for u in range(U):
                    exp(m + u + 1, u, SCALE)
                    copy_probs(m + u + 1, u)
                for u in range(U):
                    copy_turned(d + 6 + u, o_T[u])
                copy_turned(d + 8, whole["c_T"][:], desk_ps[:, 0:U * P].rearrange("p (u n) -> p u n", u=U))
                for u in range(U):
                    copy_turned(d + 11 + u, x_T[u])
                for u in range(U):
                    act.wait_ge(s["qk_done"], base["qk"] + 2 * t + 2 + u + 3)
                    act.activation(q_T[u], scores_ps[:, u, 0, 0:P], ACT.Identity, bias=c_col[:, 2:3],
                                   scale=SCALE).then_inc(s["q_copied"], 1)
                for u in range(U):
                    exp(m + 2 + u + 1, u, 1.0)
                    copy_probs(m + 2 + u + 1, u)
                for u in range(U):
                    copy_turned(d + 13 + u, o_T[u])

            def head(r):
                t = U * r
                d = base["desk"] + USES[5] * r
                m = base["att"] + 2 * t
                for u in range(U):
                    copy_turned(d + u, x_T[u])

            def tail(r):
                t = U * r
                d = base["desk"] + USES[5] * r
                m = base["att"] + 2 * t
                copy_turned(d + 17, whole["o_T"][:], desk_ps[:, 0:U * P].rearrange("p (u n) -> p u n", u=U))
                copy_turned(d + 18, logits1[:, bass.ds(t, U), :], desk_ps[:, 0:U * E1].rearrange("p (u n) -> p u n", u=U))

            rounds(act, rest, [("head", head), ("tail", tail)])

            route_exponentials(2, E1)
            act.wait_ge(routed, 2)
            with act.Fori(0, NJ // V) as r:
                act.wait_ge(s["table_loaded"], r + 2)
                act.activation(table_for[:], ident[:, 0:1], ACT.Gelu).then_inc(s["table_loaded"], 1)
                for w in range(2):
                    experts = [act.value_load(expert_of[0:1, bass.ds(V * r + 2 * w + i, 1)], min_val=0, max_val=E1 - 1)
                               for i in range(2)]
                    act.wait_ge(s["o_down"], 2 * r + w + 1)
                    act.wait_ge(s["o_hturned"], 2 * r + w + 3)
                    for i, e in enumerate(experts):
                        cols = slice(P * i, P * i + P)
                        last = act.activation(o_g_T[w][:, cols], scores_ps[:, w, 1, cols], ACT.Gelu,
                                              scale=o_g[:, bass.ds(e, 1)], bias=o_b[:, bass.ds(e, 1)])
                    last.then_inc(s["o_g_done"], 1)

        @block.vector
        def _(dve):
            for k in dve_done:
                dve.sem_inc(s[k], 2 * CREDIT if k in by_half else CREDIT)
            dve.wait_ge(w_turned, 1)
            dve.wait_ge(loaded, 16 * len(w_loads))
            dve.tensor_copy(consts16[:], shared[:, 0:cb_n]).then_inc(w_ready, 1)
            dve.tensor_copy(a_w[:], setup_ps[:, 0:7, :]).then_inc(w_ready, 1)
            dve.tensor_copy(g_w[:], setup_ps[:, 8:11, 0:2 * MH]).then_inc(w_ready, 1)
            dve.tensor_scalar(m_row[:, 0, :], m_row[:, 0, :], 1.0, None, ALU.add).then_inc(w_ready, 1)

            def rotate(dst, src):
                dv = dst.rearrange("p (h k c) -> p h k c", h=H, k=2)
                sv = src.rearrange("p (h k c) -> p h k c", h=H, k=2)
                dve.tensor_scalar(dv[:, :, 0, :], sv[:, :, 1, :], -1.0, None, ALU.mult)
                return dve.tensor_copy(dv[:, :, 1, :], sv[:, :, 0, :])

            fr = f_raw[:].rearrange("p (h k c) -> p k h c", h=H, k=3)
            for k, at in enumerate((0, 2, 4)):
                last = dve.tensor_copy(f_w[:, at, :].rearrange("p (h c) -> p h c", h=H), fr[:, k])
            last.then_inc(w_copied, 1)
            dve.wait_ge(w_copied, 1)
            rotate(f_w[:, 1, :], f_w[:, 0, :])
            rotate(f_w[:, 3, :], f_w[:, 2, :]).then_inc(w_ready, 1)

            def spread_keys(u, src, bias, head, count):
                for g in range(NR):
                    hs = slice(8 * g, 8 * g + 8)
                    out_v = k_bd[u].rearrange("p (h t) -> p h t", h=H)[:, hs]
                    in_v = src.unsqueeze(1).broadcast_to([P, 8, P])
                    mask = const(head)[:, hs].unsqueeze(2).broadcast_to([P, 8, P])
                    dve.scalar_tensor_tensor(out_v, in_v, bias, mask, ALU.add, ALU.mult).then_inc(count, 1)

            def softmax_shift(m, u):
                for g in range(NR):
                    dve.wait_ge(s["scores_done"], 2 * m + g + 3)
                    sc = scores_ps[:, u, g, :].rearrange("p (h t) -> p h t", t=S)
                    best = row_max[u][:, 8 * g:8 * g + 8]
                    dve.tensor_reduce(best, sc, AX, ALU.max).then_inc(s["max_done"], 1)
                    dve.wait_ge(s["max_done"], 2 * m + g + 3)
                    dve.wait_ge(s["turn1_done"], m)
                    dve.tensor_tensor(probs[u][:, 512 * g:512 * g + 512].rearrange("p (h t) -> p h t", t=S), sc,
                                      best.unsqueeze(2).broadcast_to([P, 8, S]), ALU.subtract)\
                       .then_inc(s["shifted"], 1)

            def normalise(m, u):
                dve.wait_ge(s["pv_done"], m + 2)
                hv = heads_ps[:, 0:288].rearrange("p (g b h c) -> p g b h c", g=8, b=NB, h=2)
                for b in range(NB):
                    rows = slice(S * b, S * b + S)
                    last = dve.reciprocal(recip[u][rows].rearrange("p (g h) -> p g h", g=8), hv[rows, :, b, :, HD])
                last.then_inc(s["recip_done"], 1)
                dve.wait_ge(s["recip_done"], m + 2)
                for b in range(NB):
                    rows = slice(S * b, S * b + S)
                    r = recip[u][rows].rearrange("p (g h) -> p g h", g=8).unsqueeze(3).broadcast_to([S, 8, 2, HD])
                    last = dve.tensor_tensor(ctx_o[u][rows].rearrange("p (g h c) -> p g h c", g=8, h=2),
                                             hv[rows, :, b, :, 0:HD], r, ALU.mult)
                last.then_inc(s["normed"], 1)

            def copy_values(use, u, bias):
                dve.wait_ge(desk_full, use + 1)
                vv = v_bd[u].rearrange("p (g b h c) -> p g b h c", g=8, b=NB, h=2)
                pv = desk_ps[:, 0:P].rearrange("p (b g c) -> p g b c", b=NB, g=8)
                bv = bias.rearrange("p (g h c) -> p g h c", g=8, h=2) if bias is not None else None
                for par in range(2):
                    rows = slice(S * par, S * par + S)
                    if bias is None:
                        last = dve.tensor_copy(vv[rows, :, :, par, 0:HD], pv[rows])
                        continue
                    last = dve.tensor_tensor(vv[rows, :, :, par, 0:HD], pv[rows],
                                             bv[rows, :, par, :].unsqueeze(2).broadcast_to([S, 8, NB, HD]),
                                             ALU.add)
                last.then_inc(desk_empty, 1)

            def ln_stats(o, u, src):
                dve.bn_stats(stat[u], src).then_inc(s["stat_done"], 1)
                o2 = dve.to_reg(o + 2)
                dve.wait_ge(w_turned, 1)
                dve.wait_ge(s["stat_done"], o2)
                dve.bn_aggr(mv[u], stat[u]).then_inc(s["mv_done"], 1)
                dve.wait_ge(s["mv_done"], o + 2)
                dve.tensor_scalar(veps[u], mv[u][:, 1:2], EPS_LN, None, ALU.add).then_inc(s["veps_done"], 1)

            def ln_apply(o, u, dst, src):
                dve.wait_ge(s["rstd_done"], o + 2)
                dve.tensor_scalar(dst, src, mv[u][:, 0:1], rstd[u], ALU.subtract, ALU.mult)\
                   .then_inc(s["ln_done"], 1)

            with dve.Fori(0, NT // U) as r:
                t = U * r
                d = USES[1] * r
                for u in range(U):
                    copy_values(d + 1 + u, u, a_row[:, 0, :])
                for u in range(U):
                    dve.wait_ge(s["qk_done"], t + u + 3)
                    spread_keys(u, scores_ps[:, u, 1, 0:P], a_col[:, 1:2], "head16", s["k_copied"])
                for u in range(U):
                    softmax_shift(2 * t + u + 1, u)
                for u in range(U):
                    normalise(2 * t + u + 1, u)
                for u in range(U):
                    softmax_shift(2 * t + 2 + u + 1, u)
                for u in range(U):
                    normalise(2 * t + 2 + u + 1, u)
                for u in range(U):
                    dve.wait_ge(s["out_done"], t + u + 3)
                    dve.wait_ge(s["x_res_done"], t + u + 3)
                    dve.tensor_tensor(y[u], scores_ps[:, u, 0, 0:P], x_res[u], ALU.add).then_inc(s["y_done"], 1)
                for u in range(U):
                    dve.wait_ge(s["y_done"], t + u + 3)
                    ln_stats(t + u + 1, u, y[u])
                for u in range(U):
                    dve.wait_ge(x_stored[u], 8 * t + 16)
                    ln_apply(t + u + 1, u, x_out[u], y[u])

            for c in range(HOPS // 4):
                dve.wait_ge(hop_turned, c + 1)
                dve.tensor_copy(hop_T[:, 4 * c:4 * c + 4, :], setup_ps[:, 4 * (c % 4):4 * (c % 4) + 4, :])\
                   .then_inc(hop_copied, 1)
            dve.wait_ge(hop_copied, HOPS // 4)
            hop_by_query = hop_T[:].rearrange("p j (v m) -> p (j v) m", v=2)
            with dve.Fori(0, S // U) as r:
                v = U * r
                for u in range(U):
                    dve.wait_ge(s["hop_done"], v + u + 1)
                    dve.tensor_tensor(hop_bd[u].rearrange("p (h m) -> p h m", h=4),
                                      hop_by_query[:, bass.ds(v + u, 1), :].broadcast_to([P, 4, S]),
                                      const("head4").unsqueeze(2).broadcast_to([P, 4, S]), ALU.mult)\
                       .then_inc(s["hb_done"], 1)
                for u in range(U):
                    dve.wait_ge(s["hop_done"], v + u + 3)
                    dve.wait_ge(hop_stored[u], 8 * v + 16)
                    dve.tensor_copy(hop_out[u][0:B, 4 * S:8 * S], scores_ps[0:B, u, 1, 0:4 * S])\
                       .then_inc(s["hop_out1"], 1)

            base = BASE[3]

            def rope(n, u):
                dve.wait_ge(s["qk_done"], n + 2)
                qk = scores_ps[:, u].rearrange("p g (r n) -> p r g n", n=P)
                for k, (dst, table) in enumerate(((rope_c, "cos"), (rope_s, "sin"))):
                    last = dve.tensor_tensor(dst[u].rearrange("p (g n) -> p g n", g=2), qk[:, k],
                                             const(table).unsqueeze(1).broadcast_to([P, 2, P]), ALU.mult)
                last.then_inc(s["rope_done"], 1)

            def rest(r):
                t = U * r
                n = t + 1
                d = base["desk"] + USES[3] * r
                m = base["att"] + 2 * t
                ln = base["ln"] + 3 * t
                last_n = n + U - 1
                for u in range(U):
                    dve.wait_ge(s["scores_done"], 2 * (m + u + 1) + 4)
                    dve.tensor_tensor(probs[u][:, 0:512], scores_ps[:, u, 0, :], hop_in[u], ALU.add)\
                       .then_inc(s["shifted"], 2)
                for u in range(U):
                    dve.wait_ge(s["turn1_done"], m + u + 3)
                    gm = turned_ps[:, 1, :].rearrange("p (h t) -> p h t", t=S)
                    dve.tensor_reduce(row_max[u][:, 0:8], gm, AX, ALU.max).then_inc(s["max_done"], 2)
                    dve.wait_ge(s["max_done"], 2 * (m + u + 1) + 4)
                    dve.tensor_tensor(decay[u].rearrange("p (h t) -> p h t", t=S), gm,
                                      row_max[u][:, 0:8].unsqueeze(2).broadcast_to([P, 8, S]), ALU.subtract)\
                       .then_inc(s["turn1_copied"], 1)
                    dve.tensor_tensor(cmax[u], csum[u], row_max[u][:, 0:8], ALU.add).then_inc(s["cmax_done"], 1)
                for u in range(U):
                    dve.wait_ge(s["shifted"], 2 * (m + u + 1) + 4)
                    dve.wait_ge(s["decay_done"], n + u + 2)
                    dve.tensor_tensor(probs[u][:, 0:512], probs[u][:, 0:512], decay[u], ALU.mult)\
                       .then_inc(s["exp_done"], 2)
                for u in range(U):
                    dve.wait_ge(s["pv_done"], m + u + 3)
                    dve.wait_ge(s["floor_done"], n + u + 2)
                    hv = heads_ps[:, 0:272].rearrange("p (g b h c) -> p g b h c", g=4, b=NB, h=2)
                    for b in range(NB):
                        rows = slice(S * b, S * b + S)
                        last = dve.scalar_tensor_tensor(
                            denom[u][rows].rearrange("p (g h) -> p g h", g=4), hv[rows, :, b, :, MD], -1.0,
                            floor[u][rows].rearrange("p (g h) -> p g h", g=4), ALU.mult, ALU.max)
                    last.then_inc(s["denom_done"], 1)
                    dve.wait_ge(s["denom_done"], n + u + 2)
                    for b in range(NB):
                        rows = slice(S * b, S * b + S)
                        last = dve.tensor_tensor(
                            denom3[u][rows].rearrange("p (g h) -> p g h", g=4), hv[rows, :, b, :, MD],
                            denom[u][rows].rearrange("p (g h) -> p g h", g=4), ALU.max)
                    last.then_inc(s["denom3_done"], 1)
                    dve.wait_ge(s["denom3_done"], n + u + 2)
                    dve.tensor_scalar(denom2[u], denom3[u], 1e-6, None, ALU.add).then_inc(s["denom2_done"], 1)
                    dve.wait_ge(s["denom2_done"], n + u + 2)
                    dve.reciprocal(recip[u][:, 0:8], denom2[u]).then_inc(s["recip_done"], 1)
                    dve.wait_ge(s["recip_done"], m + u + 3)
                    for b in range(NB):
                        rows = slice(S * b, S * b + S)
                        rv = recip[u][rows, 0:8].rearrange("p (g h) -> p g h", g=4).unsqueeze(3)
                        last = dve.tensor_tensor(ctx_o[u][rows].rearrange("p (g h c) -> p g h c", g=4, h=2),
                                                 hv[rows, :, b, :, 0:MD], rv.broadcast_to([S, 4, 2, MD]), ALU.mult)
                    last.then_inc(s["normed"], 1)
                for u in range(U):
                    by_head = ctx_o[u].rearrange("p (h c) -> p h c", c=MD)
                    dve.wait_ge(s["normed"], m + u + 3)
                    dve.tensor_reduce(h_sum[u], by_head, AX, ALU.add).then_inc(s["h_sum_done"], 1)
                    dve.wait_ge(s["h_sum_done"], n + u + 2)
                    dve.scalar_tensor_tensor(h_mid[u].rearrange("p (h c) -> p h c", c=MD),
                                             h_sum[u].unsqueeze(2).broadcast_to([P, MH, MD]), -1.0 / MD, by_head,
                                             ALU.mult, ALU.add).then_inc(s["h_mid_done"], 1)
                for u in range(U):
                    dve.wait_ge(s["h_mid_done"], n + u + 2)
                    dve.tensor_tensor(h_sq[u], h_mid[u], h_mid[u], ALU.mult).then_inc(s["h_sq_done"], 1)
                for u in range(U):
                    dve.wait_ge(s["h_sq_done"], n + u + 2)
                    dve.tensor_reduce(h_var[u], h_sq[u].rearrange("p (h c) -> p h c", c=MD), AX, ALU.add)\
                       .then_inc(s["h_var_done"], 1)
                for u in range(U):
                    dve.wait_ge(s["h_var_done"], n + u + 2)
                    dve.tensor_scalar(h_veps[u], h_var[u], 1.0 / MD, EPS_LN, ALU.mult, ALU.add).then_inc(s["h_veps_done"], 1)
                for u in range(U):
                    dve.wait_ge(s["h_mid_done"], n + u + 2)
                    dve.tensor_tensor(h_sq[u], h_mid[u], m_row[:, 0, :], ALU.mult).then_inc(s["z1_done"], 1)
                for u in range(U):
                    dve.wait_ge(s["z1_done"], n + u + 2)
                    dve.wait_ge(s["h_rstd_done"], n + u + 2)
                    dve.tensor_tensor(z[u].rearrange("p (h c) -> p h c", c=MD),
                                      h_sq[u].rearrange("p (h c) -> p h c", c=MD),
                                      h_rstd[u].unsqueeze(2).broadcast_to([P, MH, MD]), ALU.mult)\
                       .then_inc(s["z2_done"], 1)
                for u in range(U):
                    dve.wait_ge(s["z2_done"], n + u + 2)
                    dve.wait_ge(s["xb_done"], n + u + 2)
                    dve.tensor_tensor(z[u], z[u], xb[u], ALU.add).then_inc(s["z_done"], 1)
                for u in range(U):
                    dve.wait_ge(s["z_done"], n + u + 2)
                    ln_stats(ln + u + 1, u, z[u])
                for u in range(U):
                    dve.wait_ge(s["r4_done"], n + u)
                    ln_apply(ln + u + 1, u, x2[u], z[u])
                for u in range(U):
                    dve.wait_ge(s["ln_done"], ln + u + 3)
                    ln_stats(ln + U + u + 1, u, x2[u])
                for u in range(U):
                    dve.wait_ge(xn_stored[u], 16 * t + 32)
                    ln_apply(ln + U + u + 1, u, xn[u], x2[u])
                for u in range(U):
                    rope(base["qk"] + n + u, u)
                for u in range(U):
                    copy_values(d + 7 + u, u, None)
                for u in range(U):
                    dve.wait_ge(s["rope_k_done"], n + u + 2)
                    spread_keys(u, rope_k[u], 0.0, "head16", s["k_copied"])
                for u in range(U):
                    softmax_shift(m + 2 + u + 1, u)
                for u in range(U):
                    normalise(m + 2 + u + 1, u)

            def head(r):
                t = U * r
                n = t + 1
                d = base["desk"] + USES[3] * r
                m = base["att"] + 2 * t
                ln = base["ln"] + 3 * t
                last_n = n + U - 1
                gate_in, gate_f = whole["gates"][:, :, 0:MH], whole["gates"][:, :, MH:2 * MH]
                dve.wait_ge(desk_full, d + 2)
                dve.tensor_tensor(whole["gates"][:], desk_ps[:, 0:16 * U].rearrange("p (u h) -> p u h", u=U),
                                  g_row[:].unsqueeze(1).broadcast_to([P, U, 16]), ALU.add).then_inc(s["gates_done"], U)
                dve.wait_ge(s["gates_done"], last_n + 2)
                dve.sem_inc(desk_empty, 1)
                dve.scalar_tensor_tensor(whole["neg_abs"][:], gate_f, -1.0, gate_f, ALU.mult, ALU.min)\
                   .then_inc(s["neg_abs_done"], U)

            def sums(r):
                t = U * r
                n = t + 1
                d = base["desk"] + USES[3] * r
                m = base["att"] + 2 * t
                ln = base["ln"] + 3 * t
                last_n = n + U - 1
                last_n = n + U - 1
                gate_in, gate_f = whole["gates"][:, :, 0:MH], whole["gates"][:, :, MH:2 * MH]
                dve.wait_ge(s["soft_done"], last_n + 2)
                dve.scalar_tensor_tensor(whole["log_f"][:], gate_f, 0.0, whole["soft"][:], ALU.min, ALU.subtract)\
                   .then_inc(s["log_f_done"], U)
                dve.wait_ge(desk_full, d + 3)
                sums = desk_ps[:, 0:U * MH].rearrange("p (u h) -> p u h", u=U)
                dve.tensor_copy(whole["csum"][:], sums)
                dve.tensor_tensor(whole["g_key"][:], gate_in, sums, ALU.subtract).then_inc(s["g_key_done"], U)
                dve.wait_ge(s["g_key_done"], last_n + 2)
                dve.sem_inc(desk_empty, 1)

            def tail(r):
                t = U * r
                n = t + 1
                d = base["desk"] + USES[3] * r
                m = base["att"] + 2 * t
                ln = base["ln"] + 3 * t
                last_n = n + U - 1
                for u in range(U):
                    dve.wait_ge(s["out_done"], base["out"] + n + u + 2)
                    dve.tensor_tensor(y[u], scores_ps[:, u, 0, 0:P], x2[u], ALU.add).then_inc(s["y_done"], 1)
                for u in range(U):
                    dve.wait_ge(s["y_done"], base["out"] + n + u + 2)
                    ln_stats(ln + 2 * U + u + 1, u, y[u])

            def norm(r):
                t = U * r
                n = t + 1
                d = base["desk"] + USES[3] * r
                m = base["att"] + 2 * t
                ln = base["ln"] + 3 * t
                last_n = n + U - 1
                for u in range(U):
                    ln_apply(ln + 2 * U + u + 1, u, xn[u], y[u])

            rounds(dve, rest, [("tail", tail), ("head", head), ("head", sums), ("tail", norm)])

            dve.wait_ge(late, 16 * len(late_loads))
            for k, at in enumerate((2, 4)):
                dve.tensor_copy(l_w[:, at, :].rearrange("p (g n) -> p g n", g=4),
                                l_raw[:, 32 * k:32 * k + 32].unsqueeze(1).broadcast_to([P, 4, 32]))
            dve.tensor_scalar(c_col[:, 2:3], c_col[:, 0:1], SCALE, None, ALU.mult).then_inc(w_ready, 1)
            dve.wait_ge(w_ready, W_READY + 1)
            rotate(l_w[:, 1, :], l_w[:, 0, :])
            rotate(l_w[:, 3, :], l_w[:, 2, :]).then_inc(w_ready, 1)

            links = [0]

            def link(ins):
                links[0] += 1
                ins.then_inc(route_chain, 1)
                dve.wait_ge(route_chain, links[0])

            def one_hot(dst, values, best, E):
                em = const("expert")[:, 0:E].unsqueeze(1).broadcast_to([P, NT, E])
                tmp = r_tmp[:, :, 0:E]
                link(dve.tensor_tensor(tmp, values, best.unsqueeze(2).broadcast_to([P, NT, E]), ALU.is_equal))
                link(dve.tensor_tensor(tmp, tmp, em, ALU.mult))
                link(dve.tensor_reduce(r_b[:], tmp, AX, ALU.min))
                link(dve.tensor_tensor(dst, em, r_b[:].unsqueeze(2).broadcast_to([P, NT, E]), ALU.is_equal))

            def route(n, E, logits, capped):
                gate, tmp, one, two, pos = (a[:, :, 0:E] for a in (r_gate, r_tmp, r_one, r_two, r_pos))
                wide = [P, NT, E]
                link(dve.tensor_reduce(r_a[:], logits[:], AX, ALU.max))
                dve.tensor_tensor(gate, logits[:], r_a[:].unsqueeze(2).broadcast_to(wide), ALU.subtract)\
                   .then_inc(route_shifted, 1)
                dve.wait_ge(route_exp, n)
                link(dve.tensor_reduce(r_a[:], gate, AX, ALU.add))
                link(dve.reciprocal(r_b[:], r_a[:]))
                link(dve.tensor_tensor(gate, gate, r_b[:].unsqueeze(2).broadcast_to(wide), ALU.mult))
                link(dve.tensor_reduce(weight[:, 0, :], gate, AX, ALU.max))
                one_hot(one, gate, weight[:, 0, :], E)
                link(dve.scalar_tensor_tensor(gate, one, -2.0, gate, ALU.mult, ALU.add))
                link(dve.tensor_reduce(weight[:, 1, :], gate, AX, ALU.max))
                one_hot(two, gate, weight[:, 1, :], E)
                dve.tensor_tensor(r_mask[:, 0:NT * E].rearrange("p (t e) -> p t e", e=E), one, two, ALU.add)\
                   .then_inc(route_masked, 1)
                dve.wait_ge(route_counted, n)
                tiles_in_bank = 512 // E
                scan = [r_scan, r_scan2]
                for c in range(-(-NT * E // 512)):
                    n_t = min(tiles_in_bank, NT - tiles_in_bank * c)
                    part = slice(tiles_in_bank * c, tiles_in_bank * c + n_t)
                    dve.tensor_copy(pos[:, part], scores_ps[:, 0, c, 0:n_t * E].rearrange("p (t e) -> p t e", e=E))
                    last = dve.tensor_copy(r_scan[:, part, 0:E],
                                           scores_ps[:, 1, c, 0:n_t * E].rearrange("p (t e) -> p t e", e=E))
                    link(last)
                dve.sem_inc(counts_read, 1)
                link(dve.tensor_tensor(pos, pos, r_scan[:, :, 0:E], ALU.subtract))
                step = 1
                while step < NT:
                    a, b = scan
                    dve.tensor_copy(b[:, 0:step, 0:E], a[:, 0:step, 0:E])
                    link(dve.tensor_tensor(b[:, step:NT, 0:E], a[:, step:NT, 0:E], a[:, 0:NT - step, 0:E], ALU.add))
                    scan = [b, a]
                    step *= 2
                total = scan[0]
                link(dve.scalar_tensor_tensor(pos, pos, -1.0, total[:, :, 0:E], ALU.add, ALU.add))
                if capped:
                    link(dve.tensor_scalar(tmp, pos, float(CAP), FAR, ALU.is_ge, ALU.mult))
                    link(dve.tensor_tensor(pos, pos, tmp, ALU.add))
                    region = const("region0")
                else:
                    link(dve.tensor_scalar(r_int[:], total[:, NT - 1, 0:E], float(P - 1), None, ALU.add))
                    link(dve.tensor_scalar(r_int[:], r_int[:], 7, 7, ALU.logical_shift_right,
                                           ALU.logical_shift_left))
                    link(dve.tensor_copy(r_cnt[:], r_int[:]))
                    link(dve.tensor_copy(r_end[:], r_cnt[:]))
                    ends, step = [r_end, r_cnt2], 1
                    while step < E:
                        a, b = ends
                        dve.tensor_copy(b[:, 0:step], a[:, 0:step])
                        link(dve.tensor_tensor(b[:, step:E], a[:, step:E], a[:, 0:E - step], ALU.add))
                        ends = [b, a]
                        step *= 2
                    end = ends[0]
                    link(dve.tensor_tensor(r_base[:], end[:], r_cnt[:], ALU.subtract))
                    link(dve.tensor_tensor(r_le, end[:].unsqueeze(1).broadcast_to([P, NJ, E]),
                                           const("tile_start").unsqueeze(2).broadcast_to([P, NJ, E]), ALU.is_le))
                    link(dve.tensor_reduce(r_ej[:], r_le, AX, ALU.add))
                    link(dve.tensor_scalar(expert_of[:], r_ej[:], float(E - 1), None, ALU.min))
                    region = r_base[:]
                link(dve.tensor_tensor(pos, pos, region.unsqueeze(1).broadcast_to(wide), ALU.add))
                for k, hot in enumerate((one, two)):
                    link(dve.tensor_tensor(tmp, hot, pos, ALU.mult))
                    link(dve.tensor_reduce(slot_f[:, k, :], tmp, AX, ALU.add))
                n_slots = NSLOT0 if capped else NSLOT1
                if capped:
                    link(dve.tensor_scalar(slot_put[:], slot_f[:], 0.0, None, ALU.add))
                    link(dve.scalar_tensor_tensor(weight[:], slot_f[:], FAR / 2, weight[:], ALU.is_lt, ALU.mult))
                else:
                    link(dve.tensor_scalar(r_slot[:], slot_f[:], 0.0, None, ALU.add))
                    link(dve.tensor_scalar(r_low[:], r_slot[:], P - 1, None, ALU.bitwise_and))
                    link(dve.tensor_scalar(r_slot[:], r_slot[:], 7, None, ALU.logical_shift_right))
                    link(dve.scalar_tensor_tensor(slot_put[:], r_low[:], float(NJ), r_slot[:], ALU.mult, ALU.add))
                    link(dve.tensor_tensor(r_a[:], weight[:, 0, :], weight[:, 1, :], ALU.add))
                    link(dve.tensor_scalar(r_a[:], r_a[:], 1e-9, None, ALU.max))
                    link(dve.reciprocal(r_b[:], r_a[:]))
                    link(dve.tensor_tensor(weight[:], weight[:], r_b[:].unsqueeze(1).broadcast_to([P, 2, NT]), ALU.mult))
                link(dve.tensor_scalar(slot_get[:, :, 0:NT], slot_f[:], float(n_slots - 1), None, ALU.min))

            dve.wait_ge(desk_empty, BASE[5]["desk"] + 1)
            route(1, E0, logits0, True)
            dve.sem_inc(routed, 1)

            with dve.Fori(0, E0 // 2) as r:
                for i in range(2 * GE):
                    w, u, q = i // GE, i % 2, 2 * GE * r + i
                    dve.wait_ge(s["e_turned"], q + 3)
                    dve.tensor_scalar(e_T[u], turned_ps[:, u, 0:GS], f_col[:, 2:3], f_col[:, 3:4], ALU.mult, ALU.add)\
                       .then_inc(s["e_T_done"], 1)
                    dve.wait_ge(s["down_done"], q + 3)
                    dve.wait_ge(e_stored[u], 16 * (GE * r + i // 2) + 16)
                    dve.wait_ge(e_loaded[w], 64 * r + 64)
                    dve.tensor_tensor(e_out[u].rearrange("p (j d) -> p j d", d=D),
                                      (heads_ps, desk_ps)[u][:, 0:GS].rearrange("p (j d) -> p j d", d=D),
                                      e_b2[w][:].unsqueeze(1).broadcast_to([P, J, D]), ALU.add)\
                       .then_inc(s["e_out_done"], 1)
                    if i % GE == GE - 1:
                        dve.wait_ge(s["e_out_done"], q + 3)
                        dve.sem_inc(s["expert_done"], 1)

            def combine(n, u, rows, count, loads, dst):
                dve.wait_ge(count, loads)
                dve.wait_ge(s["weights_got"], n + 2)
                dve.scalar_tensor_tensor(y[u], rows[:, 0:D], got_w[u][:, 0:1], x_in[u], ALU.mult, ALU.add)\
                   .then_inc(s["c1_done"], 1)
                dve.wait_ge(s["c1_done"], n + 2)
                dve.scalar_tensor_tensor(dst[u], rows[:, D:2 * D], got_w[u][:, 1:2], y[u], ALU.mult, ALU.add)\
                   .then_inc(s["c2_done"], 1)

            def get_weights(n, tile, u):
                dve.tensor_copy(got_w[u], weight[:, :, bass.ds(tile, 1)].rearrange("p k t -> p (k t)"))\
                   .then_inc(s["weights_got"], 1)

            base = BASE[5]
            def rest(r):
                t = U * r
                n = t + 1
                d = base["desk"] + USES[5] * r
                m = base["att"] + 2 * t
                ln = base["ln"] + 3 * t
                o2 = base["out"] + 2 * t
                for u in range(U):
                    dve.wait_ge(s["rope_k_done"], NT + n + u + 2)
                    spread_keys(u, rope_k[u], 0.0, "head16", s["k_copied"])
                    copy_values(d + 4 + u, u, None)
                for u in range(U):
                    softmax_shift(m + u + 1, u)
                for u in range(U):
                    normalise(m + u + 1, u)
                for u in range(U):
                    dve.wait_ge(s["out_done"], o2 + u + 3)
                    dve.tensor_tensor(y[u], scores_ps[:, u, 0, 0:P], x4[u], ALU.add).then_inc(s["y_done"], 1)
                for u in range(U):
                    copy_values(d + 9 + u, u, c_row[:, 0, :])
                for u in range(U):
                    dve.wait_ge(s["y_done"], o2 + u + 3)
                    ln_stats(ln + 2 * U + u + 1, u, y[u])
                for u in range(U):
                    dve.wait_ge(s["x5b_done"], n + u)
                    ln_apply(ln + 2 * U + u + 1, u, x5[u], y[u])
                for u in range(U):
                    dve.wait_ge(s["qk_done"], base["qk"] + 2 * t + 2 + u + 3)
                    spread_keys(u, scores_ps[:, u, 1, 0:P], c_col[:, 1:2], "head16", s["k_copied"])
                for u in range(U):
                    mm = m + 2 + u + 1
                    dve.wait_ge(s["turn1_done"], mm)
                    dve.wait_ge(s["fm_done"], n + u + 2)
                    for g in range(NR):
                        dve.wait_ge(s["scores_done"], 2 * mm + g + 3)
                        pv = probs[u][:, 512 * g:512 * g + 512].rearrange("p (h t) -> p h t", t=S)
                        best = row_max[u][:, 8 * g:8 * g + 8]
                        dve.tensor_tensor(pv, scores_ps[:, u, g, :].rearrange("p (h t) -> p h t", t=S),
                                          fm[u].unsqueeze(1).broadcast_to([P, 8, S]), ALU.add)\
                           .then_inc(s["biased"], 1)
                        dve.wait_ge(s["biased"], 2 * (n + u) + g + 3)
                        dve.tensor_reduce(best, pv, AX, ALU.max).then_inc(s["max_done"], 1)
                        dve.wait_ge(s["max_done"], 2 * mm + g + 3)
                        dve.tensor_tensor(pv, pv, best.unsqueeze(2).broadcast_to([P, 8, S]), ALU.subtract)\
                           .then_inc(s["shifted"], 1)
                for u in range(U):
                    normalise(m + 2 + u + 1, u)

            def head(r):
                t = U * r
                n = t + 1
                d = base["desk"] + USES[5] * r
                m = base["att"] + 2 * t
                ln = base["ln"] + 3 * t
                o2 = base["out"] + 2 * t
                for u in range(U):
                    get_weights(n + u, t + u, u)
                for u in range(U):
                    dve.wait_ge(in_loaded[u], 16 * NT + 8 * t + 16)
                    combine(n + u, u, got[u], got_loaded[u], 16 * t + 32, z)
                for u in range(U):
                    dve.wait_ge(s["c2_done"], n + u + 2)
                    ln_stats(ln + u + 1, u, z[u])
                for u in range(U):
                    ln_apply(ln + u + 1, u, x4[u], z[u])

            def rotation(r):
                t = U * r
                n = t + 1
                d = base["desk"] + USES[5] * r
                m = base["att"] + 2 * t
                ln = base["ln"] + 3 * t
                o2 = base["out"] + 2 * t
                for u in range(U):
                    rope(o2 + u + 1, u)

            def tail(r):
                t = U * r
                n = t + 1
                d = base["desk"] + USES[5] * r
                m = base["att"] + 2 * t
                ln = base["ln"] + 3 * t
                o2 = base["out"] + 2 * t
                for u in range(U):
                    dve.wait_ge(s["out_done"], o2 + 2 + u + 3)
                    dve.wait_ge(s["x5b_done"], n + u + 2)
                    dve.tensor_tensor(y[u], scores_ps[:, u, 0, 0:P], x5b[u], ALU.add).then_inc(s["y_done"], 1)
                for u in range(U):
                    dve.wait_ge(s["y_done"], o2 + 2 + u + 3)
                    ln_stats(ln + 4 * U + u + 1, u, y[u])

            def norm(r):
                t = U * r
                n = t + 1
                d = base["desk"] + USES[5] * r
                m = base["att"] + 2 * t
                ln = base["ln"] + 3 * t
                o2 = base["out"] + 2 * t
                for u in range(U):
                    dve.wait_ge(x6_stored[u], 8 * t + 16)
                    ln_apply(ln + 4 * U + u + 1, u, x6[u], y[u])

            def skip_x6(r):
                for k in ("stat_done", "mv_done", "veps_done", "ln_done"):
                    dve.wait_ge(s[k], base["ln"] + U + 2)
                    dve.sem_inc(s[k], U)

            def skip_x4(r):
                for k in ("stat_done", "mv_done", "veps_done", "ln_done"):
                    dve.wait_ge(s[k], base["ln"] + 3 * NT + 2)
                    dve.sem_inc(s[k], U)

            rounds(dve, rest, [("head", head), ("last", skip_x4), ("tail", tail), ("first", skip_x6), ("head", rotation), ("tail", norm)])

            dve.wait_ge(desk_empty, BASE[5]["desk"] + USES[5] * NT // U + 4 + 1)
            link(dve.tensor_tensor(logits1[:], logits1[:], rt_row[:].unsqueeze(1).broadcast_to([P, NT, E1]), ALU.add))
            route(2, E1, logits1, False)
            dve.sem_inc(routed, 1)
            def expert(r, w, i):
                return dve.value_load(expert_of[0:1, bass.ds(V * r + 2 * w + i, 1)], min_val=0, max_val=E1 - 1)

            def cols(i):
                return slice(P * i, P * i + P)

            with dve.Fori(0, NJ // V) as r:
                for w in range(2):
                    dve.wait_ge(s["o_turned"], 2 * r + w + 3)
                    dve.tensor_copy(o_in_T[w], turned_ps[:, w, 0:2 * P]).then_inc(s["o_T_done"], 1)
                for w in range(2):
                    q = 2 * r + w + 1
                    experts = [expert(r, w, i) for i in range(2)]
                    dve.wait_ge(s["o_up"], q + 2)
                    for i, e in enumerate(experts):
                        last = dve.tensor_tensor(o_h[w][:, cols(i)], scores_ps[:, w, 0, cols(i)],
                                                 o_b1[:, bass.ds(e, 1), :].rearrange("p e h -> p (e h)"), ALU.add)
                    last.then_inc(s["o_h_done"], 1)
                    dve.wait_ge(s["o_h_done"], q + 2)
                    for i in range(2):
                        last = dve.bn_stats(o_stat[w][:, 6 * i:6 * i + 6], o_h[w][:, cols(i)])
                    last.then_inc(s["o_stat_done"], 1)
                    q2 = dve.to_reg(q + 2)
                    dve.wait_ge(w_turned, 1)
                    dve.wait_ge(s["o_stat_done"], q2)
                    for i in range(2):
                        last = dve.bn_aggr(o_mv[w][:, 2 * i:2 * i + 2], o_stat[w][:, 6 * i:6 * i + 6])
                    last.then_inc(s["o_mv_done"], 1)
                    dve.wait_ge(s["o_mv_done"], q + 2)
                    dve.tensor_scalar(o_veps[w], o_mv[w].rearrange("p (i k) -> p k i", k=2)[:, 1, :], EPS_LN, None,
                                      ALU.add).then_inc(s["o_veps_done"], 1)
                for w in range(2):
                    q = 2 * r + w + 1
                    dve.wait_ge(s["o_rstd_done"], q + 2)
                    dve.wait_ge(s["o_hturned"], q)
                    for i in range(2):
                        last = dve.tensor_scalar(o_hn[w][:, cols(i)], o_h[w][:, cols(i)], o_mv[w][:, 2 * i:2 * i + 1],
                                                 o_rstd[w][:, i:i + 1], ALU.subtract, ALU.mult)
                    last.then_inc(s["o_hn_done"], 1)
                for w in range(2):
                    q = 2 * r + w + 1
                    experts = [expert(r, w, i) for i in range(2)]
                    dve.wait_ge(s["o_down"], q + 2)
                    dve.wait_ge(o_stored[w], 16 * r + 16)
                    for i, e in enumerate(experts):
                        last = dve.tensor_tensor(o_out[w][:, cols(i)], (heads_ps, desk_ps)[w][:, cols(i)],
                                                 o_b2[:, bass.ds(e, 1), :].rearrange("p e h -> p (e h)"), ALU.add)
                    last.then_inc(s["o_out_done"], 1)

            with dve.Fori(0, NT // V) as r:
                for pair in range(0, V, U):
                    t = V * r + pair
                    n = NT + t + 1
                    for u in range(U):
                        get_weights(n + u, t + u, u)
                    for u in range(U):
                        k = pair + u
                        dve.wait_ge(z_loaded[u], 8 * t + 16)
                        combine(n + u, u, far_got[k], far_loaded[k], 32 * r + 32, z)
                    for u in range(U):
                        dve.wait_ge(s["c2_done"], n + u + 2)
                        ln_stats(LAST_LN + t + u + 1, u, z[u])
                    for u in range(U):
                        dve.wait_ge(z_stored[u], 8 * t + 16)
                        ln_apply(LAST_LN + t + u + 1, u, x_out[u], z[u])

        @block.gpsimd
        def _(pool):
            for k in pool_done:
                pool.sem_inc(s[k], CREDIT)
            pool.memset(minus_half[:], -0.5)
            pool.memset(zeros_i[:], 0).then_inc(zero_sem, 1)
            pool.memset(slot_get[:], 0)
            pool.memset(at1_all[:], 0)
            pool.iota(token[:], [[P, NT]], base=0, channel_multiplier=1)
            for u in range(U):
                pool.memset(pad_T[u], 0.0)
                pool.memset(m_vbd[u], 0.0)
                pool.memset(v_bd[u], 0.0).then_inc(zeroed, 1)
            pool.wait_ge(zeroed, U)
            pool.wait_ge(loaded, 16 * len(w_loads))
            for u in range(U):
                vv = v_bd[u].rearrange("p (g b h c) -> p g b h c", g=8, b=NB, h=2)
                for par in range(2):
                    last = pool.memset(vv[S * par:S * par + S, :, :, par, HD:HD + 1], 1.0)
                mvv = m_vbd[u].rearrange("p (g b h c) -> p g b h c", g=4, b=NB, h=2)
                for par in range(2):
                    last = pool.memset(mvv[S * par:S * par + S, :, :, par, MD:MD + 1], 1.0)
            last.then_inc(zeroed, 1)
            for j in range(HOPS):
                pool.indirect_dma_start(out=hop_rows[:, j, :], out_offset=None, in_=T["L0_xattn_rpe"],
                                        in_offset=bass.IndirectOffsetOnAxis(ap=hop_at[:, j:j + 1], axis=0))\
                    .then_inc(hop_gathered, 16)

            def ln_rstd(o, u):
                pool.wait_ge(s["veps_done"], o + 2)
                pool.tensor_tensor(rstd[u], veps[u], minus_half[:, 0:1], ALU.pow).then_inc(s["rstd_done"], 1)

            with pool.Fori(0, NT // U) as r:
                t = U * r
                d = USES[1] * r
                for u in range(U):
                    pool.wait_ge(in_loaded[u], 8 * t + 16)
                    pool.wait_ge(desk_full, d + 1)
                    pool.wait_ge(s["y_done"], t + u + 1)
                    pool.tensor_tensor(x_res[u], x_in[u], a_row[:, 1, :], ALU.add).then_inc(s["x_res_done"], 1)
                for u in range(U):
                    ln_rstd(t + u + 1, u)

            base = BASE[3]
            def rest(r):
                t = U * r
                n = t + 1
                d = base["desk"] + USES[3] * r
                m = base["att"] + 2 * t
                ln = base["ln"] + 3 * t
                for u in range(U):
                    pool.wait_ge(s["h_veps_done"], n + u + 2)
                    pool.tensor_tensor(h_rstd[u], h_veps[u], minus_half[:, 0:8], ALU.pow)\
                        .then_inc(s["h_rstd_done"], 1)
                for u in range(U):
                    ln_rstd(ln + u + 1, u)
                for u in range(U):
                    ln_rstd(ln + U + u + 1, u)
                for u in range(U):
                    pool.wait_ge(s["rope_done"], n + u + 2)
                    pool.tensor_tensor(q_T[u], rope_c[u][:, 0:P], rope_s[u][:, 0:P], ALU.add)\
                        .then_inc(s["q_copied"], 1)
                    pool.tensor_tensor(rope_k[u], rope_c[u][:, P:2 * P], rope_s[u][:, P:2 * P], ALU.add)\
                        .then_inc(s["rope_k_done"], 1)

            def head(r):
                t = U * r
                n = t + 1
                d = base["desk"] + USES[3] * r
                m = base["att"] + 2 * t
                ln = base["ln"] + 3 * t
                for u in range(U):
                    pool.wait_ge(desk_empty, d + 2)
                    pool.wait_ge(s["scores_done"], 2 * (m + u + 1))
                    pool.tensor_tensor(k_bd[u][:, 0:MH * P].rearrange("p (h t) -> p h t", h=MH),
                                       c_T[u].unsqueeze(1).broadcast_to([P, MH, P]),
                                       const("head8q").unsqueeze(2).broadcast_to([P, MH, P]), ALU.mult)\
                        .then_inc(s["k_copied"], 2)
                for u in range(U):
                    pool.wait_ge(s["ln_done"], ln - 2 * U + u + 1 + U)
                    pool.tensor_tensor(xb[u], x_in[u], m_row[:, 1, :], ALU.add).then_inc(s["xb_done"], 1)

            def key_gates(r):
                t = U * r
                n = t + 1
                d = base["desk"] + USES[3] * r
                m = base["att"] + 2 * t
                ln = base["ln"] + 3 * t
                for u in range(U):
                    pool.wait_ge(s["g_key_done"], n + u + 2)
                    pool.tensor_tensor(g_diag[u].rearrange("p (h t) -> p h t", t=S),
                                       g_key[u].unsqueeze(2).broadcast_to([P, MH, S]),
                                       const("diag64").unsqueeze(1).broadcast_to([P, MH, S]), ALU.mult)\
                        .then_inc(s["g_diag_done"], 1)

            def tail(r):
                t = U * r
                n = t + 1
                d = base["desk"] + USES[3] * r
                m = base["att"] + 2 * t
                ln = base["ln"] + 3 * t
                for u in range(U):
                    ln_rstd(ln + 2 * U + u + 1, u)
                for u in range(U):
                    pool.wait_ge(s["y_done"], base["out"] + n + u + 2)
                    pool.wait_ge(xn_stored[u], 16 * t + 32)
                    pool.tensor_tensor(r4[u], y[u], x2[u], ALU.add).then_inc(s["r4_done"], 1)

            rounds(pool, rest, [("tail", tail), ("head", head), ("head", key_gates)])

            def put(n0):
                table, n_slots = (token_of0, NSLOT0) if n0 == 0 else (token_of1, NSLOT1)
                with pool.Fori(0, NT // U) as r:
                    for u in range(U):
                        pool.wait_ge(s["put_free"], n0 + U * r + u + 1)
                        pool.tensor_copy(put_at[u], slot_put[:, :, bass.ds(U * r + u, 1)].rearrange("p k t -> p (k t)"))
                        pool.tensor_copy(put_tok[u], token[:, bass.ds(U * r + u, 1)]).then_inc(s["put_ready"], 1)
                        nu = pool.to_reg(n0 + U * r + u + 3)
                        pool.wait_ge(table_sem, 32)
                        pool.wait_ge(s["put_ready"], nu)
                        for k in range(2):
                            pool.indirect_dma_start(
                                out=table, out_offset=bass.IndirectOffsetOnAxis(ap=put_at[u][:, k:k + 1], axis=0),
                                in_=put_tok[u], in_offset=None, bounds_check=n_slots - 1, oob_is_err=False)\
                                .then_inc(put_done[u], 16)

            for u in range(U):
                pool.wait_ge(xn_stored[u], 32 * (NT // U) + 32)
            pool.wait_ge(routed, 1)
            put(0)

            def load_expert(r, w):
                pool.wait_ge(s["expert_done"], 2 * r + w + 1)
                e = 2 * r + w
                for dst, src in (
                    (e_w1[w][:], T["L0_ffn_W1"][bass.ds(e, 1)].rearrange("e c f -> c (e f)")),
                    (e_w2[w][:], T["L0_ffn_W2"][bass.ds(e, 1)].rearrange("e (f p) d -> p (e f) d", p=P)),
                    (e_b1[w][:], T["L0_ffn_b1"][bass.ds(e, 1)].rearrange("e (f p) -> p (e f)", p=P)),
                    (e_b2[w][:], T["L0_ffn_b2"][bass.ds(e, 1)].rearrange("e d -> (e d)").partition_broadcast(P)),
                ):
                    pool.dma_start(dst, src, allow_slow_non_contiguous=True).then_inc(e_loaded[w], 16)

            pool.wait_ge(at_loaded, 16)
            with pool.Fori(0, E0 // 2) as r:
                for i in range(2 * GE):
                    u, q = i % 2, 2 * GE * r + i
                    if i % GE == 0:
                        load_expert(r, i // GE)
                    pool.wait_ge(s["e_turned"], q + 1)
                    pool.tensor_copy(e_at[u], at0_all[:, bass.ds(q, 1), :].rearrange("p q j -> p (q j)"))\
                        .then_inc(s["at_done"], 1)
                    nq = pool.to_reg(q + 3)
                    pool.wait_ge(routed, 1)
                    pool.wait_ge(s["at_done"], nq)
                    for j in range(J):
                        pool.indirect_dma_start(out=e_in[u][:, P * j:P * j + P], out_offset=None, in_=xn_dram,
                                                in_offset=bass.IndirectOffsetOnAxis(ap=e_at[u][:, j:j + 1], axis=0))\
                            .then_inc(e_in_loaded[u], 16)

            def get(n, c, tile, rows, at, dst, count):
                pool.wait_ge(s["c2_done"], c + 2)
                pool.tensor_copy(at, slot_get[:, :, bass.ds(tile, 1)].rearrange("p k t -> p (k t)"))\
                    .then_inc(s["got_ready"], 1)
                nu = pool.to_reg(n + 2)
                pool.wait_ge(routed, 1)
                pool.wait_ge(s["got_ready"], nu)
                for k in range(2):
                    pool.indirect_dma_start(out=dst[:, D * k:D * k + D], out_offset=None, in_=rows,
                                            in_offset=bass.IndirectOffsetOnAxis(ap=at[:, k:k + 1], axis=0))\
                        .then_inc(count, 16)

            for u in range(U):
                pool.wait_ge(e_stored[u], 16 * GE * E0 // 2 + 16)
            base = BASE[5]
            for u in range(U):
                get(u + 1, u + 1 - U, u, moe0, got_at[u], got[u], got_loaded[u])
            def rest(r):
                t = U * r
                n = t + 1
                ln = base["ln"] + 3 * t
                m = base["att"] + 2 * t
                for u in range(U):
                    pool.wait_ge(s["rope_done"], NT + n + u + 2)
                    pool.tensor_tensor(q_T[u], rope_c[u][:, 0:P], rope_s[u][:, 0:P], ALU.add)\
                        .then_inc(s["q_copied"], 1)
                    pool.tensor_tensor(rope_k[u], rope_c[u][:, P:2 * P], rope_s[u][:, P:2 * P], ALU.add)\
                        .then_inc(s["rope_k_done"], 1)
                for u in range(U):
                    get(n + U + u, n + u, t + U + u, moe0, got_at[u], got[u], got_loaded[u])
                for u in range(U):
                    pool.wait_ge(c_loaded[u], 32 * NT + 24 * t + 48)
                    pool.wait_ge(s["biased"], 2 * (n + u))
                    pool.tensor_tensor(fm[u], fm_in[u][:, 0:S], fm_in[u][:, S:2 * S], ALU.add)\
                        .then_inc(s["fm_done"], 1)
                for u in range(U):
                    ln_rstd(ln + 2 * U + u + 1, u)
                for u in range(U):
                    pool.wait_ge(s["ln_done"], ln + 2 * U + u + 3)
                    pool.wait_ge(s["y_done"], base["out"] + 2 * t + u + 1)
                    pool.tensor_tensor(x5b[u], x5[u], c_row[:, 1, :], ALU.add).then_inc(s["x5b_done"], 1)

            def head(r):
                t = U * r
                n = t + 1
                ln = base["ln"] + 3 * t
                m = base["att"] + 2 * t
                for u in range(U):
                    ln_rstd(ln + u + 1, u)

            def tail(r):
                t = U * r
                n = t + 1
                ln = base["ln"] + 3 * t
                m = base["att"] + 2 * t
                for u in range(U):
                    ln_rstd(ln + 4 * U + u + 1, u)

            def skip_x6(r):
                pool.wait_ge(s["rstd_done"], base["ln"] + U + 2)
                pool.sem_inc(s["rstd_done"], U)

            def skip_x4(r):
                pool.wait_ge(s["rstd_done"], base["ln"] + 3 * NT + 2)
                pool.sem_inc(s["rstd_done"], U)

            rounds(pool, rest, [("head", head), ("last", skip_x4), ("first", skip_x6), ("tail", tail)])

            pool.wait_ge(routed, 2)
            put(NT)
            for u in range(U):
                pool.wait_ge(x6_stored[u], 16 * (NT // U) + 16)
            pool.wait_ge(at_loaded, 32)

            def get_slots(r, w):
                q = 2 * r + w + 1
                pool.wait_ge(s["o_turned"], q)
                pool.tensor_copy(o_at[w], at1_all[:, bass.ds(V * r + 2 * w, 2)]).then_inc(s["at_done"], 1)
                nq = pool.to_reg(NSLOT0 // GS + q + 2)
                pool.wait_ge(routed, 2)
                pool.wait_ge(s["at_done"], nq)
                for i in range(2):
                    pool.indirect_dma_start(out=o_in[w][:, P * i:P * i + P], out_offset=None, in_=x6_dram,
                                            in_offset=bass.IndirectOffsetOnAxis(ap=o_at[w][:, i:i + 1], axis=0))\
                        .then_inc(o_in_loaded[w], 16)

            for w in range(2):
                get_slots(0, w)
            with pool.Fori(0, NJ // V) as r:
                for w in range(2):
                    pool.wait_ge(s["o_veps_done"], 2 * r + w + 3)
                    pool.tensor_tensor(o_rstd[w], o_veps[w], minus_half[:, 0:2], ALU.pow)\
                        .then_inc(s["o_rstd_done"], 1)
                    get_slots(r + 1, w)
            for u in range(U):
                pool.wait_ge(o_stored[u], 16 * (NJ // V) + 16)
                pool.wait_ge(o_in_loaded[u], 32 * (NJ // V) + 32)
            for k in range(V):
                get(NT + U + k + 1, NT, k, moe1, far_at[k], far_got[k], far_loaded[k])
            with pool.Fori(0, NT // V) as r:
                for pair in range(0, V, U):
                    for k in range(pair, pair + U):
                        ln_rstd(LAST_LN + V * r + k + 1, k % U)
                    for k in range(pair, pair + U):
                        tile = V * r + k
                        get(NT + U + V + tile + 1, NT + tile + 1, tile + V, moe1, far_at[k], far_got[k], far_loaded[k])


def launch_args(nc, inputs):
    cf, cb = constants(inputs["x"].shape[0] * S)
    arrays, T = {}, {}
    given = dict(inputs)
    given["consts"] = np.concatenate(list(cf.values()), axis=1)
    given["consts16"] = np.concatenate(list(cb.values()), axis=1).astype(np.float32)
    for name, a in given.items():
        a = np.ascontiguousarray(a)
        arrays[f"in_{name}"] = a
        T[name] = nc.dram_tensor(f"in_{name}", a.shape, mybir.dt.from_np(a.dtype), kind="ExternalInput").ap()
    return arrays, T


def kernel(**inputs):
    import concourse.bacc as bacc
    from concourse.bass_utils import run_bass_kernel_spmd

    nc = bacc.Bacc("TRN2", target_bir_lowering=False, num_devices=1)
    arrays, T = launch_args(nc, inputs)
    out = nc.dram_tensor("out_0", inputs["x"].shape, F32, kind="ExternalOutput").ap()
    build(nc, T, out)
    return run_bass_kernel_spmd(nc, [arrays], core_ids=[0]).results[0]["out_0"]
```
